# Optimizing a Trainium2 kernel written in Bass

```python
import numpy as np
import jax
import jax.numpy as jnp

def _softmax(x, axis=-1):
    return jax.nn.softmax(x, axis=axis)

def _gelu(x):
    return jax.nn.gelu(x, approximate=True)

def _silu(x):
    return jax.nn.silu(x)

def _sigmoid(x):
    return jax.nn.sigmoid(x)

def _layernorm(x, axis=-1, eps=1e-05):
    m = jnp.mean(x, axis=axis, keepdims=True)
    v = jnp.var(x, axis=axis, keepdims=True)
    return (x - m) / jnp.sqrt(v + eps)

def _scatter_add(tgt, idx, src, axis=0):
    return tgt.at[idx].add(src)

def _segment_sum(src, seg, n):
    return jax.ops.segment_sum(src, seg, n)
kernel_name = 'mk_xattn_seq_d4_seqx_r4_6b86f1'

def setup_inputs(seed: int=0):
    np.random.seed(seed)
    _w = jnp.asarray

    def _rec_inputs():
        import jax
        import jax.numpy as jnp
        _rk = jax.random.key(seed)
        x = -0.0002928 + 1 * jax.random.normal(jax.random.fold_in(_rk, 1), (4, 512, 256), jnp.float32)
        _lenS = 512 - jax.random.randint(jax.random.fold_in(_rk, 7), (4,), 0, max(1, 512 // 4) + 1, jnp.int32)
        _lenS2 = 512 - jax.random.randint(jax.random.fold_in(_rk, 8), (4,), 0, max(1, 512 // 4) + 1, jnp.int32)
        _ctx_1024P = jax.random.normal(jax.random.fold_in(_rk, 11), (4, 16, 256), jnp.float32)
        _ctx_1024c = jax.random.dirichlet(jax.random.fold_in(_rk, 511), 0.3 * jnp.ones((16,), jnp.float32), (4, 512))
        _ctx_1024t = jnp.einsum('bsk,bkd->bsd', _ctx_1024c, _ctx_1024P)
        _ctx_1024t = _ctx_1024t * jax.lax.rsqrt(jnp.mean(jnp.square(_ctx_1024t)) + 1e-12) * 0.953939
        ctx_1024 = -1.39393e-06 + 0.999914 * (_ctx_1024t + 0.3 * jax.random.normal(jax.random.fold_in(_rk, 611), (4, 512, 256), jnp.float32))
        _validS = jnp.arange(512)[None, :] < _lenS[:, None]
        _validS2 = jnp.arange(512)[None, :] < _lenS2[:, None]
        _causal = jnp.tril(jnp.ones((512, 512), dtype=bool))
        mask_BxS2_ik0 = jnp.where(jnp.broadcast_to(_validS2[:, :], (4, 512)), 0, 1).astype(jnp.int32)
        return (x, ctx_1024, mask_BxS2_ik0)
    x, ctx_1024, mask_BxS2_ik0 = _rec_inputs()

    def _L0_xattn_setup():
        import jax, jax.numpy as jnp
        import numpy as np
        H, DM, LQ, LK, DK, DV = (16, 256, 512, 512, 64, 64)
        B = 2
        key = jax.random.key(seed)
        ks = jax.random.split(key, 12)
        s = 0.02
        return {'Q': jax.random.normal(ks[0], (B, LQ, DM), jnp.float32), 'K': jax.random.normal(ks[1], (B, LK, DM), jnp.float32), 'V': jax.random.normal(ks[2], (B, LK, DM), jnp.float32), 'mask': jax.random.randint(ks[3], (B, LQ), 0, 2, jnp.int32), 'W_Q': jax.random.normal(ks[4], (H * DK, DM), jnp.float32) * s, 'b_Q': jnp.zeros((H * DK,), jnp.float32), 'W_K': jax.random.normal(ks[5], (H * DK, DM), jnp.float32) * s, 'b_K': jnp.zeros((H * DK,), jnp.float32), 'W_V': jax.random.normal(ks[6], (H * DV, DM), jnp.float32) * s, 'b_V': jnp.zeros((H * DV,), jnp.float32), 'W_O': jax.random.normal(ks[7], (DM, H * DV), jnp.float32) * s, 'b_O': jnp.zeros((DM,), jnp.float32)}
    _L0_xattn_all = _L0_xattn_setup()
    _L0_xattn_in = {k: v for k, v in _L0_xattn_all.items() if k in ('W_Q', 'b_Q', 'W_K', 'b_K', 'W_V', 'b_V', 'W_O', 'b_O')}
    del _L0_xattn_all

    def _L1_xattn_setup():
        import jax, jax.numpy as jnp
        import numpy as np
        NUM_ITERATIONS = 3
        LN_EPS = 1e-05
        key = jax.random.key(seed)
        ks = jax.random.split(key, 10)
        B, L, Lv, H = (8, 512, 64, 256)
        s = 1.0 / np.sqrt(H)
        s2 = 1.0 / np.sqrt(2 * H)
        return {'text_feat': jax.random.normal(ks[0], (B, L, H), dtype=jnp.float32), 'vision_feat': jax.random.normal(ks[1], (B, Lv, H), dtype=jnp.float32), 'Wt': jax.random.uniform(ks[2], (H, H), jnp.float32, -s, s), 'bt': jax.random.uniform(ks[3], (H,), jnp.float32, -s, s), 'Wv': jax.random.uniform(ks[4], (H, H), jnp.float32, -s, s), 'bv': jax.random.uniform(ks[5], (H,), jnp.float32, -s, s), 'Wg': jax.random.uniform(ks[6], (H, 2 * H), jnp.float32, -s2, s2), 'bg': jax.random.uniform(ks[7], (H,), jnp.float32, -s2, s2), 'gamma': jnp.ones((H,), jnp.float32), 'beta': jnp.zeros((H,), jnp.float32)}
    _L1_xattn_all = _L1_xattn_setup()
    _L1_xattn_in = {k: v for k, v in _L1_xattn_all.items() if k in ('Wt', 'bt', 'Wv', 'bv', 'Wg', 'bg', 'gamma', 'beta')}
    del _L1_xattn_all

    def _L2_xattn_setup():
        import jax, jax.numpy as jnp
        import numpy as np
        B, S, H, N_HEAD = (2, 512, 256, 16)
        NEG = float(-2 ** 32 + 1)
        EPS = 1e-08
        key = jax.random.key(seed)
        ks = jax.random.split(key, 11)
        sc = 0.02
        return {'queries': jax.random.normal(ks[0], (B, S, H), dtype=jnp.float32), 'keys': jax.random.normal(ks[1], (B, S, H), dtype=jnp.float32), 'values': jax.random.normal(ks[2], (B, S, H), dtype=jnp.float32), 'Wq': jax.random.normal(ks[3], (H, H), dtype=jnp.float32) * sc, 'bq': jax.random.normal(ks[4], (H,), dtype=jnp.float32) * sc, 'Wk': jax.random.normal(ks[5], (H, H), dtype=jnp.float32) * sc, 'bk': jax.random.normal(ks[6], (H,), dtype=jnp.float32) * sc, 'Wv': jax.random.normal(ks[7], (H, H), dtype=jnp.float32) * sc, 'bv': jax.random.normal(ks[8], (H,), dtype=jnp.float32) * sc, 'Wo': jax.random.normal(ks[9], (H, H), dtype=jnp.float32) * sc, 'bo': jax.random.normal(ks[10], (H,), dtype=jnp.float32) * sc}
    _L2_xattn_all = _L2_xattn_setup()
    _L2_xattn_in = {k: v for k, v in _L2_xattn_all.items() if k in ('Wq', 'bq', 'Wk', 'bk', 'Wv', 'bv', 'Wo', 'bo')}
    del _L2_xattn_all

    def _L3_xattn_setup():
        import jax, jax.numpy as jnp
        import numpy as np
        B, L, M, D, H, FF, W = (2, 512, 512, 256, 16, 1024, 64)
        DH = D // H

        def _layernorm(x, g, b, eps=1e-05):
            mu = x.mean(-1, keepdims=True)
            var = ((x - mu) ** 2).mean(-1, keepdims=True)
            return (x - mu) / jnp.sqrt(var + eps) * g + b

        def _mha(qx, kx, wq, bq, wk, bk, wv, bv, wo, bo, mask, bias):
            Bq, Lq, _ = qx.shape
            Lk = kx.shape[1]
            q = (qx @ wq + bq).reshape(Bq, Lq, H, DH).transpose(0, 2, 1, 3)
            k = (kx @ wk + bk).reshape(Bq, Lk, H, DH).transpose(0, 2, 1, 3)
            v = (kx @ wv + bv).reshape(Bq, Lk, H, DH).transpose(0, 2, 1, 3)
            s = jnp.einsum('bhqd,bhkd->bhqk', q, k) / jnp.sqrt(jnp.asarray(DH, qx.dtype))
            if bias is not None:
                s = s + bias[None]
            if mask is not None:
                s = jnp.where(mask[None, None], s, jnp.asarray(-1000000000.0, qx.dtype))
            a = jax.nn.softmax(s, axis=-1)
            o = jnp.einsum('bhqk,bhkd->bhqd', a, v).transpose(0, 2, 1, 3).reshape(Bq, Lq, D)
            return o @ wo + bo

        def _forward(x, mem, swq, sbq, swk, sbk, swv, sbv, swo, sbo, cwq, cbq, cwk, cbk, cwv, cbv, cwo, cbo, w1, b1, w2, b2, g1, be1, g2, be2, g3, be3):
            i = jnp.arange(L)[:, None]
            j = jnp.arange(L)[None, :]
            mask = (j <= i) & (i - j < W)
            slopes = 2.0 ** (-8.0 * jnp.arange(1, H + 1, dtype=x.dtype) / H)
            bias = slopes[:, None, None] * (j - i).astype(x.dtype)[None]
            sa = _mha(x, x, swq, sbq, swk, sbk, swv, sbv, swo, sbo, mask, bias)
            x = _layernorm(x + sa, g1, be1)
            ca = _mha(x, mem, cwq, cbq, cwk, cbk, cwv, cbv, cwo, cbo, None, None)
            x = _layernorm(x + ca, g2, be2)
            ff = jax.nn.gelu(x @ w1 + b1, approximate=False) @ w2 + b2
            return _layernorm(x + ff, g3, be3)
        key = jax.random.key(seed)
        ks = jax.random.split(key, 16)
        s = 0.02
        inp = {'x': jax.random.normal(ks[0], (B, L, D), jnp.float32), 'mem': jax.random.normal(ks[1], (B, M, D), jnp.float32)}
        for n, k in zip(['swq', 'swk', 'swv', 'swo'], jax.random.split(ks[2], 4)):
            inp[n] = jax.random.normal(k, (D, D), jnp.float32) * s
        for n in ['sbq', 'sbk', 'sbv', 'sbo']:
            inp[n] = jnp.zeros((D,), jnp.float32)
        for n, k in zip(['cwq', 'cwk', 'cwv', 'cwo'], jax.random.split(ks[3], 4)):
            inp[n] = jax.random.normal(k, (D, D), jnp.float32) * s
        for n in ['cbq', 'cbk', 'cbv', 'cbo']:
            inp[n] = jnp.zeros((D,), jnp.float32)
        inp['w1'] = jax.random.normal(ks[4], (D, FF), jnp.float32) * s
        inp['b1'] = jnp.zeros((FF,), jnp.float32)
        inp['w2'] = jax.random.normal(ks[5], (FF, D), jnp.float32) * s
        inp['b2'] = jnp.zeros((D,), jnp.float32)
        for n in ['g1', 'g2', 'g3']:
            inp[n] = jnp.ones((D,), jnp.float32)
        for n in ['be1', 'be2', 'be3']:
            inp[n] = jnp.zeros((D,), jnp.float32)
        return inp
    _L3_xattn_all = _L3_xattn_setup()
    _L3_xattn_in = {k: v for k, v in _L3_xattn_all.items() if k in ('swq', 'sbq', 'swk', 'sbk', 'swv', 'sbv', 'swo', 'sbo', 'cwq', 'cbq', 'cwk', 'cbk', 'cwv', 'cbv', 'cwo', 'cbo', 'w1', 'b1', 'w2', 'b2', 'g1', 'be1', 'g2', 'be2', 'g3', 'be3')}
    del _L3_xattn_all
    return {'x': x, 'ctx_1024': ctx_1024, 'mask_BxS2_ik0': mask_BxS2_ik0, 'L0_xattn_W_Q': _L0_xattn_in['W_Q'], 'L0_xattn_b_Q': _L0_xattn_in['b_Q'], 'L0_xattn_W_K': _L0_xattn_in['W_K'], 'L0_xattn_b_K': _L0_xattn_in['b_K'], 'L0_xattn_W_V': _L0_xattn_in['W_V'], 'L0_xattn_b_V': _L0_xattn_in['b_V'], 'L0_xattn_W_O': _L0_xattn_in['W_O'], 'L0_xattn_b_O': _L0_xattn_in['b_O'], 'L1_xattn_Wt': _L1_xattn_in['Wt'], 'L1_xattn_bt': _L1_xattn_in['bt'], 'L1_xattn_Wv': _L1_xattn_in['Wv'], 'L1_xattn_bv': _L1_xattn_in['bv'], 'L1_xattn_Wg': _L1_xattn_in['Wg'], 'L1_xattn_bg': _L1_xattn_in['bg'], 'L1_xattn_gamma': _L1_xattn_in['gamma'], 'L1_xattn_beta': _L1_xattn_in['beta'], 'L2_xattn_Wq': _L2_xattn_in['Wq'], 'L2_xattn_bq': _L2_xattn_in['bq'], 'L2_xattn_Wk': _L2_xattn_in['Wk'], 'L2_xattn_bk': _L2_xattn_in['bk'], 'L2_xattn_Wv': _L2_xattn_in['Wv'], 'L2_xattn_bv': _L2_xattn_in['bv'], 'L2_xattn_Wo': _L2_xattn_in['Wo'], 'L2_xattn_bo': _L2_xattn_in['bo'], 'L3_xattn_swq': _L3_xattn_in['swq'], 'L3_xattn_sbq': _L3_xattn_in['sbq'], 'L3_xattn_swk': _L3_xattn_in['swk'], 'L3_xattn_sbk': _L3_xattn_in['sbk'], 'L3_xattn_swv': _L3_xattn_in['swv'], 'L3_xattn_sbv': _L3_xattn_in['sbv'], 'L3_xattn_swo': _L3_xattn_in['swo'], 'L3_xattn_sbo': _L3_xattn_in['sbo'], 'L3_xattn_cwq': _L3_xattn_in['cwq'], 'L3_xattn_cbq': _L3_xattn_in['cbq'], 'L3_xattn_cwk': _L3_xattn_in['cwk'], 'L3_xattn_cbk': _L3_xattn_in['cbk'], 'L3_xattn_cwv': _L3_xattn_in['cwv'], 'L3_xattn_cbv': _L3_xattn_in['cbv'], 'L3_xattn_cwo': _L3_xattn_in['cwo'], 'L3_xattn_cbo': _L3_xattn_in['cbo'], 'L3_xattn_w1': _L3_xattn_in['w1'], 'L3_xattn_b1': _L3_xattn_in['b1'], 'L3_xattn_w2': _L3_xattn_in['w2'], 'L3_xattn_b2': _L3_xattn_in['b2'], 'L3_xattn_g1': _L3_xattn_in['g1'], 'L3_xattn_be1': _L3_xattn_in['be1'], 'L3_xattn_g2': _L3_xattn_in['g2'], 'L3_xattn_be2': _L3_xattn_in['be2'], 'L3_xattn_g3': _L3_xattn_in['g3'], 'L3_xattn_be3': _L3_xattn_in['be3']}

def reference(x, ctx_1024, mask_BxS2_ik0, L0_xattn_W_Q, L0_xattn_b_Q, L0_xattn_W_K, L0_xattn_b_K, L0_xattn_W_V, L0_xattn_b_V, L0_xattn_W_O, L0_xattn_b_O, L1_xattn_Wt, L1_xattn_bt, L1_xattn_Wv, L1_xattn_bv, L1_xattn_Wg, L1_xattn_bg, L1_xattn_gamma, L1_xattn_beta, L2_xattn_Wq, L2_xattn_bq, L2_xattn_Wk, L2_xattn_bk, L2_xattn_Wv, L2_xattn_bv, L2_xattn_Wo, L2_xattn_bo, L3_xattn_swq, L3_xattn_sbq, L3_xattn_swk, L3_xattn_sbk, L3_xattn_swv, L3_xattn_sbv, L3_xattn_swo, L3_xattn_sbo, L3_xattn_cwq, L3_xattn_cbq, L3_xattn_cwk, L3_xattn_cbk, L3_xattn_cwv, L3_xattn_cbv, L3_xattn_cwo, L3_xattn_cbo, L3_xattn_w1, L3_xattn_b1, L3_xattn_w2, L3_xattn_b2, L3_xattn_g1, L3_xattn_be1, L3_xattn_g2, L3_xattn_be2, L3_xattn_g3, L3_xattn_be3):
    import jax
    import jax.numpy as jnp

    def _L0_xattn_ref(Q, K, V, mask, W_Q, b_Q, W_K, b_K, W_V, b_V, W_O, b_O):
        import jax, jax.numpy as jnp
        import numpy as np
        H, DM, LQ, LK, DK, DV = (16, 256, 512, 512, 64, 64)
        B = 2
        b = Q.shape[0]
        q = (Q @ W_Q.T + b_Q).reshape(b, LQ, H, DK)
        k = (K @ W_K.T + b_K).reshape(b, LK, H, DK)
        v = (V @ W_V.T + b_V).reshape(b, LK, H, DV)
        A = jnp.einsum('bqhd,bkhd->bhqk', q, k) / jnp.sqrt(jnp.float32(DK))
        A = jnp.where(mask[:, None, :, None] == 0, -jnp.inf, A)
        alpha = jax.nn.softmax(A, axis=2)
        out = jnp.einsum('bhqk,bkhd->bqhd', alpha, v).reshape(b, LQ, H * DV)
        return out @ W_O.T + b_O + Q

    def _L1_xattn_ref(text_feat, vision_feat, Wt, bt, Wv, bv, Wg, bg, gamma, beta):
        import jax, jax.numpy as jnp
        import numpy as np
        NUM_ITERATIONS = 3
        LN_EPS = 1e-05
        B, L, H = text_feat.shape
        vision_pooled = jnp.mean(vision_feat, axis=1, keepdims=True)
        text_proj = jnp.einsum('blh,oh->blo', text_feat, Wt) + bt
        vision_proj = jnp.einsum('bkh,oh->bko', vision_pooled, Wv) + bv
        vision_proj = jnp.broadcast_to(vision_proj, (B, L, H))
        agreement = jnp.sum(text_proj * vision_proj, axis=-1, keepdims=True)
        coupling = jnp.zeros((B, L, 1), dtype=text_feat.dtype)
        fused = text_feat
        for _ in range(NUM_ITERATIONS):
            routing_weights = jax.nn.softmax(coupling, axis=1)
            weighted_vision = routing_weights * vision_proj
            Wg_t, Wg_v = (Wg[:, :H], Wg[:, H:])
            gate_pre = jnp.einsum('blh,oh->blo', text_proj, Wg_t) + jnp.einsum('blh,oh->blo', weighted_vision, Wg_v) + bg
            gate = jax.nn.sigmoid(gate_pre)
            fused = text_feat + gate * weighted_vision
            coupling = coupling + agreement
        mu = jnp.mean(fused, axis=-1, keepdims=True)
        var = jnp.mean(jnp.square(fused - mu), axis=-1, keepdims=True)
        out = (fused - mu) / jnp.sqrt(var + LN_EPS) * gamma + beta
        return out

    def _L2_xattn_ref(queries, keys, values, Wq, bq, Wk, bk, Wv, bv, Wo, bo):
        import jax, jax.numpy as jnp
        import numpy as np
        B, S, H, N_HEAD = (2, 512, 256, 16)
        NEG = float(-2 ** 32 + 1)
        EPS = 1e-08
        n = N_HEAD
        Bb, Sq, Hh = queries.shape
        Sk = keys.shape[1]
        d = Hh // n
        Q = jax.nn.relu(queries @ Wq + bq)
        K = jax.nn.relu(keys @ Wk + bk)
        V = jax.nn.relu(values @ Wv + bv)
        Q_ = Q.reshape(Bb, Sq, n, d).transpose(2, 0, 1, 3)
        K_ = K.reshape(Bb, Sk, n, d).transpose(2, 0, 1, 3)
        V_ = V.reshape(Bb, Sk, n, d).transpose(2, 0, 1, 3)
        key_masks = jnp.sign(jnp.abs(jnp.sum(K, axis=-1)))
        scores = jnp.einsum('hbqd,hbkd->hbqk', Q_, K_) / d ** 0.5
        scores = jnp.where(key_masks[None, :, None, :] == 0.0, NEG, scores)
        tril = jnp.tril(jnp.ones((Sq, Sk), dtype=scores.dtype))
        scores = jnp.where(tril[None, None] == 0.0, NEG, scores)
        attn = jax.nn.softmax(scores, axis=-1)
        out = jnp.einsum('hbqk,hbkd->hbqd', attn, V_)
        out = out.transpose(1, 2, 0, 3).reshape(Bb, Sq, Hh)
        out = jax.nn.relu(out @ Wo + bo)
        out = queries + out
        mean = out.mean(axis=-1, keepdims=True)
        std = jnp.std(out, axis=-1, ddof=1, keepdims=True)
        return (out - mean) / (std + EPS)

    def _L3_xattn_ref(x, mem, swq, sbq, swk, sbk, swv, sbv, swo, sbo, cwq, cbq, cwk, cbk, cwv, cbv, cwo, cbo, w1, b1, w2, b2, g1, be1, g2, be2, g3, be3):
        import jax, jax.numpy as jnp
        import numpy as np
        B, L, M, D, H, FF, W = (2, 512, 512, 256, 16, 1024, 64)
        DH = D // H

        def _layernorm(x, g, b, eps=1e-05):
            mu = x.mean(-1, keepdims=True)
            var = ((x - mu) ** 2).mean(-1, keepdims=True)
            return (x - mu) / jnp.sqrt(var + eps) * g + b

        def _mha(qx, kx, wq, bq, wk, bk, wv, bv, wo, bo, mask, bias):
            Bq, Lq, _ = qx.shape
            Lk = kx.shape[1]
            q = (qx @ wq + bq).reshape(Bq, Lq, H, DH).transpose(0, 2, 1, 3)
            k = (kx @ wk + bk).reshape(Bq, Lk, H, DH).transpose(0, 2, 1, 3)
            v = (kx @ wv + bv).reshape(Bq, Lk, H, DH).transpose(0, 2, 1, 3)
            s = jnp.einsum('bhqd,bhkd->bhqk', q, k) / jnp.sqrt(jnp.asarray(DH, qx.dtype))
            if bias is not None:
                s = s + bias[None]
            if mask is not None:
                s = jnp.where(mask[None, None], s, jnp.asarray(-1000000000.0, qx.dtype))
            a = jax.nn.softmax(s, axis=-1)
            o = jnp.einsum('bhqk,bhkd->bhqd', a, v).transpose(0, 2, 1, 3).reshape(Bq, Lq, D)
            return o @ wo + bo

        def _forward(x, mem, swq, sbq, swk, sbk, swv, sbv, swo, sbo, cwq, cbq, cwk, cbk, cwv, cbv, cwo, cbo, w1, b1, w2, b2, g1, be1, g2, be2, g3, be3):
            i = jnp.arange(L)[:, None]
            j = jnp.arange(L)[None, :]
            mask = (j <= i) & (i - j < W)
            slopes = 2.0 ** (-8.0 * jnp.arange(1, H + 1, dtype=x.dtype) / H)
            bias = slopes[:, None, None] * (j - i).astype(x.dtype)[None]
            sa = _mha(x, x, swq, sbq, swk, sbk, swv, sbv, swo, sbo, mask, bias)
            x = _layernorm(x + sa, g1, be1)
            ca = _mha(x, mem, cwq, cbq, cwk, cbk, cwv, cbv, cwo, cbo, None, None)
            x = _layernorm(x + ca, g2, be2)
            ff = jax.nn.gelu(x @ w1 + b1, approximate=False) @ w2 + b2
            return _layernorm(x + ff, g3, be3)
        return _forward(x, mem, swq, sbq, swk, sbk, swv, sbv, swo, sbo, cwq, cbq, cwk, cbk, cwv, cbv, cwo, cbo, w1, b1, w2, b2, g1, be1, g2, be2, g3, be3)
    x = _L0_xattn_ref(x, ctx_1024, ctx_1024, mask_BxS2_ik0, L0_xattn_W_Q, L0_xattn_b_Q, L0_xattn_W_K, L0_xattn_b_K, L0_xattn_W_V, L0_xattn_b_V, L0_xattn_W_O, L0_xattn_b_O)
    x = _L1_xattn_ref(x, ctx_1024, L1_xattn_Wt, L1_xattn_bt, L1_xattn_Wv, L1_xattn_bv, L1_xattn_Wg, L1_xattn_bg, L1_xattn_gamma, L1_xattn_beta)
    x = _L2_xattn_ref(x, ctx_1024, ctx_1024, L2_xattn_Wq, L2_xattn_bq, L2_xattn_Wk, L2_xattn_bk, L2_xattn_Wv, L2_xattn_bv, L2_xattn_Wo, L2_xattn_bo)
    x = _L3_xattn_ref(x, ctx_1024, L3_xattn_swq, L3_xattn_sbq, L3_xattn_swk, L3_xattn_sbk, L3_xattn_swv, L3_xattn_sbv, L3_xattn_swo, L3_xattn_sbo, L3_xattn_cwq, L3_xattn_cbq, L3_xattn_cwk, L3_xattn_cbk, L3_xattn_cwv, L3_xattn_cbv, L3_xattn_cwo, L3_xattn_cbo, L3_xattn_w1, L3_xattn_b1, L3_xattn_w2, L3_xattn_b2, L3_xattn_g1, L3_xattn_be1, L3_xattn_g2, L3_xattn_be2, L3_xattn_g3, L3_xattn_be3)
    return x

_drawn_inputs = setup_inputs


def setup_inputs(seed=0):
    import zlib

    import numpy as np

    out = dict(_drawn_inputs(seed))
    spreads = {'L0_xattn_b_Q': (0.0, 2.0),
     'L0_xattn_b_K': (0.0, 0.8),
     'L0_xattn_b_V': (0.0, 0.1),
     'L0_xattn_b_O': (0.0, 0.1),
     'L1_xattn_gamma': (1.0, 0.2),
     'L1_xattn_beta': (0.0, 0.1),
     'L3_xattn_sbq': (0.0, 0.8),
     'L3_xattn_sbk': (0.0, 2.0),
     'L3_xattn_sbv': (0.0, 0.275),
     'L3_xattn_sbo': (0.0, 0.1),
     'L3_xattn_cbq': (0.0, 0.8),
     'L3_xattn_cbk': (0.0, 2.0),
     'L3_xattn_cbv': (0.0, 0.1),
     'L3_xattn_cbo': (0.0, 0.1),
     'L3_xattn_b1': (0.0, 0.1),
     'L3_xattn_b2': (0.0, 0.1),
     'L3_xattn_g1': (1.0, 0.2),
     'L3_xattn_be1': (0.0, 0.1),
     'L3_xattn_g2': (1.0, 0.2),
     'L3_xattn_be2': (0.0, 0.1),
     'L3_xattn_g3': (1.0, 0.2),
     'L3_xattn_be3': (0.0, 0.1)}
    factors = {'L0_xattn_W_Q': 3.885,
     'L0_xattn_W_K': 4.276,
     'L1_xattn_Wt': 21.86,
     'L1_xattn_bt': 64.0,
     'L1_xattn_Wv': 8.0,
     'L1_xattn_bv': 64.0,
     'L1_xattn_Wg': 38.138,
     'L1_xattn_bg': 64.0,
     'L2_xattn_Wq': 8.0,
     'L2_xattn_bq': 45.081,
     'L2_xattn_Wk': 8.0,
     'L2_xattn_bk': 64.0,
     'L2_xattn_Wv': 3.521,
     'L2_xattn_bv': 23.937,
     'L2_xattn_bo': 4.588,
     'L3_xattn_swq': 8.0,
     'L3_xattn_swk': 8.0,
     'L3_xattn_cwq': 8.0,
     'L3_xattn_cwk': 8.0}
    for name, (base, spread) in spreads.items():
        noise = np.random.default_rng([zlib.crc32(name.encode()), seed]).standard_normal(out[name].shape)
        drawn = base * np.exp(spread * noise) if base else spread * noise
        out[name] = jnp.asarray(drawn.astype(out[name].dtype))
    for name, factor in factors.items():
        out[name] = (out[name] * factor).astype(out[name].dtype)
    return out
```

```python
from contextlib import ExitStack

import concourse.bass as bass
from concourse import mybir

ALU = mybir.AluOpType
ACT = mybir.ActivationFunctionType
F32 = mybir.dt.float32
BF16 = mybir.dt.bfloat16
I32 = mybir.dt.int32
AX = mybir.AxisListType

B, S, D = 4, 512, 256
P = 128
NT = S // P
DT = D // P
H = 16
DK0 = 64
HD0 = H * DK0
PAIRS = H // 2
DH = D // H
GROUPS = H // 4
FF = 1024
FT = FF // P
W = 64
BAND = P + W
NEG = -1.0e30
CAUSAL, BANDED, FULL = range(3)
SLOTS = 3
UNITS0 = PAIRS * NT
UNITS = GROUPS * NT
PV_ITER = UNITS0 + 3 * UNITS
OUT_ITER = PAIRS + 3 * GROUPS

COLS = [("bq0", 8), ("bk0", 8), ("bt", 2), ("bq2", 2), ("bk2", 2), ("sbq", 2), ("sbk", 2), ("cbq", 2), ("cbk", 2),
        ("b1", 8), ("ga1", 2), ("be1", 2), ("g1", 2), ("b1n", 2), ("g2", 2), ("b2n", 2)]
ROWS = [("bv0", 4), ("bo0", 1), ("bv1", 1), ("bg", 1), ("ga1", 1), ("be1", 1), ("bv2", 1), ("bo2", 1), ("sbv", 1),
        ("cbv", 1), ("b2", 1), ("g1", 1), ("b1n", 1), ("g2", 1), ("b2n", 1), ("g3", 1), ("b3n", 1)]
CONSTS = [("ident", P), ("maskA", P), ("maskB", P), ("bandA", BAND), ("bandB", BAND),
          ("rowsB0", P), ("rowsB1", P), ("rowsJ", BAND), ("slopeA", 4 * P), ("tri", P),
          ("slopeM", 4 * P), ("even", 2)]


def offsets(parts):
    at, out = 0, {}
    for name, n in parts:
        out[name] = at
        at += n
    return out, at


COL, NCOLS = offsets(COLS)
ROW, NROWS = offsets(ROWS)
CST, NCONST = offsets(CONSTS)
NBF = CST["tri"]


def heads_of(g):
    return [8 * (g // 2) + 2 * s + g % 2 for s in range(4)]


def attention_jobs(a):
    jobs = [(a, "A", 0, qt, u) for qt in range(NT) for u in range(2)]
    for g in range(GROUPS):
        jobs.append((a, "T", g))
        for t in range(NT):
            for u in range(2):
                jobs.append((a, "B", g, t, u))
                if g + 1 < GROUPS:
                    jobs.append((a, "A", g + 1, t, u))
    return jobs


def plan_jobs():
    jobs = [("V0", t) for t in range(NT)] + [("QK0", 0)]
    for p in range(PAIRS):
        jobs += [("S0", p, kt) for kt in range(NT)]
        if p + 1 < PAIRS:
            jobs.append(("QK0", p + 1))
    jobs += [("O0", j) for j in range(2)]
    jobs += [("vp",), ("vpT",), ("X", 0), ("K2",)] + [("V2", j) for j in range(2)] + [("uv",), ("tp",), ("ksum",), ("agree",)]
    jobs += [("cnt",), ("rcol",), ("meanV",)] + [("gate", j) for j in range(2)] + [("meanO",), ("KC",)]
    jobs += [("VC", j) for j in range(2)] + [("X", 1), ("Q2",)]
    jobs += attention_jobs(CAUSAL) + [("O2", j) for j in range(2)] + [("X", 2), ("QS",), ("KS",)] + [("VS", j) for j in range(2)]
    jobs += attention_jobs(BANDED) + [("OS", j) for j in range(2)] + [("X", 3), ("QC",)]
    jobs += attention_jobs(FULL) + [("OC", j) for j in range(2)] + [("X", 4)]
    jobs += [("F1", j) for j in range(FT // 2)] + [("F2", j) for j in range(2)]
    while len(jobs) % SLOTS:
        jobs.append(("pad", len(jobs)))
    return jobs


JOBS = plan_jobs()
JOB = {name: n for n, name in enumerate(JOBS)}
ROUNDS = len(JOBS) // SLOTS

DVE_LINKS = 92
ACT_LINKS = 5
POOL_LINKS = 4
HOLDS = UNITS0 + 5 + 3 * GROUPS


def build(nc, io, out):
    with ExitStack() as ctx:
        def sb(name, shape, dt=F32):
            return ctx.enter_context(nc.sbuf_tensor(name, shape, dt))

        def sem(name):
            return ctx.enter_context(nc.semaphore(name))

        ring = ctx.enter_context(nc.psum_tensor("ring", [P, SLOTS, 2, 512], F32))
        obank = ctx.enter_context(nc.psum_tensor("obank", [P, 2, 512], F32))

        wq0 = sb("wq0", [P, DT, HD0])
        wk0 = sb("wk0", [P, DT, HD0])
        wvo = sb("wvo", [P, 2048])
        wv0 = wvo[:, :].rearrange("p (t n) -> p t n", t=DT)
        wo0 = wvo[:, :].rearrange("p (t n) -> p t n", t=HD0 // P)
        w_l1 = {n: sb("w1_" + n, [P, DT, D]) for n in ("t", "v", "gt", "gv")}
        w_sq = {n: sb("w_" + n, [P, DT, D]) for n in ("q2", "k2", "v2", "sq", "sk", "sv", "cq", "ck", "cv")}
        w_out = {a: sb(f"w_out{a}", [P, GROUPS, D]) for a in (CAUSAL, BANDED, FULL)}
        w_om = sb("w_om", [P, DT, D])
        cols = sb("cols", [P, NCOLS])
        rows = sb("rows", [P, NROWS, D])
        ident = sb("ident", [P, P])
        tri = sb("tri", [P, P])
        even = sb("even", [P, 2])
        ones = sb("ones", [P, P])
        cbf = sb("cbf", [P, NBF], BF16)
        kcol = sb("kcol", [P, 3, 2, DT])
        qcol = sb("qcol", [P, 8])
        km4 = sb("km4", [P, 2])
        epsc = sb("epsc", [P, 1])

        act_t = sb("act_t", [P, DT, S])
        ctx_t = sb("ctx_t", [P, DT, S])
        region_e = sb("region_e", [P, 8192])
        region_b = sb("region_b", [P, 4096])
        region_c = sb("region_c", [P, 4096])
        region_d = sb("region_d", [P, 2048])
        region_q = sb("region_q", [P, 2048])
        e0 = region_e[:, :].rearrange("p (u h q) -> p u h q", u=8, h=2)
        e16 = region_e[:, :].rearrange("p (u s q) -> p u s q", u=4, s=4)
        hid = region_e[:, 0:4096].rearrange("p (t q) -> p t q", t=FT)
        v0 = region_b[:, :].rearrange("p (t n) -> p t n", t=NT)
        w_f1 = region_b[:, 0:2048].rearrange("p (t n) -> p t n", t=DT)
        w_f2 = region_b[:, 2048:4096].rearrange("p (t n) -> p t n", t=FT)
        o0 = region_c[:, :].rearrange("p (t q) -> p t q", t=PAIRS)

        def kv(region):
            return (region[:, 0:2048].rearrange("p (e t k) -> p e t k", e=2, t=DT),
                    region[:, 2048:4096].rearrange("p (t h c) -> p t h c", t=NT, h=H))

        k_of = {CAUSAL: kv(region_b)[0], BANDED: kv(region_b)[0], FULL: kv(region_c)[0]}
        v_of = {CAUSAL: kv(region_b)[1], BANDED: kv(region_b)[1], FULL: kv(region_c)[1]}
        sm0 = region_d[:, :].rearrange("p (u h q) -> p u h q", u=2, h=2)
        v2 = region_d[:, 0:1024].rearrange("p (t n) -> p t n", t=NT)
        oT = region_d[:, :].rearrange("p (g q) -> p g q", g=GROUPS)
        qk0 = region_q[:, :].rearrange("p (u a q) -> p u a q", u=2, a=2)
        tp_t = region_q[:, 0:1024].rearrange("p (t q) -> p t q", t=DT)
        q_t = region_q[:, 1024:2048].rearrange("p (t q) -> p t q", t=DT)

        vs0 = sb("vs0", [P, 4, 2, DK0])
        rbuf = sb("rbuf", [P, S])
        mask_i = rbuf[:, :].bitcast(I32)
        maskb = sb("maskb", [P, S])
        nat_x = sb("nat_x", [P, NT, D])
        nat_y = sb("nat_y", [P, NT, D])
        x_nat = nat_y
        nat_n = sb("nat_n", [P, NT, D])
        mrow = sb("mrow", [P, 2, S], BF16)
        mcol = sb("mcol", [P, 2, NT, P], BF16)
        mcol_s = sb("mcol_s", [P, GROUPS, NT, P], BF16)
        nmin0 = sb("nmin0", [P, UNITS0, 2])
        sum0 = sb("sum0", [P, UNITS0, 2])
        rs0 = sb("rs0", [P, UNITS0, 2])
        nmax = sb("nmax", [P, NT, 4])
        nanfix = sb("nanfix", [P, 4])
        stats = sb("stats", [P, NT, 6])
        mv = sb("mv", [P, NT, 2])
        lnv = sb("lnv", [P, NT])
        std = sb("std", [P, NT])
        rstd = sb("rstd", [P, NT])
        std1 = sb("std1", [P, NT])
        pooled = sb("pooled", [P, DT])
        small = sb("small", [P, DT])
        held = sb("held", [P, HOLDS + SLOTS])
        rrow = rbuf
        one_sum = sb("one_sum", [1, 4])
        rcol = sb("rcol", [P, NT])
        vp_b = region_q[:, 1024:1024 + D]
        u_b = region_q[:, 1024 + D:1024 + 2 * D]
        wide = sb("wide", [P, DT, P])
        km = sb("km", [P, NT])
        degen = sb("degen", [P, NT])
        mean_o = sb("mean_o", [P, D])

        def col(name, t=0):
            return cols[:, COL[name] + t:COL[name] + t + 1]

        def row(name, n=1):
            return rows[:, ROW[name]:ROW[name] + n, :]

        def cb(name, n, part=slice(0, P), at=0):
            return cbf[part, CST[name] + at:CST[name] + at + n]

        filled = [sem(f"filled{s}") for s in range(SLOTS)]
        drained = [sem(f"drained{s}") for s in range(SLOTS)]
        pv_done = sem("pv_done")
        out_drained = sem("out_drained")
        exp0_done = sem("exp0_done")
        exp_done = sem("exp_done")
        vs_ready = sem("vs_ready")
        k_loaded = {n: sem("ld_" + n) for n in ("act", "ctx", "x", "mask", "wq0", "wk0", "wv0", "wo0", "ff", "small",
                                               "const", "l1", "l2", "ls", "lc")}
        stored = sem("stored")
        setup_dve = sem("setup_dve")
        setup_act = sem("setup_act")
        setup_pool = sem("setup_pool")
        dve_link = sem("dve_link")
        act_link = sem("act_link")
        pool_link = sem("pool_link")
        mask_ready = sem("mask_ready")
        resid0_ready = sem("resid0_ready")
        pooled_ready = sem("pooled_ready")
        wide_ready = sem("wide_ready")
        agree_max = sem("agree_max")
        agree_exp = sem("agree_exp")
        agree_inv = sem("agree_inv")
        gate_ready = sem("gate_ready")
        km_ready = sem("km_ready")
        vmask_ready = sem("vmask_ready")
        ones_ready = sem("ones_ready")
        mcol_ready = sem("mcol_ready")
        heads_ready = sem("heads_ready")
        heads0_ready = sem("heads0_ready")
        var_ready = sem("var_ready")
        rstd_ready = sem("rstd_ready")
        norm_ready = sem("norm_ready")
        resid_ready = sem("resid_ready")

        def slot(name):
            return ring[:, JOB[name] % SLOTS, :, :]

        def filled_by(name, b):
            return filled[JOB[name] % SLOTS], b * ROUNDS + JOB[name] // SLOTS + 1

        def drained_by(name, b):
            return drained[JOB[name] % SLOTS], b * ROUNDS + JOB[name] // SLOTS + 2

        def free_for(name, b):
            return drained[JOB[name] % SLOTS], b * ROUNDS + JOB[name] // SLOTS + 1

        def ends_fill(name):
            return filled[JOB[name] % SLOTS], 1

        def ends_drain(name):
            return drained[JOB[name] % SLOTS], 1

        def width(a, g_tile):
            if a == FULL:
                return 0, S
            if a == CAUSAL:
                return P * g_tile, S - P * g_tile
            return P * g_tile, min(BAND, S - P * g_tile)

        def seen(a, qt):
            if a == FULL:
                return 0, S
            if a == CAUSAL:
                return 0, P * (qt + 1)
            lo = max(0, P * qt - W)
            return lo, P * (qt + 1) - lo

        block = ctx.enter_context(nc.Block())

        @block.sync
        def _(sp):
            def load(dst, src, name):
                sp.dma_start(dst, src).then_inc(k_loaded[name], 16)

            def load_act(b):
                load(act_t[:, :, :], io["xT"][b].rearrange("(t p) s -> p t s", p=P), "act")

            def load_ctx(b):
                load(ctx_t[:, :, :], io["ctxT"][b].rearrange("(t p) s -> p t s", p=P), "ctx")

            def load_x(b):
                load(x_nat[:, :, :], io["x"][b].rearrange("(t p) d -> p t d", p=P), "x")

            def load_mask(b):
                load(mask_i, io["mask"][b:b + 1, :].broadcast_to([P, S]), "mask")

            load_ctx(0)
            load(wv0, io["wv0"].rearrange("(t p) n -> p t n", p=P), "wv0")
            load_act(0)
            load(wq0[:, :, :], io["wq0"].rearrange("(t p) n -> p t n", p=P), "wq0")
            load(wk0[:, :, :], io["wk0"].rearrange("(t p) n -> p t n", p=P), "wk0")
            load_mask(0)
            load_x(0)
            for n in ("t", "v", "gt", "gv"):
                load(w_l1[n][:, :, :], io["w1_" + n].rearrange("(t p) n -> p t n", p=P), "l1")
            for names, a, s in ((("q2", "k2", "v2"), CAUSAL, "l2"), (("sq", "sk", "sv"), BANDED, "ls"),
                                (("cq", "ck", "cv"), FULL, "lc")):
                for n in names:
                    load(w_sq[n][:, :, :], io["w_" + n].rearrange("(t p) n -> p t n", p=P), s)
                load(w_out[a][:, :, :], io[f"w_out{a}"].rearrange("(g p) n -> p g n", p=P), s)
                if a == CAUSAL:
                    load(w_om[:, :, :], io["w_om"].rearrange("(t p) n -> p t n", p=P), s)
            for b in range(B):
                for t in range(NT):
                    sp.wait_ge(*filled_by(("V0", t), b))
                if b:
                    sp.wait_ge(stored, b * 16)
                load(wo0, io["wo0"].rearrange("(t p) n -> p t n", p=P), "wo0")
                if b + 1 < B:
                    for j in range(2):
                        sp.wait_ge(*filled_by(("O0", j), b))
                        sp.wait_ge(*drained_by(("O0", j), b))
                    load(wv0, io["wv0"].rearrange("(t p) n -> p t n", p=P), "wv0")
                    sp.wait_ge(*filled_by(("KC",), b))
                    sp.wait_ge(*filled_by(("VC", 0), b))
                    sp.wait_ge(*filled_by(("VC", 1), b))
                    sp.wait_ge(pooled_ready, b + 1)
                    load_ctx(b + 1)
                sp.wait_ge(pv_done, b * PV_ITER + UNITS0 + 2 * UNITS)
                load(w_f1, io["w_f1"].rearrange("(t p) n -> p t n", p=P), "ff")
                load(w_f2, io["w_f2"].rearrange("(t p) n -> p t n", p=P), "ff")
                if b + 1 < B:
                    sp.wait_ge(out_drained, (b + 1) * OUT_ITER)
                    load_mask(b + 1)
                    for j in range(FT // 2):
                        sp.wait_ge(*filled_by(("F1", j), b))
                    load_act(b + 1)
                    sp.wait_ge(norm_ready, (b + 1) * 5)
                    load_x(b + 1)
                sp.wait_ge(resid_ready, (b + 1) * 4)
                sp.dma_start(out[b].rearrange("(t p) d -> p t d", p=P), nat_x[:, :, :]).then_inc(stored, 16)
            sp.wait_ge(stored, B * 16)

        @block.gpsimd
        def _(pool):
            pool.memset(ones[:, :], 1.0).then_inc(setup_pool, 1)
            pool.memset(mcol[:, :, :, :], 0.0).then_inc(setup_pool, 1)
            pool.memset(epsc[:, :], 1e-5).then_inc(setup_pool, 1)
            for s in range(SLOTS):
                pool.memset(held[:, HOLDS + s:HOLDS + s + 1], 0.0).then_inc(drained[s], 1)
            pool.wait_ge(k_loaded["small"], 32)
            pool.tensor_tensor(row("b2n"), row("b2n"), row("b2"), ALU.add).then_inc(setup_pool, 1)
            pool.wait_ge(setup_pool, 4)

            def wide_row(name):
                return row(name).broadcast_to([P, NT, D])

            with pool.Fori(0, B) as b:
                links = [0]

                def link(ins):
                    links[0] += 1
                    ins.then_inc(pool_link, 1)
                    pool.wait_ge(pool_link, b * POOL_LINKS + links[0])

                def put_ones(v):
                    one = ones[:, 0:NT * H].rearrange("p (t h) -> p t h", t=NT).unsqueeze(3).broadcast_to([P, NT, H, DH])
                    pool.tensor_tensor(v[:, :, :, DH:2 * DH], one, one, ALU.mult).then_inc(ones_ready, 1)

                pool.wait_ge(k_loaded["x"], b * 16 + 16)
                pool.tensor_tensor(x_nat[:, :, :], x_nat[:, :, :], wide_row("bo0"), ALU.add).then_inc(resid0_ready, 1)

                pool.wait_ge(*filled_by(("VC", 0), b))
                put_ones(v_of[FULL])

                def residual(n, gamma, beta):
                    pool.wait_ge(norm_ready, b * 5 + n + 1)
                    link(pool.tensor_tensor(nat_x[:, :, :], nat_n[:, :, :], wide_row(gamma), ALU.mult))
                    pool.tensor_tensor(nat_x[:, :, :], nat_x[:, :, :], wide_row(beta), ALU.add).then_inc(resid_ready, 1)

                residual(0, "ga1", "be1")
                pool.wait_ge(*filled_by(("VS", 0), b))
                put_ones(v_of[BANDED])
                residual(2, "g1", "b1n")
                residual(3, "g2", "b2n")
                residual(4, "g3", "b3n")
                assert links[0] == POOL_LINKS, links

        @block.scalar
        def _(act):
            act.dma_start(rows[:, :, :], io["rows"].rearrange("(a n) d -> a n d", a=1).broadcast_to([P, NROWS, D]))\
                .then_inc(k_loaded["small"], 16)
            act.dma_start(cols[:, :], io["cols"]).then_inc(k_loaded["small"], 16)
            act.dma_start(region_e[:, 0:NCONST], io["consts"]).then_inc(k_loaded["const"], 16)
            act.wait_ge(k_loaded["small"], 32)
            act.activation(qcol[:, :], cols[:, COL["bq0"]:COL["bq0"] + 8], ACT.Copy, scale=DK0 ** -0.5).then_inc(setup_act, 1)
            act.wait_ge(setup_dve, 3)
            for i, name in enumerate(("bk2", "sbk", "cbk")):
                for e in range(2):
                    act.activation(kcol[:, i, e, :], cols[:, COL[name]:COL[name] + DT], ACT.Copy,
                                   scale=km4[:, e:e + 1]).then_inc(setup_act, 1)
            act.wait_ge(setup_act, 7)
            act.wait_ge(setup_dve, 5)
            act.wait_ge(setup_pool, 4)

            with act.Fori(0, B) as b:
                links = [0]

                def link(ins):
                    links[0] += 1
                    ins.then_inc(act_link, 1)
                    act.wait_ge(act_link, b * ACT_LINKS + links[0])

                def drain_qk(p):
                    act.wait_ge(*filled_by(("QK0", p), b))
                    src = slot(("QK0", p))
                    act.activation(qk0[:, p % 2, 0, :], src[:, 0, :], ACT.Identity, bias=qcol[:, p:p + 1], scale=DK0 ** -0.5)
                    act.activation(qk0[:, p % 2, 1, :], src[:, 1, :], ACT.Identity, bias=col("bk0", p)).then_inc(*ends_drain(("QK0", p)))

                drain_qk(0)
                for p in range(PAIRS):
                    for kt in range(NT):
                        n = NT * p + kt
                        act.wait_ge(*drained_by(("S0", p, kt), b))
                        if n >= 8:
                            act.wait_ge(pv_done, b * PV_ITER + n - 7)
                        for h in range(2):
                            ins = act.activation(e0[:, n % 8, h, :], sm0[:, n % 2, h, :], ACT.Exp, bias=nmin0[:, n, h:h + 1],
                                                 scale=-1.0, accum_out=sum0[:, n, h:h + 1])
                        ins.then_inc(exp0_done, 1)
                    if p + 1 < PAIRS:
                        drain_qk(p + 1)

                act.wait_ge(*filled_by(("vpT",), b))
                act.activation(wide[:, :, :], slot(("vpT",))[:, 0, 0:D].rearrange("p (t n) -> p t n", t=DT), ACT.Copy)\
                    .then_inc(*ends_drain(("vpT",)))

                def drain_k(name, a, i, func):
                    act.wait_ge(*filled_by(name, b))
                    for e in range(2):
                        for t in range(DT):
                            ins = act.activation(k_of[a][:, e, t, :], slot(name)[:, t, :], func, bias=kcol[:, i, e, t:t + 1],
                                                 scale=km4[:, e:e + 1])
                    ins.then_inc(*ends_drain(name))

                def drain_x(n, gamma=None, beta=None):
                    act.wait_ge(*filled_by(("X", n), b))
                    src = slot(("X", n))
                    if gamma is None:
                        act.activation(act_t[:, :, :], src, ACT.Copy).then_inc(*ends_drain(("X", n)))
                        return
                    for t in range(DT):
                        ins = act.activation(act_t[:, t, :], src[:, t, :], ACT.Identity, bias=col(beta, t), scale=col(gamma, t))
                    ins.then_inc(*ends_drain(("X", n)))

                def rsqrt(n, sign, scale=1.0, eps=True):
                    act.wait_ge(var_ready, b * 5 + n + 1)
                    if eps:
                        link(act.activation(lnv[:, :], mv[:, :, 1], ACT.Ln, bias=epsc[:, 0:1]))
                    else:
                        link(act.activation(lnv[:, :], std1[:, :], ACT.Ln, scale=scale))
                    act.activation(std[:, :], lnv[:, :], ACT.Exp, scale=0.5 * sign).then_inc(rstd_ready, 1)

                drain_x(0)
                drain_k(("K2",), CAUSAL, 0, ACT.Relu)
                act.wait_ge(*filled_by(("tp",), b))
                for t in range(DT):
                    ins = act.activation(tp_t[:, t, :], slot(("tp",))[:, t, :], ACT.Identity, bias=col("bt", t))
                ins.then_inc(*ends_drain(("tp",)))
                act.wait_ge(agree_max, b + 1)
                act.activation(rrow[0:1, :], slot(("agree",))[0:1, 0, :], ACT.Exp, bias=one_sum[0:1, 1:2], scale=2.0,
                               accum_out=one_sum[0:1, 2:3]).then_inc(*ends_drain(("agree",)))
                for j in range(2):
                    act.wait_ge(*drained_by(("gate", j), b))
                    part = nat_n[:, 2 * j:2 * j + 2, :]
                    act.activation(part, part, ACT.Sigmoid).then_inc(gate_ready, 1)
                drain_k(("KC",), FULL, 2, ACT.Identity)
                rsqrt(0, -1)
                drain_x(1, "ga1", "be1")

                def attention(a):
                    for g in range(GROUPS):
                        act.wait_ge(*filled_by((a, "T", g), b))
                        act.activation(mrow[:, g % 2, :], slot((a, "T", g))[:, 0, 0:256].bitcast(BF16), ACT.Copy)\
                            .then_inc(*ends_drain((a, "T", g)))
                        for kt in range(NT):
                            n = UNITS * a + NT * g + kt
                            q0, nq = width(a, kt)
                            for u in range(2):
                                act.wait_ge(*filled_by((a, "B", g, kt, u), b))
                                act.wait_ge(pv_done, b * PV_ITER + UNITS0 + max(0, n - 3))
                                act.activation(e16[:, n % 4, 2 * u:2 * u + 2, 0:nq], slot((a, "B", g, kt, u))[:, :, 0:nq], ACT.Exp)\
                                    .then_inc(*ends_drain((a, "B", g, kt, u)))

                attention(CAUSAL)
                rsqrt(1, +1, scale=D / (D - 1), eps=False)
                drain_x(2)
                drain_k(("KS",), BANDED, 1, ACT.Identity)
                attention(BANDED)
                rsqrt(2, -1)
                drain_x(3, "g1", "b1n")
                attention(FULL)
                rsqrt(3, -1)
                drain_x(4, "g2", "b2n")
                for j in range(FT // 2):
                    act.wait_ge(*filled_by(("F1", j), b))
                    for i in range(2):
                        ins = act.activation(hid[:, 2 * j + i, :], slot(("F1", j))[:, i, :], ACT.Gelu, bias=col("b1", 2 * j + i))
                    ins.then_inc(*ends_drain(("F1", j)))
                rsqrt(4, -1)
                assert links[0] == ACT_LINKS, links

        @block.vector
        def _(dve):
            dve.wait_ge(k_loaded["const"], 16)
            c = region_e
            dve.tensor_copy(cbf[:, :], c[:, 0:NBF]).then_inc(setup_dve, 1)
            dve.tensor_copy(ident[:, :], c[:, CST["ident"]:CST["ident"] + P]).then_inc(setup_dve, 1)
            dve.tensor_scalar(km4[:, :], c[:, CST["even"]:CST["even"] + 2], 0.25, None, ALU.mult).then_inc(setup_dve, 1)
            dve.tensor_copy(tri[:, :], c[:, CST["tri"]:CST["tri"] + P]).then_inc(setup_dve, 1)
            for g in range(GROUPS):
                ins = dve.tensor_copy(mcol_s[:, g, :, :],
                                      c[:, CST["slopeM"] + g * P:CST["slopeM"] + (g + 1) * P].unsqueeze(1).broadcast_to([P, NT, P]))
            ins.then_inc(setup_dve, 1)
            dve.wait_ge(setup_dve, 5)
            dve.wait_ge(setup_pool, 4)
            dve.wait_ge(setup_act, 7)

            with dve.Fori(0, B) as b:
                links = [0]

                def link(ins):
                    links[0] += 1
                    ins.then_inc(dve_link, 1)
                    dve.wait_ge(dve_link, b * DVE_LINKS + links[0])

                holds = [0]

                def hold():
                    dve.memset(held[0:1, holds[0]:holds[0] + 1], 0.0)
                    holds[0] += 1

                dve.wait_ge(k_loaded["mask"], b * 16 + 16)
                link(dve.tensor_scalar(maskb[:, :], mask_i, 0.0, NEG, ALU.is_equal, ALU.mult))
                link(dve.tensor_reduce(nanfix[:, 0:1], maskb[:, :], AX.X, ALU.max))
                link(dve.tensor_scalar(nanfix[:, 1:2], nanfix[:, 0:1], 0.0, None, ALU.is_equal))
                link(dve.reciprocal(nanfix[:, 2:3], nanfix[:, 1:2]))
                link(dve.tensor_scalar(nanfix[:, 3:4], nanfix[:, 2:3], 0.0, None, ALU.mult))

                for t in range(NT):
                    dve.wait_ge(*filled_by(("V0", t), b))
                    dve.tensor_tensor(v0[:, t, :], slot(("V0", t)).rearrange("p a n -> p (a n)"),
                                      row("bv0", 4).rearrange("p a n -> p (a n)"), ALU.add).then_inc(*ends_drain(("V0", t)))
                dve.wait_ge(*drained_by(("V0", NT - 1), b))
                dve.wait_ge(k_loaded["ctx"], b * 16 + 16)
                link(dve.tensor_reduce(small[:, 0:2], ctx_t[:, :, :], AX.X, ALU.add))
                dve.tensor_scalar(pooled[:, :], small[:, 0:2], 1.0 / S, None, ALU.mult).then_inc(pooled_ready, 1)
                dve.wait_ge(pooled_ready, b + 1)
                dve.tensor_copy(wide[:, :, :], pooled[:, :].unsqueeze(2).broadcast_to([P, DT, P])).then_inc(wide_ready, 1)

                def scale_v(n):
                    p, kt = n // NT, n % NT
                    dve.wait_ge(exp0_done, b * UNITS0 + n + 1)
                    link(dve.reciprocal(rs0[:, n, :], sum0[:, n, :]))
                    if n >= 4:
                        dve.wait_ge(pv_done, b * PV_ITER + n - 3)
                    dve.tensor_tensor(vs0[:, n % 4, :, :], v0[:, kt, 2 * DK0 * p:2 * DK0 * (p + 1)].rearrange("p (h c) -> p h c", h=2),
                                      rs0[:, n, :].unsqueeze(2).broadcast_to([P, 2, DK0]), ALU.mult).then_inc(vs_ready, 1)

                def drain_heads0(p):
                    dve.wait_ge(pv_done, b * PV_ITER + NT * (p + 1))
                    dve.tensor_copy(o0[:, p, :], obank[:, p % 2, :]).then_inc(out_drained, 1)

                for n in range(UNITS0):
                    p, kt = n // NT, n % NT
                    dve.wait_ge(*filled_by(("S0", p, kt), b))
                    if n >= 2:
                        dve.wait_ge(exp0_done, b * UNITS0 + n - 1)
                    hold()
                    for h in range(2):
                        ins = dve.tensor_tensor_reduce(out=sm0[:, n % 2, h, :], in0=slot(("S0", p, kt))[:, h, :], in1=maskb[:, :],
                                                       scale=-1.0, scalar=3.0e38, op0=ALU.add, op1=ALU.min,
                                                       accum_out=nmin0[:, n, h:h + 1])
                    ins.then_inc(*ends_drain(("S0", p, kt)))
                    if n >= 1:
                        scale_v(n - 1)
                    if kt == 2 and p >= 2:
                        drain_heads0(p - 2)
                scale_v(UNITS0 - 1)
                drain_heads0(PAIRS - 2)
                drain_heads0(PAIRS - 1)

                dve.wait_ge(resid0_ready, b + 1)
                for j in range(2):
                    dve.wait_ge(*filled_by(("O0", j), b))
                    dve.scalar_tensor_tensor(out=nat_x[:, 2 * j:2 * j + 2, :], in0=slot(("O0", j))[:, :, 0:D], scalar=nanfix[:, 3:4],
                                             in1=x_nat[:, 2 * j:2 * j + 2, :], op0=ALU.add, op1=ALU.add)\
                        .then_inc(*ends_drain(("O0", j)))

                dve.wait_ge(*filled_by(("vp",), b))
                dve.tensor_tensor(vp_b[:, :], slot(("vp",))[:, 0, 0:D], row("bv1").squeeze(1), ALU.add).then_inc(*ends_drain(("vp",)))

                def drain_v(name, bias, dst):
                    for j in range(2):
                        dve.wait_ge(*filled_by((name, j), b))
                        for i in range(2):
                            ins = dve.tensor_tensor(dst(2 * j + i), slot((name, j))[:, i, 0:D].rearrange("p (h c) -> p h c", h=H),
                                                    row(bias).squeeze(1).rearrange("p (h c) -> p h c", h=H), ALU.add)
                        ins.then_inc(*ends_drain((name, j)))

                drain_v("V2", "bv2", lambda t: v2[:, t, :].rearrange("p (h c) -> p h c", h=H))
                dve.wait_ge(*filled_by(("uv",), b))
                dve.tensor_copy(u_b[:, :], slot(("uv",))[:, 0, 0:D]).then_inc(*ends_drain(("uv",)))
                dve.wait_ge(*filled_by(("ksum",), b))
                dve.tensor_scalar(km[:, :], slot(("ksum",))[:, 0, 0:NT], 0.0, None, ALU.is_gt).then_inc(*ends_drain(("ksum",)))
                dve.wait_ge(*filled_by(("agree",), b))
                link(dve.tensor_reduce(one_sum[0:1, 0:1], slot(("agree",))[0:1, 0, :], AX.X, ALU.max))
                dve.tensor_scalar(one_sum[0:1, 1:2], one_sum[0:1, 0:1], -2.0, None, ALU.mult).then_inc(agree_max, 1)
                link(dve.tensor_scalar(v2[:, :, :], v2[:, :, :], 0.0, None, ALU.max))
                dve.wait_ge(*drained_by(("ksum",), b))
                for t in range(NT):
                    dve.tensor_scalar(v_of[CAUSAL][:, t, :, 0:DH], v2[:, t, :].rearrange("p (h c) -> p h c", h=H),
                                      km[:, t:t + 1], None, ALU.mult)
                    ins = dve.tensor_scalar(v_of[CAUSAL][:, t, :, DH:2 * DH], ones[:, 0:DH].unsqueeze(1).broadcast_to([P, H, DH]),
                                            km[:, t:t + 1], None, ALU.mult)
                ins.then_inc(vmask_ready, 1)
                dve.wait_ge(*drained_by(("agree",), b))
                dve.reciprocal(one_sum[0:1, 3:4], one_sum[0:1, 2:3]).then_inc(agree_inv, 1)
                dve.wait_ge(*filled_by(("cnt",), b))
                dve.tensor_scalar(degen[:, :], slot(("cnt",))[:, 0, 0:NT], 0.5, None, ALU.is_lt).then_inc(*ends_drain(("cnt",)))
                dve.wait_ge(*filled_by(("rcol",), b))
                dve.tensor_copy(rcol[:, :], slot(("rcol",))[:, 0, 0:NT]).then_inc(*ends_drain(("rcol",)))
                dve.wait_ge(*filled_by(("meanV",), b))
                dve.tensor_scalar(wide[:, :, :], slot(("meanV",))[:, 0, 0:DT].unsqueeze(2).broadcast_to([P, DT, P]), 1.0 / S, None, ALU.mult)\
                    .then_inc(*ends_drain(("meanV",)))
                dve.wait_ge(*drained_by(("rcol",), b))
                for j in range(2):
                    dve.wait_ge(*filled_by(("gate", j), b))
                    for i in range(2):
                        t = 2 * j + i
                        ins = dve.scalar_tensor_tensor(out=nat_n[:, t, :], in0=u_b[:, :], scalar=rcol[:, t:t + 1],
                                                       in1=slot(("gate", j))[:, i, 0:D], op0=ALU.mult, op1=ALU.add)
                    ins.then_inc(*ends_drain(("gate", j)))
                dve.wait_ge(gate_ready, b * 2 + 2)
                for t in range(NT):
                    ins = dve.scalar_tensor_tensor(out=nat_y[:, t, :], in0=vp_b[:, :], scalar=rcol[:, t:t + 1], in1=nat_n[:, t, :],
                                                   op0=ALU.mult, op1=ALU.mult)
                link(ins)
                link(dve.tensor_tensor(nat_y[:, :, :], nat_y[:, :, :], nat_x[:, :, :], ALU.add))

                def norm(n):
                    for t in range(NT):
                        ins = dve.bn_stats(stats[:, t, :], nat_y[:, t, :])
                    link(ins)
                    hold()
                    for t in range(NT):
                        ins = dve.bn_aggr(mv[:, t, :], stats[:, t, :])
                    if n == 1:
                        link(ins)
                        ins = dve.tensor_scalar(std1[:, :], mv[:, :, 1], 1e-18, None, ALU.max)
                    ins.then_inc(var_ready, 1)
                    dve.wait_ge(rstd_ready, b * 5 + n + 1)
                    scale = std
                    if n == 1:
                        link(dve.tensor_scalar(std1[:, :], std[:, :], 1e-8, None, ALU.add))
                        link(dve.reciprocal(rstd[:, :], std1[:, :]))
                        scale = rstd
                    for t in range(NT):
                        ins = dve.tensor_scalar(nat_n[:, t, :], nat_y[:, t, :], mv[:, t, 0:1], scale[:, t:t + 1],
                                                ALU.subtract, ALU.mult)
                    ins.then_inc(norm_ready, 1)

                norm(0)
                dve.wait_ge(*filled_by(("meanO",), b))
                dve.tensor_tensor(mean_o[:, :], slot(("meanO",))[:, 0, 0:D], row("bo2").squeeze(1), ALU.add)\
                    .then_inc(*ends_drain(("meanO",)))
                drain_v("VC", "cbv", lambda t: v_of[FULL][:, t, :, 0:DH])

                def drain_q(name, bias, relu=False):
                    dve.wait_ge(*filled_by(name, b))
                    for t in range(DT):
                        ins = dve.tensor_scalar(q_t[:, t, :], slot(name)[:, t, :], col(bias, t), 0.0 if relu else None,
                                                ALU.add, ALU.max if relu else ALU.bypass)
                    ins.then_inc(*ends_drain(name))

                def maxima(a, g, qt, u):
                    _, nk = seen(a, qt)
                    name = (a, "A", g, qt, u)
                    dve.wait_ge(*filled_by(name, b))
                    dve.tensor_reduce(nmax[:, qt, 2 * u:2 * u + 2], slot(name)[:, :, 0:nk], AX.X, ALU.max, negate=True)\
                        .then_inc(*ends_drain(name))

                def maxima_cols(a, g):
                    m = (mcol_s[:, g, :, :] if a == BANDED else mcol[:, g % 2, :, :]).rearrange("p t (s c) -> p t s c", s=4)
                    dve.wait_ge(*drained_by((a, "A", g, NT - 1, 1), b))
                    link(dve.tensor_copy(m[:, :, :, 0], nmax[:, :, :]))
                    dve.tensor_tensor(m[:, :, :, 1], nmax[:, :, :], m[:, :, :, 0], ALU.subtract).then_inc(mcol_ready, 1)
                    dve.wait_ge(mcol_ready, b * 12 + a * GROUPS + g + 1)

                def head_out(a, g):
                    n = a * GROUPS + g
                    dve.wait_ge(out_drained, b * OUT_ITER + PAIRS + n)
                    dve.wait_ge(pv_done, b * PV_ITER + UNITS0 + NT * (n + 1))
                    hold()
                    o = obank[:, (PAIRS + n) % 2, :]
                    link(dve.stream_shuffle(rbuf[:, :], o, [DH + i % DH for i in range(32)]))
                    if a == CAUSAL:
                        link(dve.tensor_scalar(rbuf[:, :], rbuf[:, :], 1e-30, None, ALU.max))
                    link(dve.reciprocal(rbuf[:, :], rbuf[:, :]))
                    dve.tensor_tensor(oT[:, g, :], o, rbuf[:, :], ALU.mult).then_inc(out_drained, 1)

                def attention(a):
                    for qt in range(NT):
                        for u in range(2):
                            maxima(a, 0, qt, u)
                    maxima_cols(a, 0)
                    for g in range(GROUPS):
                        if g + 1 < GROUPS:
                            for qt in range(NT):
                                for u in range(2):
                                    maxima(a, g + 1, qt, u)
                            maxima_cols(a, g + 1)
                        if g >= 1:
                            head_out(a, g - 1)
                    head_out(a, GROUPS - 1)

                drain_q(("Q2",), "bq2", relu=True)
                attention(CAUSAL)
                dve.wait_ge(resid_ready, b * 4 + 1)
                for j in range(2):
                    dve.wait_ge(*filled_by(("O2", j), b))
                    for i in range(2):
                        t = 2 * j + i
                        ins = dve.scalar_tensor_tensor(out=nat_y[:, t, :], in0=mean_o[:, :], scalar=degen[:, t:t + 1],
                                                       in1=slot(("O2", j))[:, i, 0:D], op0=ALU.mult, op1=ALU.add)
                    ins.then_inc(*ends_drain(("O2", j)))
                    dve.wait_ge(*drained_by(("O2", j), b))
                    part = slice(2 * j, 2 * j + 2)
                    link(dve.scalar_tensor_tensor(out=nat_y[:, part, :], in0=nat_y[:, part, :], scalar=0.0, in1=nat_x[:, part, :],
                                                  op0=ALU.max, op1=ALU.add))
                norm(1)

                def drain_out(name, resid):
                    for j in range(2):
                        part = slice(2 * j, 2 * j + 2)
                        dve.wait_ge(*filled_by((name, j), b))
                        dve.tensor_tensor(nat_y[:, part, :], slot((name, j))[:, :, 0:D], resid[:, part, :], ALU.add)\
                            .then_inc(*ends_drain((name, j)))
                    for j in range(2):
                        dve.wait_ge(*drained_by((name, j), b))

                drain_q(("QS",), "sbq")
                drain_v("VS", "sbv", lambda t: v_of[BANDED][:, t, :, 0:DH])
                attention(BANDED)
                drain_out("OS", nat_n)
                norm(2)
                drain_q(("QC",), "cbq")
                attention(FULL)
                dve.wait_ge(resid_ready, b * 4 + 2)
                drain_out("OC", nat_x)
                norm(3)
                dve.wait_ge(resid_ready, b * 4 + 3)
                drain_out("F2", nat_x)
                norm(4)
                dve.wait_ge(norm_ready, b * 5 + 5)
                assert links[0] == DVE_LINKS, links

        @block.tensor
        def _(pe):
            pe.wait_ge(setup_dve, 5)
            pe.wait_ge(setup_act, 7)
            pe.wait_ge(setup_pool, 4)
            with pe.Fori(0, B) as b:
                order = [0]

                def start(name):
                    assert JOBS[order[0]] == name, (JOBS[order[0]], name)
                    order[0] += 1
                    pe.wait_ge(*free_for(name, b))
                    return slot(name)

                def project(name, w, src, tiles):
                    dst = start(name)
                    for i, m in enumerate(tiles):
                        for t in range(DT):
                            ins = pe.matmul(dst[:, i, :], w[:, t, m * P:(m + 1) * P], src[:, t, :], start=(t == 0), stop=(t == DT - 1))
                    ins.then_inc(*ends_fill(name))

                def project_nat(name, w, src):
                    for j in range(2):
                        dst = start((name, j))
                        for i in range(2):
                            m = 2 * j + i
                            for t in range(DT):
                                ins = pe.matmul(dst[:, i, 0:D], src[:, t, m * P:(m + 1) * P], w[:, t, :], start=(t == 0), stop=(t == DT - 1))
                        ins.then_inc(*ends_fill((name, j)))

                def out_project(name, w, src, n):
                    for j in range(2):
                        dst = start((name, j))
                        for i in range(2):
                            m = 2 * j + i
                            for t in range(n):
                                ins = pe.matmul(dst[:, i, 0:D], src[:, t, m * P:(m + 1) * P], w[:, t, :], start=(t == 0), stop=(t == n - 1))
                        ins.then_inc(*ends_fill((name, j)))

                pe.wait_ge(k_loaded["ctx"], b * 16 + 16)
                pe.wait_ge(k_loaded["wv0"], b * 16 + 16)
                for kt in range(NT):
                    dst = start(("V0", kt))
                    for i in range(2):
                        for t in range(DT):
                            ins = pe.matmul(dst[:, i, :], ctx_t[:, t, kt * P:(kt + 1) * P], wv0[:, t, i * 512:(i + 1) * 512],
                                            start=(t == 0), stop=(t == DT - 1))
                    ins.then_inc(*ends_fill(("V0", kt)))

                def qk(p):
                    dst = start(("QK0", p))
                    for i, (w, src) in enumerate(((wq0, act_t), (wk0, ctx_t))):
                        for t in range(DT):
                            ins = pe.matmul(dst[:, i, :], w[:, t, p * P:(p + 1) * P], src[:, t, :], start=(t == 0), stop=(t == DT - 1))
                    ins.then_inc(*ends_fill(("QK0", p)))

                def scores0(p, kt):
                    name = ("S0", p, kt)
                    dst = start(name)
                    if kt == 0:
                        pe.wait_ge(*drained_by(("QK0", p), b))
                    for h in range(2):
                        strip = slice(DK0 * h, DK0 * (h + 1))
                        ins = pe.matmul(dst[:, h, :], qk0[strip, p % 2, 1, kt * P:(kt + 1) * P], qk0[strip, p % 2, 0, :], start=True, stop=True)
                    ins.then_inc(*ends_fill(name))

                def values0(p, kt):
                    n = NT * p + kt
                    if kt == 0 and p >= 2:
                        pe.wait_ge(out_drained, b * OUT_ITER + p - 1)
                    pe.wait_ge(exp0_done, b * UNITS0 + n + 1)
                    pe.wait_ge(vs_ready, b * UNITS0 + n + 1)
                    for h in range(2):
                        ins = pe.matmul(obank[DK0 * h:DK0 * (h + 1), p % 2, :], vs0[:, n % 4, h, :], e0[:, n % 8, h, :],
                                        start=(kt == 0), stop=(kt == NT - 1))
                    ins.then_inc(pv_done, 1)

                pe.wait_ge(k_loaded["act"], b * 16 + 16)
                pe.wait_ge(k_loaded["wq0"], 16)
                pe.wait_ge(k_loaded["wk0"], 16)
                qk(0)
                for p in range(PAIRS):
                    for kt in range(NT):
                        scores0(p, kt)
                        if p >= 1:
                            values0(p - 1, kt)
                    if p + 1 < PAIRS:
                        qk(p + 1)
                for kt in range(NT):
                    values0(PAIRS - 1, kt)
                pe.wait_ge(out_drained, b * OUT_ITER + PAIRS)
                pe.wait_ge(k_loaded["wo0"], b * 16 + 16)
                out_project("O0", wo0, o0, PAIRS)

                pe.wait_ge(k_loaded["l1"], 64)
                pe.wait_ge(wide_ready, b + 1)
                dst = start(("vp",))
                for t in range(DT):
                    ins = pe.matmul(dst[:, 0, 0:D], wide[:, t, :], w_l1["v"][:, t, :], start=(t == 0), stop=(t == DT - 1))
                ins.then_inc(*ends_fill(("vp",)))
                dst = start(("vpT",))
                pe.wait_ge(*drained_by(("vp",), b))
                for t in range(DT):
                    ins = pe.transpose(dst[:, 0, t * P:(t + 1) * P], vp_b[:, t * P:(t + 1) * P], ident[:, :])
                ins.then_inc(*ends_fill(("vpT",)))
                def turn(n, src):
                    dst = start(("X", n))
                    for t in range(DT):
                        for m in range(NT):
                            ins = pe.transpose(dst[:, t, m * P:(m + 1) * P], src[:, m, t * P:(t + 1) * P], ident[:, :])
                    ins.then_inc(*ends_fill(("X", n)))

                for j in range(2):
                    pe.wait_ge(*drained_by(("O0", j), b))
                turn(0, nat_x)
                pe.wait_ge(k_loaded["l2"], 80)
                project(("K2",), w_sq["k2"], ctx_t, range(DT))
                project_nat("V2", w_sq["v2"], ctx_t)
                dst = start(("uv",))
                pe.wait_ge(*drained_by(("vpT",), b))
                for t in range(DT):
                    ins = pe.matmul(dst[:, 0, 0:D], wide[:, t, :], w_l1["gv"][:, t, :], start=(t == 0), stop=(t == DT - 1))
                ins.then_inc(*ends_fill(("uv",)))
                pe.wait_ge(*drained_by(("X", 0), b))
                project(("tp",), w_l1["t"], act_t, range(DT))
                dst = start(("ksum",))
                pe.wait_ge(*drained_by(("K2",), b))
                for kt in range(NT):
                    for i in range(2 * DT):
                        ins = pe.matmul(dst[:, 0, kt:kt + 1], k_of[CAUSAL][:, i // DT, i % DT, kt * P:(kt + 1) * P], ones[:, 0:1],
                                        start=(i == 0), stop=(i == 2 * DT - 1))
                ins.then_inc(*ends_fill(("ksum",)))
                dst = start(("agree",))
                pe.wait_ge(*drained_by(("tp",), b))
                for t in range(DT):
                    ins = pe.matmul(dst[0:1, 0, :], wide[:, t, 0:1], tp_t[:, t, :], start=(t == 0), stop=(t == DT - 1))
                ins.then_inc(*ends_fill(("agree",)))
                dst = start(("cnt",))
                pe.wait_ge(*drained_by(("ksum",), b))
                for qt in range(NT):
                    for kt in range(qt + 1):
                        ins = pe.matmul(dst[:, 0, qt:qt + 1], (tri if kt == qt else ones)[:, :], km[:, kt:kt + 1],
                                        start=(kt == 0), stop=(kt == qt))
                ins.then_inc(*ends_fill(("cnt",)))
                dst = start(("rcol",))
                pe.wait_ge(*drained_by(("agree",), b))
                pe.wait_ge(agree_inv, b + 1)
                for t in range(NT):
                    ins = pe.matmul(dst[:, 0, t:t + 1], rrow[0:1, t * P:(t + 1) * P], one_sum[0:1, 3:4], start=True, stop=True)
                ins.then_inc(*ends_fill(("rcol",)))
                dst = start(("meanV",))
                pe.wait_ge(vmask_ready, b + 1)
                for i in range(DT):
                    for kt in range(NT):
                        ins = pe.matmul(dst[:, 0, i:i + 1], v2[:, kt, i * P:(i + 1) * P], ones[:, 0:1], start=(kt == 0), stop=(kt == NT - 1))
                ins.then_inc(*ends_fill(("meanV",)))
                for j in range(2):
                    dst = start(("gate", j))
                    for i in range(2):
                        m = 2 * j + i
                        for t in range(DT):
                            pe.matmul(dst[:, i, 0:D], tp_t[:, t, m * P:(m + 1) * P], w_l1["gt"][:, t, :], start=(t == 0), stop=False)
                        ins = pe.matmul(dst[:, i, 0:D], ones[0:1, :], rows[0:1, ROW["bg"], :], start=False, stop=True)
                    ins.then_inc(*ends_fill(("gate", j)))
                dst = start(("meanO",))
                pe.wait_ge(*drained_by(("meanV",), b))
                for t in range(DT):
                    ins = pe.matmul(dst[:, 0, 0:D], wide[:, t, :], w_om[:, t, :], start=(t == 0), stop=(t == DT - 1))
                ins.then_inc(*ends_fill(("meanO",)))
                pe.wait_ge(k_loaded["lc"], 64)
                project(("KC",), w_sq["ck"], ctx_t, range(DT))
                project_nat("VC", w_sq["cv"], ctx_t)
                pe.wait_ge(norm_ready, b * 5 + 1)
                turn(1, nat_n)
                pe.wait_ge(*drained_by(("X", 1), b))
                project(("Q2",), w_sq["q2"], act_t, range(DT))

                def pass_a(a, g, qt, u):
                    name = (a, "A", g, qt, u)
                    dst = start(name)
                    k0, nk = seen(a, qt)
                    for i in range(2):
                        s = 2 * u + i
                        strip = slice(32 * s, 32 * s + 32)
                        ins = pe.matmul(dst[:, i, 0:nk], q_t[strip, g // 2, qt * P:(qt + 1) * P], k_of[a][strip, g % 2, g // 2, k0:k0 + nk],
                                        start=True, stop=(a == FULL))
                    if a == BANDED:
                        for i in range(2):
                            part = slice(32 * (2 * u + i), 32 * (2 * u + i) + 3)
                            pe.matmul(dst[:, i, 0:nk], cb("slopeA", P, part, g * P), cb("rowsJ", nk, part, BAND - nk), start=False, stop=False)
                    if a != FULL:
                        mask, n = ("bandA", nk) if a == BANDED else ("maskA", P)
                        full_n = BAND if a == BANDED else P
                        for i in range(2):
                            ins = pe.matmul(dst[:, i, nk - n:nk], cb("ident", P), cb(mask, n, at=full_n - n), start=False, stop=True)
                    ins.then_inc(*ends_fill(name))

                def pass_b(a, g, kt, u):
                    name = (a, "B", g, kt, u)
                    dst = start(name)
                    q0, nq = width(a, kt)
                    for i in range(2):
                        s = 2 * u + i
                        strip = slice(32 * s, 32 * s + 32)
                        pe.matmul(dst[:, i, 0:nq], k_of[a][strip, g % 2, g // 2, kt * P:(kt + 1) * P], q_t[strip, g // 2, q0:q0 + nq],
                                  start=True, stop=False)
                    for i in range(2):
                        r0 = 32 * (2 * u + i)
                        if a == BANDED:
                            part = slice(r0, r0 + 5)
                            ins = pe.matmul(dst[:, i, 0:P], cb("rowsB0", P, part), mrow[part, g % 2, q0:q0 + P], start=False, stop=False)
                            if nq > P:
                                ins = pe.matmul(dst[:, i, P:nq], cb("rowsB1", P, part), mrow[part, g % 2, q0 + P:q0 + nq], start=False, stop=False)
                        else:
                            part = slice(r0, r0 + 2)
                            ins = pe.matmul(dst[:, i, 0:nq], cb("rowsB0", P, part), mrow[part, g % 2, q0:q0 + nq], start=False, stop=(a == FULL))
                    if a != FULL:
                        mask, n = ("bandB", nq) if a == BANDED else ("maskB", P)
                        for i in range(2):
                            ins = pe.matmul(dst[:, i, 0:n], cb("ident", P), cb(mask, n), start=False, stop=True)
                    ins.then_inc(*ends_fill(name))

                def values(a, g, kt):
                    n = UNITS * a + NT * g + kt
                    o = a * GROUPS + g
                    q0, nq = width(a, kt)
                    if kt == 0:
                        pe.wait_ge(out_drained, b * OUT_ITER + PAIRS + max(0, o - 1))
                    for u in range(2):
                        pe.wait_ge(*drained_by((a, "B", g, kt, u), b))
                    for s, h in enumerate(heads_of(g)):
                        ins = pe.matmul(obank[32 * s:32 * s + 32, (PAIRS + o) % 2, q0:q0 + nq], v_of[a][:, kt, h, :], e16[:, n % 4, s, 0:nq],
                                        start=(kt == 0), stop=(kt == NT - 1), skip_group_check=(a != FULL))
                    ins.then_inc(pv_done, 1)

                def attention(a):
                    for qt in range(NT):
                        for u in range(2):
                            pass_a(a, 0, qt, u)
                    for g in range(GROUPS):
                        name = (a, "T", g)
                        dst = start(name)
                        pe.wait_ge(mcol_ready, b * 12 + a * GROUPS + g + 1)
                        m = mcol_s[:, g, :, :] if a == BANDED else mcol[:, g % 2, :, :]
                        turned = dst[:, 0, 0:256].bitcast(BF16)
                        for t in range(NT):
                            ins = pe.transpose(turned[:, t * P:(t + 1) * P], m[:, t, :], cb("ident", P))
                        ins.then_inc(*ends_fill(name))
                        for kt in range(NT):
                            if g >= 1:
                                values(a, g - 1, kt)
                            for u in range(2):
                                if kt == 0 and u == 0:
                                    pe.wait_ge(*drained_by(name, b))
                                pass_b(a, g, kt, u)
                                if g + 1 < GROUPS:
                                    pass_a(a, g + 1, kt, u)
                    for kt in range(NT):
                        values(a, GROUPS - 1, kt)
                    pe.wait_ge(out_drained, b * OUT_ITER + PAIRS + (a + 1) * GROUPS)

                pe.wait_ge(*drained_by(("Q2",), b))
                attention(CAUSAL)
                out_project("O2", w_out[CAUSAL], oT, GROUPS)

                pe.wait_ge(k_loaded["ls"], 64)
                pe.wait_ge(norm_ready, b * 5 + 2)
                turn(2, nat_n)
                pe.wait_ge(*drained_by(("X", 2), b))
                project(("QS",), w_sq["sq"], act_t, range(DT))
                project(("KS",), w_sq["sk"], act_t, range(DT))
                project_nat("VS", w_sq["sv"], act_t)
                pe.wait_ge(*drained_by(("QS",), b))
                pe.wait_ge(*drained_by(("KS",), b))
                pe.wait_ge(*drained_by(("VS", 1), b))
                pe.wait_ge(ones_ready, b * 2 + 2)
                attention(BANDED)
                out_project("OS", w_out[BANDED], oT, GROUPS)
                pe.wait_ge(norm_ready, b * 5 + 3)
                turn(3, nat_n)
                pe.wait_ge(*drained_by(("X", 3), b))
                project(("QC",), w_sq["cq"], act_t, range(DT))
                pe.wait_ge(*drained_by(("QC",), b))
                attention(FULL)
                out_project("OC", w_out[FULL], oT, GROUPS)
                pe.wait_ge(norm_ready, b * 5 + 4)
                turn(4, nat_n)
                pe.wait_ge(*drained_by(("X", 4), b))
                pe.wait_ge(k_loaded["ff"], b * 32 + 32)
                for j in range(FT // 2):
                    project(("F1", j), w_f1, act_t, (2 * j, 2 * j + 1))
                for j in range(FT // 2):
                    pe.wait_ge(*drained_by(("F1", j), b))
                out_project("F2", w_f2, hid, FT)
                while order[0] < len(JOBS):
                    name = JOBS[order[0]]
                    start(name)
                    pe.nop().then_inc(*ends_fill(name))
                    pe.nop().then_inc(*ends_drain(name))


def padded(w, bias, a):
    import numpy as np
    out = np.zeros((GROUPS, 4, 32, D), np.float32)
    for g in range(GROUPS):
        for s, h in enumerate(heads_of(g)):
            out[g, s, 0:DH] = w[h * DH:(h + 1) * DH]
    out[0, 0, DH] = bias
    return out.reshape(GROUPS * P, D)


def constants():
    import numpy as np
    c = np.zeros((P, NCONST), np.float32)

    def put(name, table, at=0):
        c[:, CST[name] + at:CST[name] + at + table.shape[1]] = table

    p = np.arange(P)[:, None]
    x = np.arange(P)[None, :]
    y = np.arange(BAND)[None, :]
    put("ident", (p == x).astype(np.float32))
    put("tri", (p <= x).astype(np.float32))
    put("maskA", np.where(x > p, NEG, 0.0))
    put("maskB", np.where(p > x, NEG, 0.0))
    ahead = y - W - p
    put("bandA", np.where((ahead <= 0) & (ahead > -W), 0.0, NEG))
    behind = y - p
    put("bandB", np.where((behind >= 0) & (behind < W), 0.0, NEG))
    slopes = (2.0 ** (-8.0 * np.arange(1, H + 1, dtype=np.float32) / H)).astype(np.float32)
    parts, rest = [], slopes.copy()
    for _ in range(3):
        hi = (rest.view(np.uint32) & np.uint32(0xFFFF0000)).view(np.float32)
        parts.append(hi)
        rest = (rest - hi).astype(np.float32)
    b0, b1 = np.zeros((4, 32, P)), np.zeros((4, 32, P))
    jrow = np.zeros((4, 32, BAND))
    b0[:, 0:2] = b1[:, 0:2] = 1.0
    b0[:, 2:5] = x
    b1[:, 2:5] = x - P
    jrow[:, 0:3] = y - W
    put("rowsB0", b0.reshape(P, P))
    put("rowsB1", b1.reshape(P, P))
    put("rowsJ", jrow.reshape(P, BAND))
    for g in range(GROUPS):
        sa = np.zeros((4, 32, P))
        sm = np.zeros((P, 4, 32))
        for s, h in enumerate(heads_of(g)):
            for i in range(3):
                sa[s, i] = parts[i][h]
                sm[:, s, 2 + i] = parts[i][h]
        put("slopeA", sa.reshape(P, P), g * P)
        put("slopeM", sm.reshape(P, P), g * P)
    put("even", np.concatenate([(p // DH % 2 == 0), (p // DH % 2 == 1)], axis=1).astype(np.float32))
    return c


def arrange(i):
    import numpy as np
    f = {k: np.asarray(v) for k, v in i.items()}
    c = np.ascontiguousarray
    a = {
        "xT": c(f["x"].transpose(0, 2, 1)), "ctxT": c(f["ctx_1024"].transpose(0, 2, 1)), "x": c(f["x"]),
        "mask": c(f["mask_BxS2_ik0"]),
        "wq0": c(f["L0_xattn_W_Q"].T), "wk0": c(f["L0_xattn_W_K"].T), "wv0": c(f["L0_xattn_W_V"].T), "wo0": c(f["L0_xattn_W_O"].T),
        "w1_t": c(f["L1_xattn_Wt"].T), "w1_v": c(f["L1_xattn_Wv"].T),
        "w1_gt": c(f["L1_xattn_Wg"][:, :D].T), "w1_gv": c(f["L1_xattn_Wg"][:, D:].T),
        "w_q2": c(f["L2_xattn_Wq"]), "w_k2": c(f["L2_xattn_Wk"]), "w_v2": c(f["L2_xattn_Wv"]), "w_om": c(f["L2_xattn_Wo"]),
        "w_f1": c(f["L3_xattn_w1"]), "w_f2": c(f["L3_xattn_w2"]),
        "w_out0": padded(f["L2_xattn_Wo"], f["L2_xattn_bo"], 0),
        "w_out1": padded(f["L3_xattn_swo"], f["L3_xattn_sbo"], 1),
        "w_out2": padded(f["L3_xattn_cwo"], f["L3_xattn_cbo"], 2),
        "consts": constants(),
    }
    for n in ("sq", "sk", "sv", "cq", "ck", "cv"):
        a["w_" + n] = c(f[f"L3_xattn_{n[0]}w{n[1]}"])
    col_of = {"bq0": "L0_xattn_b_Q", "bk0": "L0_xattn_b_K", "bt": "L1_xattn_bt", "bq2": "L2_xattn_bq", "bk2": "L2_xattn_bk",
              "sbq": "L3_xattn_sbq", "sbk": "L3_xattn_sbk", "cbq": "L3_xattn_cbq", "cbk": "L3_xattn_cbk", "b1": "L3_xattn_b1",
              "ga1": "L1_xattn_gamma", "be1": "L1_xattn_beta", "g1": "L3_xattn_g1", "b1n": "L3_xattn_be1",
              "g2": "L3_xattn_g2", "b2n": "L3_xattn_be2"}
    a["cols"] = c(np.concatenate([f[col_of[n]].reshape(k, P).T for n, k in COLS], axis=1))
    row_of = {"bv0": "L0_xattn_b_V", "bo0": "L0_xattn_b_O", "bv1": "L1_xattn_bv", "bg": "L1_xattn_bg", "ga1": "L1_xattn_gamma",
              "be1": "L1_xattn_beta", "bv2": "L2_xattn_bv", "bo2": "L2_xattn_bo", "sbv": "L3_xattn_sbv", "cbv": "L3_xattn_cbv",
              "b2": "L3_xattn_b2", "g1": "L3_xattn_g1", "b1n": "L3_xattn_be1", "g2": "L3_xattn_g2", "b2n": "L3_xattn_be2",
              "g3": "L3_xattn_g3", "b3n": "L3_xattn_be3"}
    a["rows"] = c(np.concatenate([f[row_of[n]].reshape(k, D) for n, k in ROWS], axis=0))
    return a


def kernel(**inputs):
    import numpy as _np
    import concourse.bacc as _bacc
    from concourse import mybir as _mybir
    from concourse.bass_utils import run_bass_kernel_spmd as _run

    nc = _bacc.Bacc("TRN2", target_bir_lowering=False, num_devices=1)
    arrays = arrange(inputs)
    io = {n: nc.dram_tensor("in_" + n, a.shape, _mybir.dt.from_np(a.dtype), kind="ExternalInput").ap() for n, a in arrays.items()}
    out = nc.dram_tensor("out", (B, S, D), F32, kind="ExternalOutput").ap()
    build(nc, io, out)
    r = _run(nc, [{"in_" + n: a for n, a in arrays.items()}], core_ids=[0])
    return r.results[0]["out"]
```

```python
from contextlib import ExitStack

import concourse.bass as bass
from concourse import mybir

ALU = mybir.AluOpType
ACT = mybir.ActivationFunctionType
F32 = mybir.dt.float32
F32R = mybir.dt.float32r
BF16 = mybir.dt.bfloat16
I32 = mybir.dt.int32
AX = mybir.AxisListType

B, S, D = 4, 512, 256
P = 128
NT = S // P
DT = D // P
H = 16
DK0 = 64
HD0 = H * DK0
PAIRS = H // 2
DH = D // H
GROUPS = H // 4
FF = 1024
FT = FF // P
W = 64
BAND = P + W
NEG = -1.0e30
CAUSAL, BANDED, FULL = range(3)
SLOTS = 3
EXP_LN_TABLES = 6
UNITS0 = PAIRS * NT
E0 = 7
UNITS = GROUPS * NT
PV_ITER = UNITS0 + 3 * UNITS
OUT_ITER = PAIRS + 3 * GROUPS

COLS = [("bq0", 8), ("bk0", 8), ("bt", 2), ("bq2", 2), ("bk2", 2), ("sbq", 2), ("sbk", 2), ("cbq", 2), ("cbk", 2),
        ("b1", 8), ("ga1", 2), ("be1", 2), ("g1", 2), ("b1n", 2), ("g2", 2), ("b2n", 2)]
ROWS = [("bv0", 4), ("bo0", 1), ("bv1", 1), ("bg", 1), ("ga1", 1), ("be1", 1), ("bv2", 1), ("bo2", 1), ("sbv", 1),
        ("cbv", 1), ("b2", 1), ("g1", 1), ("b1n", 1), ("g2", 1), ("b2n", 1), ("g3", 1), ("b3n", 1)]
CONSTS = [("ident", P), ("maskA", P), ("maskB", P), ("bandA", BAND), ("bandB", BAND),
          ("rowsB0", 4 * P), ("rowsB1", 4 * P), ("rowsJ", 4 * BAND), ("slopeA", 4 * P), ("tri", P),
          ("slopeM", 4 * P), ("hmask", 8), ("half", 2)]


def offsets(parts):
    at, out = 0, {}
    for name, n in parts:
        out[name] = at
        at += n
    return out, at


COL, NCOLS = offsets(COLS)
ROW, NROWS = offsets(ROWS)
CST, NCONST = offsets(CONSTS)
NBF = CST["tri"]


K_JOB = {CAUSAL: ("K2",), BANDED: ("KS",), FULL: ("KC",)}


def heads_of(g):
    return [4 * g + s for s in range(4)]


def attention_jobs(a):
    jobs = [(a, "A", 0, qt, u) for qt in range(NT) for u in range(2)]
    for g in range(GROUPS):
        jobs.append((a, "T", g))
        for t in range(NT):
            for u in range(2):
                jobs.append((a, "B", g, t, u))
                if g + 1 < GROUPS:
                    jobs.append((a, "A", g + 1, t, u))
    return jobs


def plan_jobs():
    jobs = [("V0", t) for t in range(NT)] + [("QK0", 0)]
    for p in range(PAIRS):
        jobs += [("S0", p, kt) for kt in range(NT)]
        if p + 1 < PAIRS:
            jobs.insert(-2, ("QK0", p + 1))
    jobs += [("O0", j) for j in range(2)]
    jobs += [("vp",), ("vpT",), ("X", 0), ("K2",)] + [("V2", j) for j in range(2)] + [("uv",), ("tp",), ("ksum",), ("KC",)]
    jobs += [("VC", j) for j in range(2)] + [("agree",), ("cnt",), ("rcol",), ("meanV",)] + [("gate", j) for j in range(2)]
    jobs += [("meanO",), ("X", 1), ("Q2",)]
    jobs += attention_jobs(CAUSAL) + [("O2", j) for j in range(2)] + [("X", 2), ("QS",), ("KS",)] + [("VS", j) for j in range(2)]
    jobs += attention_jobs(BANDED) + [("OS", j) for j in range(2)] + [("X", 3), ("QC",)]
    jobs += attention_jobs(FULL) + [("OC", j) for j in range(2)] + [("X", 4)]
    jobs += [("F1", j) for j in range(FT // 2)] + [("F2", j) for j in range(2)]
    while len(jobs) % SLOTS:
        jobs.append(("pad", len(jobs)))
    return jobs


JOBS = plan_jobs()
JOB = {name: n for n, name in enumerate(JOBS)}
ROUNDS = len(JOBS) // SLOTS

DVE_LINKS = 92
ACT_LINKS = 5
POOL_LINKS = 4
HOLDS = UNITS0 + 5 + 3 * GROUPS


def build(nc, io, out):
    with ExitStack() as ctx:
        def sb(name, shape, dt=F32):
            return ctx.enter_context(nc.sbuf_tensor(name, shape, dt))

        def sem(name):
            return ctx.enter_context(nc.semaphore(name))

        ring = ctx.enter_context(nc.psum_tensor("ring", [P, SLOTS, 2, 512], F32))
        obank = ctx.enter_context(nc.psum_tensor("obank", [P, 2, 512], F32))

        def overlay(name, at, shape, dt=F32R):
            return nc.alloc_sbuf_tensor_at(name, shape, dt, offset=at)

        def next_offset():
            return (nc.sbuf_base + 31) // 32 * 32

        at_qk = next_offset()
        wqk0 = sb("wqk0", [P, 2, DT, HD0])
        wq0, wk0 = wqk0[:, 0, :, :], wqk0[:, 1, :, :]
        qm_hi = overlay("qm_hi", at_qk, [P, 2, 4, S])
        at_vo = next_offset()
        wvo = sb("wvo", [P, 2048])
        wv0 = wvo[:, :].rearrange("p (t n) -> p t n", t=DT)
        wo0 = wvo[:, :].rearrange("p (t n) -> p t n", t=HD0 // P)
        w_l1 = {n: sb("w1_" + n, [P, DT, D]) for n in ("t", "v", "gt", "gv")}
        w_sq = {n: sb("w_" + n, [P, DT, D]) for n in ("q2", "k2", "v2", "sq", "sk", "sv", "cq", "ck", "cv")}
        w_out = {a: sb(f"w_out{a}", [P, GROUPS, D]) for a in (CAUSAL, BANDED, FULL)}
        cols = sb("cols", [P, NCOLS])
        rows = sb("rows", [P, NROWS, D])
        ident = sb("ident", [P, P])
        tri = sb("tri", [P, P])
        hmask = sb("hmask", [P, 10])
        ones = sb("ones", [P, P])
        cbf = sb("cbf", [P, NBF], BF16)
        kcol = sb("kcol", [P, 3, DT])
        kcol0 = sb("kcol0", [P, 2, PAIRS])
        qcol = sb("qcol", [P, 8])
        epsc = sb("epsc", [P, 1])

        act_t = sb("act_t", [P, DT, S])
        ctx_t = sb("ctx_t", [P, DT, S])
        region_e = sb("region_e", [P, 8192])
        at_b = next_offset()
        region_b = sb("region_b", [P, 4096])
        at_c = next_offset()
        region_c = sb("region_c", [P, 4096])
        region_d = sb("region_d", [P, 2048])
        at_q = next_offset()
        region_q = sb("region_q", [P, 2048])
        e0 = region_e[:, 0:E0 * 1024].rearrange("p (u h q) -> p u h q", u=E0, h=2)
        k0_odd = region_e[:, E0 * 1024:8192].rearrange("p (u k) -> p u k", u=2)
        e16 = region_e[:, :].rearrange("p (u s q) -> p u s q", u=4, s=4)
        hid = region_e[:, 0:4096].rearrange("p (t q) -> p t q", t=FT)
        v0 = region_b[:, :].rearrange("p (t n) -> p t n", t=NT)
        w_f1 = region_b[:, 0:2048].rearrange("p (t n) -> p t n", t=DT)
        w_f2 = region_b[:, 2048:4096].rearrange("p (t n) -> p t n", t=FT)
        o0 = region_c[:, :].rearrange("p (t q) -> p t q", t=PAIRS)

        k_b = overlay("k_b", at_b, [P, 2, DT, S])
        k_c = overlay("k_c", at_c, [P, 2, DT, S])
        v_b = region_b[:, 2048:4096].rearrange("p (t h c) -> p t h c", t=NT, h=H)
        v_c = region_c[:, 2048:4096].rearrange("p (t h c) -> p t h c", t=NT, h=H)
        k_of = {CAUSAL: k_b, BANDED: k_b, FULL: k_c}
        v_of = {CAUSAL: v_b, BANDED: v_b, FULL: v_c}
        sm0 = region_d[:, :].rearrange("p (u h q) -> p u h q", u=2, h=2)
        v2 = region_d[:, 0:1024].rearrange("p (t n) -> p t n", t=NT)
        w_om = region_d[:, 1024:1536].rearrange("p (t n) -> p t n", t=DT)
        oT = region_d[:, :].rearrange("p (g q) -> p g q", g=GROUPS)
        qk0 = region_q[:, :].rearrange("p (u a q) -> p u a q", u=2, a=2)
        tp_t = region_q[:, 0:1024].rearrange("p (t q) -> p t q", t=DT)
        q_t = region_q[:, 1024:2048].rearrange("p (t q) -> p t q", t=DT)

        vs0 = sb("vs0", [P, 4, 2, DK0])
        rbuf = sb("rbuf", [P, S])
        mask_i = rbuf[:, :].bitcast(I32)
        maskb = sb("maskb", [P, S])
        nat_x = sb("nat_x", [P, NT, D])
        at_y = next_offset()
        nat_y = sb("nat_y", [P, NT, D])
        x_nat = nat_y
        lo_vo = overlay("lo_vo", at_vo, [P, 4, S])
        lo_q = overlay("lo_q", at_q, [P, 2, S])
        lo_y = overlay("lo_y", at_y, [P, 2, S])
        qm_lo = [[lo_vo[:, s, :] for s in range(4)], [lo_q[:, s, :] for s in range(2)] + [lo_y[:, s, :] for s in range(2)]]
        nat_n = sb("nat_n", [P, NT, D])
        k_full = {a: t[:, :, :].rearrange("p n d -> p (n d)").rearrange("p (t k) -> p t k", t=DT)
                  for a, t in ((CAUSAL, nat_n), (FULL, nat_y), (BANDED, nat_x))}
        mrow = sb("mrow", [P, 2, S], BF16)
        mcol = sb("mcol", [P, 2, NT, P], BF16)
        mcol_s = sb("mcol_s", [P, GROUPS, NT, P], BF16)
        nmin0 = sb("nmin0", [P, UNITS0, 2])
        sum0 = sb("sum0", [P, UNITS0, 2])
        rs0 = sb("rs0", [P, UNITS0, 2])
        nmax = sb("nmax", [P, NT, 4])
        nanfix = sb("nanfix", [P, 4])
        stats = sb("stats", [P, NT, 6])
        mv = sb("mv", [P, NT, 2])
        lnv = sb("lnv", [P, NT])
        std = sb("std", [P, NT])
        rstd = sb("rstd", [P, NT])
        std1 = sb("std1", [P, NT])
        pooled = sb("pooled", [P, DT])
        small = sb("small", [P, DT])
        held = sb("held", [P, HOLDS + SLOTS])
        rrow = rbuf
        one_sum = sb("one_sum", [1, 4])
        rcol = sb("rcol", [P, NT])
        vp_b = region_q[:, 1024:1024 + D]
        u_b = region_q[:, 1024 + D:1024 + 2 * D]
        wide = sb("wide", [P, DT, P])
        km = sb("km", [P, NT])
        degen = sb("degen", [P, NT])
        mean_o = sb("mean_o", [P, D])

        def col(name, t=0):
            return cols[:, COL[name] + t:COL[name] + t + 1]

        def row(name, n=1):
            return rows[:, ROW[name]:ROW[name] + n, :]

        def cb(name, n, part=slice(0, P), at=0):
            return cbf[part, CST[name] + at:CST[name] + at + n]

        filled = [sem(f"filled{s}") for s in range(SLOTS)]
        drained = [sem(f"drained{s}") for s in range(SLOTS)]
        pv_done = sem("pv_done")
        out_drained = sem("out_drained")
        exp0_done = sem("exp0_done")
        exp_done = sem("exp_done")
        vs_ready = sem("vs_ready")
        k_loaded = {n: sem("ld_" + n) for n in ("act", "ctx", "x", "mask", "wq0", "wk0", "wv0", "wo0", "ff", "small",
                                               "const", "l1", "om", "l2", "ls", "lc")}
        stored = sem("stored")
        setup_dve = sem("setup_dve")
        setup_act = sem("setup_act")
        setup_pool = sem("setup_pool")
        dve_link = sem("dve_link")
        act_link = sem("act_link")
        pool_link = sem("pool_link")
        mask_ready = sem("mask_ready")
        resid0_ready = sem("resid0_ready")
        pooled_ready = sem("pooled_ready")
        wide_ready = sem("wide_ready")
        agree_max = sem("agree_max")
        agree_exp = sem("agree_exp")
        agree_inv = sem("agree_inv")
        gate_ready = sem("gate_ready")
        km_ready = sem("km_ready")
        vmask_ready = sem("vmask_ready")
        ones_ready = sem("ones_ready")
        k_split = sem("k_split")
        qm_hi_ready = sem("qm_hi_ready")
        qm_lo_ready = sem("qm_lo_ready")
        mcol_ready = sem("mcol_ready")
        heads_ready = sem("heads_ready")
        heads0_ready = sem("heads0_ready")
        var_ready = sem("var_ready")
        rstd_ready = sem("rstd_ready")
        norm_ready = sem("norm_ready")
        resid_ready = sem("resid_ready")

        def slot(name):
            return ring[:, JOB[name] % SLOTS, :, :]

        def filled_by(name, b):
            return filled[JOB[name] % SLOTS], b * ROUNDS + JOB[name] // SLOTS + 1

        def drained_by(name, b):
            return drained[JOB[name] % SLOTS], b * ROUNDS + JOB[name] // SLOTS + 2

        def free_for(name, b):
            return drained[JOB[name] % SLOTS], b * ROUNDS + JOB[name] // SLOTS + 1

        def ends_fill(name):
            return filled[JOB[name] % SLOTS], 1

        def ends_drain(name):
            return drained[JOB[name] % SLOTS], 1

        def width(a, g_tile):
            if a == FULL:
                return 0, S
            if a == CAUSAL:
                return P * g_tile, S - P * g_tile
            return P * g_tile, min(BAND, S - P * g_tile)

        def seen(a, qt):
            if a == FULL:
                return 0, S
            if a == CAUSAL:
                return 0, P * (qt + 1)
            lo = max(0, P * qt - W)
            return lo, P * (qt + 1) - lo

        block = ctx.enter_context(nc.Block())

        @block.sync
        def _(sp):
            def load(dst, src, name):
                sp.dma_start(dst, src).then_inc(k_loaded[name], 16)

            def load_act(b):
                load(act_t[:, :, :], io["xT"][b].rearrange("(t p) s -> p t s", p=P), "act")

            def load_ctx(b):
                load(ctx_t[:, :, :], io["ctxT"][b].rearrange("(t p) s -> p t s", p=P), "ctx")

            def load_x(b):
                load(x_nat[:, :, :], io["x"][b].rearrange("(t p) d -> p t d", p=P), "x")

            def load_mask(b):
                load(mask_i, io["mask"][b:b + 1, :].broadcast_to([P, S]), "mask")

            load_ctx(0)
            load(wv0, io["wv0"].rearrange("(t p) n -> p t n", p=P), "wv0")
            load_act(0)
            load(wq0, io["wq0"].rearrange("(t p) n -> p t n", p=P), "wq0")
            load(wk0, io["wk0"].rearrange("(t p) n -> p t n", p=P), "wk0")
            load_mask(0)
            load_x(0)
            for n in ("t", "v", "gt", "gv"):
                load(w_l1[n][:, :, :], io["w1_" + n].rearrange("(t p) n -> p t n", p=P), "l1")
            for names, a, s in ((("q2", "k2", "v2"), CAUSAL, "l2"), (("sq", "sk", "sv"), BANDED, "ls"),
                                (("cq", "ck", "cv"), FULL, "lc")):
                for n in names:
                    load(w_sq[n][:, :, :], io["w_" + n].rearrange("(t p) n -> p t n", p=P), s)
                load(w_out[a][:, :, :], io[f"w_out{a}"].rearrange("(g p) n -> p g n", p=P), s)
            for b in range(B):
                for t in range(NT):
                    sp.wait_ge(*filled_by(("V0", t), b))
                if b:
                    sp.wait_ge(stored, b * 16)
                load(wo0, io["wo0"].rearrange("(t p) n -> p t n", p=P), "wo0")
                sp.wait_ge(exp0_done, (b + 1) * UNITS0)
                load(w_om, io["w_om"].rearrange("(t p) n -> p t n", p=P), "om")
                if b + 1 < B:
                    sp.wait_ge(*filled_by(("KC",), b))
                    sp.wait_ge(*filled_by(("VC", 0), b))
                    sp.wait_ge(*filled_by(("VC", 1), b))
                    sp.wait_ge(pooled_ready, b + 1)
                    load_ctx(b + 1)
                sp.wait_ge(pv_done, b * PV_ITER + UNITS0 + 2 * UNITS)
                load(w_f1, io["w_f1"].rearrange("(t p) n -> p t n", p=P), "ff")
                load(w_f2, io["w_f2"].rearrange("(t p) n -> p t n", p=P), "ff")
                if b + 1 < B:
                    sp.wait_ge(*filled_by((FULL, "B", GROUPS - 1, NT - 1, 1), b))
                    load(wv0, io["wv0"].rearrange("(t p) n -> p t n", p=P), "wv0")
                    load(wq0, io["wq0"].rearrange("(t p) n -> p t n", p=P), "wq0")
                    load(wk0, io["wk0"].rearrange("(t p) n -> p t n", p=P), "wk0")
                    sp.wait_ge(out_drained, (b + 1) * OUT_ITER)
                    load_mask(b + 1)
                    for j in range(FT // 2):
                        sp.wait_ge(*filled_by(("F1", j), b))
                    load_act(b + 1)
                    sp.wait_ge(norm_ready, (b + 1) * 5)
                    load_x(b + 1)
                sp.wait_ge(resid_ready, (b + 1) * 4)
                sp.dma_start(out[b].rearrange("(t p) d -> p t d", p=P), nat_x[:, :, :]).then_inc(stored, 16)
            sp.wait_ge(stored, B * 16)

        @block.gpsimd
        def _(pool):
            pool.memset(ones[:, :], 1.0).then_inc(setup_pool, 1)
            pool.memset(mcol[:, :, :, :], 0.0).then_inc(setup_pool, 1)
            pool.memset(epsc[:, :], 1e-5).then_inc(setup_pool, 1)
            for s in range(SLOTS):
                pool.memset(held[:, HOLDS + s:HOLDS + s + 1], 0.0).then_inc(drained[s], 1)
            pool.wait_ge(k_loaded["small"], 32)
            pool.tensor_tensor(row("b2n"), row("b2n"), row("b2"), ALU.add).then_inc(setup_pool, 1)
            pool.wait_ge(setup_pool, 4)

            def wide_row(name):
                return row(name).broadcast_to([P, NT, D])

            with pool.Fori(0, B) as b:
                links = [0]

                def link(ins):
                    links[0] += 1
                    ins.then_inc(pool_link, 1)
                    pool.wait_ge(pool_link, b * POOL_LINKS + links[0])

                def put_ones(v):
                    one = ones[:, 0:NT * H].rearrange("p (t h) -> p t h", t=NT).unsqueeze(3).broadcast_to([P, NT, H, DH])
                    pool.tensor_tensor(v[:, :, :, DH:2 * DH], one, one, ALU.mult).then_inc(ones_ready, 1)

                def split_k(a):
                    pool.wait_ge(*drained_by(K_JOB[a], b))
                    pool.tensor_tensor(k_of[a][:, 1, :, :], k_full[a], k_of[a][:, 0, :, :], ALU.subtract).then_inc(k_split, 1)

                pool.wait_ge(k_loaded["x"], b * 16 + 16)
                pool.tensor_tensor(x_nat[:, :, :], x_nat[:, :, :], wide_row("bo0"), ALU.add).then_inc(resid0_ready, 1)

                split_k(CAUSAL)
                split_k(FULL)
                pool.wait_ge(*filled_by(("VC", 0), b))
                put_ones(v_of[FULL])

                def residual(n, gamma, beta):
                    pool.wait_ge(norm_ready, b * 5 + n + 1)
                    link(pool.tensor_tensor(nat_x[:, :, :], nat_n[:, :, :], wide_row(gamma), ALU.mult))
                    pool.tensor_tensor(nat_x[:, :, :], nat_x[:, :, :], wide_row(beta), ALU.add).then_inc(resid_ready, 1)

                residual(0, "ga1", "be1")
                split_k(BANDED)
                pool.wait_ge(*filled_by(("VS", 0), b))
                put_ones(v_of[BANDED])
                residual(2, "g1", "b1n")
                residual(3, "g2", "b2n")
                residual(4, "g3", "b3n")
                assert links[0] == POOL_LINKS, links

        @block.scalar
        def _(act):
            def load_exp_ln():
                act.add_instruction(mybir.InstLoadActFuncSet(name=nc.get_next_instruction_name(), engine=mybir.EngineType.Activation,
                                                             ins=[], outs=[], act_func_set_id=EXP_LN_TABLES))

            load_exp_ln()
            act.dma_start(rows[:, :, :], io["rows"].rearrange("(a n) d -> a n d", a=1).broadcast_to([P, NROWS, D]))\
                .then_inc(k_loaded["small"], 16)
            act.dma_start(cols[:, :], io["cols"]).then_inc(k_loaded["small"], 16)
            act.dma_start(region_e[:, 0:NCONST], io["consts"]).then_inc(k_loaded["const"], 16)
            act.wait_ge(k_loaded["small"], 32)
            act.activation(qcol[:, :], cols[:, COL["bq0"]:COL["bq0"] + 8], ACT.Copy, scale=DK0 ** -0.5).then_inc(setup_act, 1)
            act.wait_ge(setup_dve, 3)
            for i, name in enumerate(("bk2", "sbk", "cbk")):
                act.activation(kcol[:, i, :], cols[:, COL[name]:COL[name] + DT], ACT.Copy, scale=DH ** -0.5).then_inc(setup_act, 1)
            for h in range(2):
                act.activation(kcol0[:, h, :], cols[:, COL["bk0"]:COL["bk0"] + PAIRS], ACT.Copy,
                               scale=hmask[:, 8 + h:9 + h]).then_inc(setup_act, 1)
            act.wait_ge(setup_act, 6)
            act.wait_ge(setup_dve, 5)
            act.wait_ge(setup_pool, 4)

            with act.Fori(0, B) as b:
                links = [0]

                def link(ins):
                    links[0] += 1
                    ins.then_inc(act_link, 1)
                    act.wait_ge(act_link, b * ACT_LINKS + links[0])

                def drain_qk(p):
                    act.wait_ge(*filled_by(("QK0", p), b))
                    src = slot(("QK0", p))
                    act.activation(qk0[:, p % 2, 0, :], src[:, 0, :], ACT.Identity, bias=qcol[:, p:p + 1], scale=DK0 ** -0.5)
                    for h, dst in enumerate((qk0[:, p % 2, 1, :], k0_odd[:, p % 2, :])):
                        ins = act.activation(dst, src[:, 1, :], ACT.Identity, bias=kcol0[:, h, p:p + 1], scale=hmask[:, 8 + h:9 + h])
                    ins.then_inc(*ends_drain(("QK0", p)))

                drain_qk(0)
                for p in range(PAIRS):
                    for kt in range(NT):
                        n = NT * p + kt
                        act.wait_ge(*drained_by(("S0", p, kt), b))
                        if n >= E0:
                            act.wait_ge(pv_done, b * PV_ITER + n - E0 + 1)
                        for h in range(2):
                            ins = act.activation(e0[:, n % E0, h, :], sm0[:, n % 2, h, :], ACT.Exp, bias=nmin0[:, n, h:h + 1],
                                                 scale=-1.0, accum_out=sum0[:, n, h:h + 1])
                        ins.then_inc(exp0_done, 1)
                        if kt == 1 and p + 1 < PAIRS:
                            drain_qk(p + 1)

                act.wait_ge(*filled_by(("vpT",), b))
                act.activation(wide[:, :, :], slot(("vpT",))[:, 0, 0:D].rearrange("p (t n) -> p t n", t=DT), ACT.Copy)\
                    .then_inc(*ends_drain(("vpT",)))

                def drain_k(name, a, i, func):
                    act.wait_ge(*filled_by(name, b))
                    for dst in (k_of[a][:, 0, :, :], k_full[a]):
                        for t in range(DT):
                            ins = act.activation(dst[:, t, :], slot(name)[:, t, :], func, bias=kcol[:, i, t:t + 1], scale=DH ** -0.5)
                    ins.then_inc(*ends_drain(name))

                def high_parts(a, g):
                    if g >= 2:
                        act.wait_ge(*filled_by((a, "B", g - 2, NT - 1, 1), b))
                    for s in range(4):
                        h = 4 * (g % 2) + s
                        act.activation(qm_hi[:, g % 2, s, :], q_t[:, g // 2, :], ACT.Copy, scale=hmask[:, h:h + 1])\
                            .then_inc(qm_hi_ready, 1)

                def drain_x(n, gamma=None, beta=None):
                    act.wait_ge(*filled_by(("X", n), b))
                    src = slot(("X", n))
                    if gamma is None:
                        act.activation(act_t[:, :, :], src, ACT.Copy).then_inc(*ends_drain(("X", n)))
                        return
                    for t in range(DT):
                        ins = act.activation(act_t[:, t, :], src[:, t, :], ACT.Identity, bias=col(beta, t), scale=col(gamma, t))
                    ins.then_inc(*ends_drain(("X", n)))

                def rsqrt(n, sign, scale=1.0, eps=True):
                    act.wait_ge(var_ready, b * 5 + n + 1)
                    if eps:
                        link(act.activation(lnv[:, :], mv[:, :, 1], ACT.Ln, bias=epsc[:, 0:1]))
                    else:
                        link(act.activation(lnv[:, :], std1[:, :], ACT.Ln, scale=scale))
                    act.activation(std[:, :], lnv[:, :], ACT.Exp, scale=0.5 * sign).then_inc(rstd_ready, 1)

                drain_x(0)
                drain_k(("K2",), CAUSAL, 0, ACT.Relu)
                act.wait_ge(*filled_by(("tp",), b))
                for t in range(DT):
                    ins = act.activation(tp_t[:, t, :], slot(("tp",))[:, t, :], ACT.Identity, bias=col("bt", t))
                ins.then_inc(*ends_drain(("tp",)))
                act.wait_ge(*filled_by(("ksum",), b))
                drain_k(("KC",), FULL, 2, ACT.Identity)
                act.wait_ge(agree_max, b + 1)
                act.activation(rrow[0:1, :], slot(("agree",))[0:1, 0, :], ACT.Exp, bias=one_sum[0:1, 1:2], scale=2.0,
                               accum_out=one_sum[0:1, 2:3]).then_inc(*ends_drain(("agree",)))
                for j in range(2):
                    act.wait_ge(*drained_by(("gate", j), b))
                    part = nat_n[:, 2 * j:2 * j + 2, :]
                    act.activation(part, part, ACT.Sigmoid).then_inc(gate_ready, 1)
                load_exp_ln()
                rsqrt(0, -1)
                drain_x(1, "ga1", "be1")

                def attention(a, q_job):
                    act.wait_ge(*drained_by(q_job, b))
                    high_parts(a, 0)
                    high_parts(a, 1)
                    for g in range(GROUPS):
                        act.wait_ge(*filled_by((a, "T", g), b))
                        act.activation(mrow[:, g % 2, :], slot((a, "T", g))[:, 0, 0:256].bitcast(BF16), ACT.Copy)\
                            .then_inc(*ends_drain((a, "T", g)))
                        for kt in range(NT):
                            n = UNITS * a + NT * g + kt
                            q0, nq = width(a, kt)
                            for u in range(2):
                                act.wait_ge(*filled_by((a, "B", g, kt, u), b))
                                act.wait_ge(pv_done, b * PV_ITER + UNITS0 + max(0, n - 3))
                                act.activation(e16[:, n % 4, 2 * u:2 * u + 2, 0:nq], slot((a, "B", g, kt, u))[:, :, 0:nq], ACT.Exp)\
                                    .then_inc(*ends_drain((a, "B", g, kt, u)))
                        if g + 2 < GROUPS:
                            high_parts(a, g + 2)

                attention(CAUSAL, ("Q2",))
                rsqrt(1, +1, scale=D / (D - 1), eps=False)
                drain_x(2)
                drain_k(("KS",), BANDED, 1, ACT.Identity)
                attention(BANDED, ("QS",))
                rsqrt(2, -1)
                drain_x(3, "g1", "b1n")
                attention(FULL, ("QC",))
                rsqrt(3, -1)
                drain_x(4, "g2", "b2n")
                for j in range(FT // 2):
                    act.wait_ge(*filled_by(("F1", j), b))
                    for i in range(2):
                        ins = act.activation(hid[:, 2 * j + i, :], slot(("F1", j))[:, i, :], ACT.Gelu, bias=col("b1", 2 * j + i))
                    ins.then_inc(*ends_drain(("F1", j)))
                load_exp_ln()
                rsqrt(4, -1)
                assert links[0] == ACT_LINKS, links

        @block.vector
        def _(dve):
            dve.wait_ge(k_loaded["const"], 16)
            c = region_e
            dve.tensor_copy(cbf[:, :], c[:, 0:NBF]).then_inc(setup_dve, 1)
            dve.tensor_copy(ident[:, :], c[:, CST["ident"]:CST["ident"] + P]).then_inc(setup_dve, 1)
            dve.tensor_copy(hmask[:, :], c[:, CST["hmask"]:CST["hmask"] + 10]).then_inc(setup_dve, 1)
            dve.tensor_copy(tri[:, :], c[:, CST["tri"]:CST["tri"] + P]).then_inc(setup_dve, 1)
            for g in range(GROUPS):
                ins = dve.tensor_copy(mcol_s[:, g, :, :],
                                      c[:, CST["slopeM"] + g * P:CST["slopeM"] + (g + 1) * P].unsqueeze(1).broadcast_to([P, NT, P]))
            ins.then_inc(setup_dve, 1)
            dve.wait_ge(setup_dve, 5)
            dve.wait_ge(setup_pool, 4)
            dve.wait_ge(setup_act, 6)

            with dve.Fori(0, B) as b:
                links = [0]

                def link(ins):
                    links[0] += 1
                    ins.then_inc(dve_link, 1)
                    dve.wait_ge(dve_link, b * DVE_LINKS + links[0])

                holds = [0]

                def hold():
                    dve.memset(held[0:1, holds[0]:holds[0] + 1], 0.0)
                    holds[0] += 1

                dve.wait_ge(k_loaded["mask"], b * 16 + 16)
                link(dve.tensor_scalar(maskb[:, :], mask_i, 0.0, NEG, ALU.is_equal, ALU.mult))
                link(dve.tensor_reduce(nanfix[:, 0:1], maskb[:, :], AX.X, ALU.max))
                link(dve.tensor_scalar(nanfix[:, 1:2], nanfix[:, 0:1], 0.0, None, ALU.is_equal))
                link(dve.reciprocal(nanfix[:, 2:3], nanfix[:, 1:2]))
                link(dve.tensor_scalar(nanfix[:, 3:4], nanfix[:, 2:3], 0.0, None, ALU.mult))

                for t in range(NT):
                    dve.wait_ge(*filled_by(("V0", t), b))
                    dve.tensor_tensor(v0[:, t, :], slot(("V0", t)).rearrange("p a n -> p (a n)"),
                                      row("bv0", 4).rearrange("p a n -> p (a n)"), ALU.add).then_inc(*ends_drain(("V0", t)))
                dve.wait_ge(*drained_by(("V0", NT - 1), b))
                dve.wait_ge(k_loaded["ctx"], b * 16 + 16)
                link(dve.tensor_reduce(small[:, 0:2], ctx_t[:, :, :], AX.X, ALU.add))
                dve.tensor_scalar(pooled[:, :], small[:, 0:2], 1.0 / S, None, ALU.mult).then_inc(pooled_ready, 1)
                dve.wait_ge(pooled_ready, b + 1)
                dve.tensor_copy(wide[:, :, :], pooled[:, :].unsqueeze(2).broadcast_to([P, DT, P])).then_inc(wide_ready, 1)

                def scale_v(n):
                    p, kt = n // NT, n % NT
                    dve.wait_ge(exp0_done, b * UNITS0 + n + 1)
                    link(dve.reciprocal(rs0[:, n, :], sum0[:, n, :]))
                    if n >= 4:
                        dve.wait_ge(pv_done, b * PV_ITER + n - 3)
                    dve.tensor_tensor(vs0[:, n % 4, :, :], v0[:, kt, 2 * DK0 * p:2 * DK0 * (p + 1)].rearrange("p (h c) -> p h c", h=2),
                                      rs0[:, n, :].unsqueeze(2).broadcast_to([P, 2, DK0]), ALU.mult).then_inc(vs_ready, 1)

                def drain_heads0(p):
                    dve.wait_ge(pv_done, b * PV_ITER + NT * (p + 1))
                    dve.tensor_copy(o0[:, p, :], obank[:, p % 2, :]).then_inc(out_drained, 1)

                for n in range(UNITS0):
                    p, kt = n // NT, n % NT
                    dve.wait_ge(*filled_by(("S0", p, kt), b))
                    if n >= 2:
                        dve.wait_ge(exp0_done, b * UNITS0 + n - 1)
                    hold()
                    for h in range(2):
                        ins = dve.tensor_tensor_reduce(out=sm0[:, n % 2, h, :], in0=slot(("S0", p, kt))[:, h, :], in1=maskb[:, :],
                                                       scale=-1.0, scalar=3.0e38, op0=ALU.add, op1=ALU.min,
                                                       accum_out=nmin0[:, n, h:h + 1])
                    ins.then_inc(*ends_drain(("S0", p, kt)))
                    if n >= 1:
                        scale_v(n - 1)
                    if kt == 2 and p >= 2:
                        drain_heads0(p - 2)
                scale_v(UNITS0 - 1)
                drain_heads0(PAIRS - 2)
                drain_heads0(PAIRS - 1)

                dve.wait_ge(resid0_ready, b + 1)
                for j in range(2):
                    dve.wait_ge(*filled_by(("O0", j), b))
                    dve.scalar_tensor_tensor(out=nat_x[:, 2 * j:2 * j + 2, :], in0=slot(("O0", j))[:, :, 0:D], scalar=nanfix[:, 3:4],
                                             in1=x_nat[:, 2 * j:2 * j + 2, :], op0=ALU.add, op1=ALU.add)\
                        .then_inc(*ends_drain(("O0", j)))

                dve.wait_ge(*filled_by(("vp",), b))
                dve.tensor_tensor(vp_b[:, :], slot(("vp",))[:, 0, 0:D], row("bv1").squeeze(1), ALU.add).then_inc(*ends_drain(("vp",)))

                def drain_v(name, bias, dst):
                    for j in range(2):
                        dve.wait_ge(*filled_by((name, j), b))
                        for i in range(2):
                            ins = dve.tensor_tensor(dst(2 * j + i), slot((name, j))[:, i, 0:D].rearrange("p (h c) -> p h c", h=H),
                                                    row(bias).squeeze(1).rearrange("p (h c) -> p h c", h=H), ALU.add)
                        ins.then_inc(*ends_drain((name, j)))

                drain_v("V2", "bv2", lambda t: v2[:, t, :].rearrange("p (h c) -> p h c", h=H))
                dve.wait_ge(*filled_by(("uv",), b))
                dve.tensor_copy(u_b[:, :], slot(("uv",))[:, 0, 0:D]).then_inc(*ends_drain(("uv",)))
                dve.wait_ge(*filled_by(("ksum",), b))
                dve.tensor_scalar(km[:, :], slot(("ksum",))[:, 0, 0:NT], 0.0, None, ALU.is_gt).then_inc(*ends_drain(("ksum",)))
                drain_v("VC", "cbv", lambda t: v_of[FULL][:, t, :, 0:DH])
                dve.wait_ge(*filled_by(("agree",), b))
                link(dve.tensor_reduce(one_sum[0:1, 0:1], slot(("agree",))[0:1, 0, :], AX.X, ALU.max))
                dve.tensor_scalar(one_sum[0:1, 1:2], one_sum[0:1, 0:1], -2.0, None, ALU.mult).then_inc(agree_max, 1)
                link(dve.tensor_scalar(v2[:, :, :], v2[:, :, :], 0.0, None, ALU.max))
                dve.wait_ge(*drained_by(("ksum",), b))
                for t in range(NT):
                    dve.tensor_scalar(v_of[CAUSAL][:, t, :, 0:DH], v2[:, t, :].rearrange("p (h c) -> p h c", h=H),
                                      km[:, t:t + 1], None, ALU.mult)
                    ins = dve.tensor_scalar(v_of[CAUSAL][:, t, :, DH:2 * DH], ones[:, 0:DH].unsqueeze(1).broadcast_to([P, H, DH]),
                                            km[:, t:t + 1], None, ALU.mult)
                ins.then_inc(vmask_ready, 1)
                dve.wait_ge(*drained_by(("agree",), b))
                dve.reciprocal(one_sum[0:1, 3:4], one_sum[0:1, 2:3]).then_inc(agree_inv, 1)
                dve.wait_ge(*filled_by(("cnt",), b))
                dve.tensor_scalar(degen[:, :], slot(("cnt",))[:, 0, 0:NT], 0.5, None, ALU.is_lt).then_inc(*ends_drain(("cnt",)))
                dve.wait_ge(*filled_by(("rcol",), b))
                dve.tensor_copy(rcol[:, :], slot(("rcol",))[:, 0, 0:NT]).then_inc(*ends_drain(("rcol",)))
                dve.wait_ge(*filled_by(("meanV",), b))
                dve.tensor_scalar(wide[:, :, :], slot(("meanV",))[:, 0, 0:DT].unsqueeze(2).broadcast_to([P, DT, P]), 1.0 / S, None, ALU.mult)\
                    .then_inc(*ends_drain(("meanV",)))
                dve.wait_ge(*drained_by(("rcol",), b))
                dve.wait_ge(k_split, b * 3 + 2)
                for j in range(2):
                    dve.wait_ge(*filled_by(("gate", j), b))
                    for i in range(2):
                        t = 2 * j + i
                        ins = dve.scalar_tensor_tensor(out=nat_n[:, t, :], in0=u_b[:, :], scalar=rcol[:, t:t + 1],
                                                       in1=slot(("gate", j))[:, i, 0:D], op0=ALU.mult, op1=ALU.add)
                    ins.then_inc(*ends_drain(("gate", j)))
                dve.wait_ge(gate_ready, b * 2 + 2)
                for t in range(NT):
                    ins = dve.scalar_tensor_tensor(out=nat_y[:, t, :], in0=vp_b[:, :], scalar=rcol[:, t:t + 1], in1=nat_n[:, t, :],
                                                   op0=ALU.mult, op1=ALU.mult)
                link(ins)
                link(dve.tensor_tensor(nat_y[:, :, :], nat_y[:, :, :], nat_x[:, :, :], ALU.add))

                def norm(n):
                    for t in range(NT):
                        ins = dve.bn_stats(stats[:, t, :], nat_y[:, t, :])
                    link(ins)
                    hold()
                    for t in range(NT):
                        ins = dve.bn_aggr(mv[:, t, :], stats[:, t, :])
                    if n == 1:
                        link(ins)
                        ins = dve.tensor_scalar(std1[:, :], mv[:, :, 1], 1e-18, None, ALU.max)
                    ins.then_inc(var_ready, 1)
                    dve.wait_ge(rstd_ready, b * 5 + n + 1)
                    scale = std
                    if n == 1:
                        link(dve.tensor_scalar(std1[:, :], std[:, :], 1e-8, None, ALU.add))
                        link(dve.reciprocal(rstd[:, :], std1[:, :]))
                        scale = rstd
                    for t in range(NT):
                        ins = dve.tensor_scalar(nat_n[:, t, :], nat_y[:, t, :], mv[:, t, 0:1], scale[:, t:t + 1],
                                                ALU.subtract, ALU.mult)
                    ins.then_inc(norm_ready, 1)

                norm(0)
                dve.wait_ge(*filled_by(("meanO",), b))
                dve.tensor_tensor(mean_o[:, :], slot(("meanO",))[:, 0, 0:D], row("bo2").squeeze(1), ALU.add)\
                    .then_inc(*ends_drain(("meanO",)))

                def drain_q(name, bias, relu=False):
                    dve.wait_ge(*filled_by(name, b))
                    for t in range(DT):
                        ins = dve.tensor_scalar(q_t[:, t, :], slot(name)[:, t, :], col(bias, t), 0.0 if relu else None,
                                                ALU.add, ALU.max if relu else ALU.bypass)
                    ins.then_inc(*ends_drain(name))

                def low_part(a, g, s):
                    h = 4 * (g % 2) + s
                    dve.wait_ge(qm_hi_ready, b * 3 * H + a * H + 4 * g + s + 1)
                    if g >= 2 and s == 0:
                        dve.wait_ge(*filled_by((a, "B", g - 2, NT - 1, 1), b))
                    dve.scalar_tensor_tensor(out=qm_lo[g % 2][s], in0=q_t[:, g // 2, :], scalar=hmask[:, h:h + 1],
                                             in1=qm_hi[:, g % 2, s, :], op0=ALU.mult, op1=ALU.subtract).then_inc(qm_lo_ready, 1)

                def maxima(a, g, qt, u):
                    _, nk = seen(a, qt)
                    name = (a, "A", g, qt, u)
                    dve.wait_ge(*filled_by(name, b))
                    dve.tensor_reduce(nmax[:, qt, 2 * u:2 * u + 2], slot(name)[:, :, 0:nk], AX.X, ALU.max, negate=True)\
                        .then_inc(*ends_drain(name))

                def maxima_cols(a, g):
                    m = (mcol_s[:, g, :, :] if a == BANDED else mcol[:, g % 2, :, :]).rearrange("p t (s c) -> p t s c", s=4)
                    dve.wait_ge(*drained_by((a, "A", g, NT - 1, 1), b))
                    link(dve.tensor_copy(m[:, :, :, 0], nmax[:, :, :]))
                    dve.tensor_tensor(m[:, :, :, 1], nmax[:, :, :], m[:, :, :, 0], ALU.subtract).then_inc(mcol_ready, 1)
                    dve.wait_ge(mcol_ready, b * 12 + a * GROUPS + g + 1)

                def head_out(a, g):
                    n = a * GROUPS + g
                    dve.wait_ge(out_drained, b * OUT_ITER + PAIRS + n)
                    dve.wait_ge(pv_done, b * PV_ITER + UNITS0 + NT * (n + 1))
                    hold()
                    o = obank[:, (PAIRS + n) % 2, :]
                    link(dve.stream_shuffle(rbuf[:, :], o, [DH + i % DH for i in range(32)]))
                    if a == CAUSAL:
                        link(dve.tensor_scalar(rbuf[:, :], rbuf[:, :], 1e-30, None, ALU.max))
                    link(dve.reciprocal(rbuf[:, :], rbuf[:, :]))
                    dve.tensor_tensor(oT[:, g, :], o, rbuf[:, :], ALU.mult).then_inc(out_drained, 1)

                def attention(a):
                    for qt in range(NT):
                        for u in range(2):
                            maxima(a, 0, qt, u)
                        low_part(a, 0, qt)
                    maxima_cols(a, 0)
                    for g in range(GROUPS):
                        if g + 1 < GROUPS:
                            for qt in range(NT):
                                for u in range(2):
                                    maxima(a, g + 1, qt, u)
                                low_part(a, g + 1, qt)
                            maxima_cols(a, g + 1)
                        if g >= 1:
                            head_out(a, g - 1)
                    head_out(a, GROUPS - 1)

                drain_q(("Q2",), "bq2", relu=True)
                attention(CAUSAL)
                dve.wait_ge(resid_ready, b * 4 + 1)
                for j in range(2):
                    dve.wait_ge(*filled_by(("O2", j), b))
                    for i in range(2):
                        t = 2 * j + i
                        ins = dve.scalar_tensor_tensor(out=nat_y[:, t, :], in0=mean_o[:, :], scalar=degen[:, t:t + 1],
                                                       in1=slot(("O2", j))[:, i, 0:D], op0=ALU.mult, op1=ALU.add)
                    ins.then_inc(*ends_drain(("O2", j)))
                    dve.wait_ge(*drained_by(("O2", j), b))
                    part = slice(2 * j, 2 * j + 2)
                    link(dve.scalar_tensor_tensor(out=nat_y[:, part, :], in0=nat_y[:, part, :], scalar=0.0, in1=nat_x[:, part, :],
                                                  op0=ALU.max, op1=ALU.add))
                norm(1)

                def drain_out(name, resid):
                    for j in range(2):
                        part = slice(2 * j, 2 * j + 2)
                        dve.wait_ge(*filled_by((name, j), b))
                        dve.tensor_tensor(nat_y[:, part, :], slot((name, j))[:, :, 0:D], resid[:, part, :], ALU.add)\
                            .then_inc(*ends_drain((name, j)))
                    for j in range(2):
                        dve.wait_ge(*drained_by((name, j), b))

                drain_q(("QS",), "sbq")
                drain_v("VS", "sbv", lambda t: v_of[BANDED][:, t, :, 0:DH])
                attention(BANDED)
                drain_out("OS", nat_n)
                norm(2)
                drain_q(("QC",), "cbq")
                attention(FULL)
                dve.wait_ge(resid_ready, b * 4 + 2)
                drain_out("OC", nat_x)
                norm(3)
                dve.wait_ge(resid_ready, b * 4 + 3)
                drain_out("F2", nat_x)
                norm(4)
                dve.wait_ge(norm_ready, b * 5 + 5)
                assert links[0] == DVE_LINKS, links

        @block.tensor
        def _(pe):
            pe.wait_ge(setup_dve, 5)
            pe.wait_ge(setup_act, 6)
            pe.wait_ge(setup_pool, 4)
            with pe.Fori(0, B) as b:
                order = [0]

                def start(name):
                    assert JOBS[order[0]] == name, (JOBS[order[0]], name)
                    order[0] += 1
                    pe.wait_ge(*free_for(name, b))
                    return slot(name)

                def project(name, w, src, tiles):
                    dst = start(name)
                    for i, m in enumerate(tiles):
                        for t in range(DT):
                            ins = pe.matmul(dst[:, i, :], w[:, t, m * P:(m + 1) * P], src[:, t, :], start=(t == 0), stop=(t == DT - 1))
                    ins.then_inc(*ends_fill(name))

                def project_nat(name, w, src):
                    for j in range(2):
                        dst = start((name, j))
                        for i in range(2):
                            m = 2 * j + i
                            for t in range(DT):
                                ins = pe.matmul(dst[:, i, 0:D], src[:, t, m * P:(m + 1) * P], w[:, t, :], start=(t == 0), stop=(t == DT - 1))
                        ins.then_inc(*ends_fill((name, j)))

                def out_project(name, w, src, n):
                    for j in range(2):
                        dst = start((name, j))
                        for i in range(2):
                            m = 2 * j + i
                            for t in range(n):
                                ins = pe.matmul(dst[:, i, 0:D], src[:, t, m * P:(m + 1) * P], w[:, t, :], start=(t == 0), stop=(t == n - 1))
                        ins.then_inc(*ends_fill((name, j)))

                pe.wait_ge(k_loaded["ctx"], b * 16 + 16)
                pe.wait_ge(k_loaded["wv0"], b * 16 + 16)
                for kt in range(NT):
                    dst = start(("V0", kt))
                    for i in range(2):
                        for t in range(DT):
                            ins = pe.matmul(dst[:, i, :], ctx_t[:, t, kt * P:(kt + 1) * P], wv0[:, t, i * 512:(i + 1) * 512],
                                            start=(t == 0), stop=(t == DT - 1))
                    ins.then_inc(*ends_fill(("V0", kt)))

                def qk(p):
                    dst = start(("QK0", p))
                    for i, (w, src) in enumerate(((wq0, act_t), (wk0, ctx_t))):
                        for t in range(DT):
                            ins = pe.matmul(dst[:, i, :], w[:, t, p * P:(p + 1) * P], src[:, t, :], start=(t == 0), stop=(t == DT - 1))
                    ins.then_inc(*ends_fill(("QK0", p)))

                def scores0(p, kt):
                    name = ("S0", p, kt)
                    dst = start(name)
                    if kt == 0:
                        pe.wait_ge(*drained_by(("QK0", p), b))
                    for h, k in enumerate((qk0[:, p % 2, 1, :], k0_odd[:, p % 2, :])):
                        ins = pe.matmul(dst[:, h, :], k[:, kt * P:(kt + 1) * P], qk0[:, p % 2, 0, :], start=True, stop=True)
                    ins.then_inc(*ends_fill(name))

                def values0(p, kt):
                    n = NT * p + kt
                    if kt == 0 and p >= 2:
                        pe.wait_ge(out_drained, b * OUT_ITER + p - 1)
                    pe.wait_ge(exp0_done, b * UNITS0 + n + 1)
                    pe.wait_ge(vs_ready, b * UNITS0 + n + 1)
                    for h in range(2):
                        ins = pe.matmul(obank[DK0 * h:DK0 * (h + 1), p % 2, :], vs0[:, n % 4, h, :], e0[:, n % E0, h, :],
                                        start=(kt == 0), stop=(kt == NT - 1))
                    ins.then_inc(pv_done, 1)

                pe.wait_ge(k_loaded["act"], b * 16 + 16)
                pe.wait_ge(k_loaded["wq0"], b * 16 + 16)
                pe.wait_ge(k_loaded["wk0"], b * 16 + 16)
                qk(0)
                for p in range(PAIRS):
                    for kt in range(NT):
                        scores0(p, kt)
                        if p >= 1:
                            values0(p - 1, kt)
                        if kt == 1 and p + 1 < PAIRS:
                            qk(p + 1)
                for kt in range(NT):
                    values0(PAIRS - 1, kt)
                pe.wait_ge(out_drained, b * OUT_ITER + PAIRS)
                pe.wait_ge(k_loaded["wo0"], b * 16 + 16)
                out_project("O0", wo0, o0, PAIRS)

                pe.wait_ge(k_loaded["l1"], 64)
                pe.wait_ge(wide_ready, b + 1)
                dst = start(("vp",))
                for t in range(DT):
                    ins = pe.matmul(dst[:, 0, 0:D], wide[:, t, :], w_l1["v"][:, t, :], start=(t == 0), stop=(t == DT - 1))
                ins.then_inc(*ends_fill(("vp",)))
                dst = start(("vpT",))
                pe.wait_ge(*drained_by(("vp",), b))
                for t in range(DT):
                    ins = pe.transpose(dst[:, 0, t * P:(t + 1) * P], vp_b[:, t * P:(t + 1) * P], ident[:, :])
                ins.then_inc(*ends_fill(("vpT",)))
                def turn(n, src):
                    dst = start(("X", n))
                    for t in range(DT):
                        for m in range(NT):
                            ins = pe.transpose(dst[:, t, m * P:(m + 1) * P], src[:, m, t * P:(t + 1) * P], ident[:, :])
                    ins.then_inc(*ends_fill(("X", n)))

                for j in range(2):
                    pe.wait_ge(*drained_by(("O0", j), b))
                turn(0, nat_x)
                pe.wait_ge(k_loaded["l2"], 64)
                project(("K2",), w_sq["k2"], ctx_t, range(DT))
                project_nat("V2", w_sq["v2"], ctx_t)
                dst = start(("uv",))
                pe.wait_ge(*drained_by(("vpT",), b))
                for t in range(DT):
                    ins = pe.matmul(dst[:, 0, 0:D], wide[:, t, :], w_l1["gv"][:, t, :], start=(t == 0), stop=(t == DT - 1))
                ins.then_inc(*ends_fill(("uv",)))
                pe.wait_ge(*drained_by(("X", 0), b))
                project(("tp",), w_l1["t"], act_t, range(DT))
                dst = start(("ksum",))
                pe.wait_ge(*drained_by(("K2",), b))
                for kt in range(NT):
                    for i in range(DT):
                        ins = pe.matmul(dst[:, 0, kt:kt + 1], k_full[CAUSAL][:, i, kt * P:(kt + 1) * P], ones[:, 0:1],
                                        start=(i == 0), stop=(i == DT - 1))
                ins.then_inc(*ends_fill(("ksum",)))
                pe.wait_ge(k_loaded["lc"], 64)
                project(("KC",), w_sq["ck"], ctx_t, range(DT))
                project_nat("VC", w_sq["cv"], ctx_t)
                dst = start(("agree",))
                pe.wait_ge(*drained_by(("tp",), b))
                for t in range(DT):
                    ins = pe.matmul(dst[0:1, 0, :], wide[:, t, 0:1], tp_t[:, t, :], start=(t == 0), stop=(t == DT - 1))
                ins.then_inc(*ends_fill(("agree",)))
                dst = start(("cnt",))
                pe.wait_ge(*drained_by(("ksum",), b))
                for qt in range(NT):
                    for kt in range(qt + 1):
                        ins = pe.matmul(dst[:, 0, qt:qt + 1], (tri if kt == qt else ones)[:, :], km[:, kt:kt + 1],
                                        start=(kt == 0), stop=(kt == qt))
                ins.then_inc(*ends_fill(("cnt",)))
                dst = start(("rcol",))
                pe.wait_ge(*drained_by(("agree",), b))
                pe.wait_ge(agree_inv, b + 1)
                for t in range(NT):
                    ins = pe.matmul(dst[:, 0, t:t + 1], rrow[0:1, t * P:(t + 1) * P], one_sum[0:1, 3:4], start=True, stop=True)
                ins.then_inc(*ends_fill(("rcol",)))
                dst = start(("meanV",))
                pe.wait_ge(vmask_ready, b + 1)
                for i in range(DT):
                    for kt in range(NT):
                        ins = pe.matmul(dst[:, 0, i:i + 1], v2[:, kt, i * P:(i + 1) * P], ones[:, 0:1], start=(kt == 0), stop=(kt == NT - 1))
                ins.then_inc(*ends_fill(("meanV",)))
                for j in range(2):
                    dst = start(("gate", j))
                    for i in range(2):
                        m = 2 * j + i
                        for t in range(DT):
                            pe.matmul(dst[:, i, 0:D], tp_t[:, t, m * P:(m + 1) * P], w_l1["gt"][:, t, :], start=(t == 0), stop=False)
                        ins = pe.matmul(dst[:, i, 0:D], ones[0:1, :], rows[0:1, ROW["bg"], :], start=False, stop=True)
                    ins.then_inc(*ends_fill(("gate", j)))
                dst = start(("meanO",))
                pe.wait_ge(*drained_by(("meanV",), b))
                pe.wait_ge(k_loaded["om"], b * 16 + 16)
                for t in range(DT):
                    ins = pe.matmul(dst[:, 0, 0:D], wide[:, t, :], w_om[:, t, :], start=(t == 0), stop=(t == DT - 1))
                ins.then_inc(*ends_fill(("meanO",)))
                pe.wait_ge(norm_ready, b * 5 + 1)
                turn(1, nat_n)
                pe.wait_ge(*drained_by(("X", 1), b))
                project(("Q2",), w_sq["q2"], act_t, range(DT))

                def pass_a(a, g, qt, u):
                    name = (a, "A", g, qt, u)
                    dst = start(name)
                    if qt == 0:
                        pe.wait_ge(qm_hi_ready, b * 3 * H + a * H + 4 * g + 2 * u + 2)
                    k0, nk = seen(a, qt)
                    for i in range(2):
                        ins = pe.matmul(dst[:, i, 0:nk], qm_hi[:, g % 2, 2 * u + i, qt * P:(qt + 1) * P], k_of[a][:, 0, g // 2, k0:k0 + nk],
                                        start=True, stop=(a == FULL))
                        if a == BANDED:
                            pe.matmul(dst[:, i, 0:nk], cb("slopeA", P, at=g * P), cb("rowsJ", nk, at=(2 * u + i) * BAND + BAND - nk),
                                      start=False, stop=False)
                        if a != FULL:
                            mask, n, whole = ("bandA", nk, BAND) if a == BANDED else ("maskA", P, P)
                            ins = pe.matmul(dst[:, i, nk - n:nk], cb("ident", P), cb(mask, n, at=whole - n), start=False, stop=True)
                    ins.then_inc(*ends_fill(name))

                def pass_b(a, g, kt, u):
                    name = (a, "B", g, kt, u)
                    dst = start(name)
                    if kt == 0:
                        pe.wait_ge(qm_lo_ready, b * 3 * H + a * H + 4 * g + 2 * u + 2)
                    q0, nq = width(a, kt)
                    k_hi, k_lo = (k_of[a][:, part, g // 2, kt * P:(kt + 1) * P] for part in range(2))
                    for i in range(2):
                        s = 2 * u + i
                        q_hi_s, q_lo_s = qm_hi[:, g % 2, s, q0:q0 + nq], qm_lo[g % 2][s][:, q0:q0 + nq]
                        pe.matmul(dst[:, i, 0:nq], k_hi, q_hi_s, start=True, stop=False)
                        pe.matmul(dst[:, i, 0:nq], k_hi, q_lo_s, start=False, stop=False)
                        pe.matmul(dst[:, i, 0:nq], k_lo, q_hi_s, start=False, stop=False)
                        if a == BANDED:
                            ins = pe.matmul(dst[:, i, 0:P], cb("rowsB0", P, at=s * P), mrow[:, g % 2, q0:q0 + P], start=False, stop=False)
                            if nq > P:
                                ins = pe.matmul(dst[:, i, P:nq], cb("rowsB1", P, at=s * P), mrow[:, g % 2, q0 + P:q0 + nq], start=False, stop=False)
                        else:
                            ins = pe.matmul(dst[:, i, 0:nq], cb("rowsB0", P, at=s * P), mrow[:, g % 2, q0:q0 + nq], start=False, stop=(a == FULL))
                        if a != FULL:
                            mask, n = ("bandB", nq) if a == BANDED else ("maskB", P)
                            ins = pe.matmul(dst[:, i, 0:n], cb("ident", P), cb(mask, n), start=False, stop=True)
                    ins.then_inc(*ends_fill(name))

                def values(a, g, kt):
                    n = UNITS * a + NT * g + kt
                    o = a * GROUPS + g
                    q0, nq = width(a, kt)
                    if kt == 0:
                        pe.wait_ge(out_drained, b * OUT_ITER + PAIRS + max(0, o - 1))
                    for u in range(2):
                        pe.wait_ge(*drained_by((a, "B", g, kt, u), b))
                    for s, h in enumerate(heads_of(g)):
                        ins = pe.matmul(obank[32 * s:32 * s + 32, (PAIRS + o) % 2, q0:q0 + nq], v_of[a][:, kt, h, :], e16[:, n % 4, s, 0:nq],
                                        start=(kt == 0), stop=(kt == NT - 1), skip_group_check=(a != FULL))
                    ins.then_inc(pv_done, 1)

                def attention(a):
                    for qt in range(NT):
                        for u in range(2):
                            pass_a(a, 0, qt, u)
                    pe.wait_ge(k_split, b * 3 + (3 if a == BANDED else 2))
                    if a == BANDED:
                        pe.wait_ge(*drained_by(("VS", 1), b))
                        pe.wait_ge(ones_ready, b * 2 + 2)
                    for g in range(GROUPS):
                        name = (a, "T", g)
                        dst = start(name)
                        pe.wait_ge(mcol_ready, b * 12 + a * GROUPS + g + 1)
                        m = mcol_s[:, g, :, :] if a == BANDED else mcol[:, g % 2, :, :]
                        turned = dst[:, 0, 0:256].bitcast(BF16)
                        for t in range(NT):
                            ins = pe.transpose(turned[:, t * P:(t + 1) * P], m[:, t, :], cb("ident", P))
                        ins.then_inc(*ends_fill(name))
                        for kt in range(NT):
                            if g >= 1:
                                values(a, g - 1, kt)
                            for u in range(2):
                                if kt == 0 and u == 0:
                                    pe.wait_ge(*drained_by(name, b))
                                pass_b(a, g, kt, u)
                                if g + 1 < GROUPS:
                                    pass_a(a, g + 1, kt, u)
                    for kt in range(NT):
                        values(a, GROUPS - 1, kt)
                    pe.wait_ge(out_drained, b * OUT_ITER + PAIRS + (a + 1) * GROUPS)

                attention(CAUSAL)
                out_project("O2", w_out[CAUSAL], oT, GROUPS)

                pe.wait_ge(k_loaded["ls"], 64)
                pe.wait_ge(norm_ready, b * 5 + 2)
                turn(2, nat_n)
                pe.wait_ge(*drained_by(("X", 2), b))
                project(("QS",), w_sq["sq"], act_t, range(DT))
                project(("KS",), w_sq["sk"], act_t, range(DT))
                project_nat("VS", w_sq["sv"], act_t)
                pe.wait_ge(*drained_by(("KS",), b))
                attention(BANDED)
                out_project("OS", w_out[BANDED], oT, GROUPS)
                pe.wait_ge(norm_ready, b * 5 + 3)
                turn(3, nat_n)
                pe.wait_ge(*drained_by(("X", 3), b))
                project(("QC",), w_sq["cq"], act_t, range(DT))
                attention(FULL)
                out_project("OC", w_out[FULL], oT, GROUPS)
                pe.wait_ge(norm_ready, b * 5 + 4)
                turn(4, nat_n)
                pe.wait_ge(*drained_by(("X", 4), b))
                pe.wait_ge(k_loaded["ff"], b * 32 + 32)
                for j in range(FT // 2):
                    project(("F1", j), w_f1, act_t, (2 * j, 2 * j + 1))
                for j in range(FT // 2):
                    pe.wait_ge(*drained_by(("F1", j), b))
                out_project("F2", w_f2, hid, FT)
                while order[0] < len(JOBS):
                    name = JOBS[order[0]]
                    start(name)
                    pe.nop().then_inc(*ends_fill(name))
                    pe.nop().then_inc(*ends_drain(name))


def padded(w, bias, a):
    import numpy as np
    out = np.zeros((GROUPS, 4, 32, D), np.float32)
    for g in range(GROUPS):
        for s, h in enumerate(heads_of(g)):
            out[g, s, 0:DH] = w[h * DH:(h + 1) * DH]
    out[0, 0, DH] = bias
    return out.reshape(GROUPS * P, D)


def constants():
    import numpy as np
    c = np.zeros((P, NCONST), np.float32)

    def put(name, table, at=0):
        c[:, CST[name] + at:CST[name] + at + table.shape[1]] = table

    p = np.arange(P)[:, None]
    x = np.arange(P)[None, :]
    y = np.arange(BAND)[None, :]
    put("ident", (p == x).astype(np.float32))
    put("tri", (p <= x).astype(np.float32))
    put("maskA", np.where(x > p, NEG, 0.0))
    put("maskB", np.where(p > x, NEG, 0.0))
    ahead = y - W - p
    put("bandA", np.where((ahead <= 0) & (ahead > -W), 0.0, NEG))
    behind = y - p
    put("bandB", np.where((behind >= 0) & (behind < W), 0.0, NEG))
    slopes = (2.0 ** (-8.0 * np.arange(1, H + 1, dtype=np.float32) / H)).astype(np.float32)
    parts, rest = [], slopes.copy()
    for _ in range(3):
        hi = (rest.view(np.uint32) & np.uint32(0xFFFF0000)).view(np.float32)
        parts.append(hi)
        rest = (rest - hi).astype(np.float32)
    for s in range(4):
        b0, b1, jrow = np.zeros((4, 32, P)), np.zeros((4, 32, P)), np.zeros((4, 32, BAND))
        b0[s, 0:2] = b1[s, 0:2] = 1.0
        b0[s, 2:5] = x
        b1[s, 2:5] = x - P
        jrow[s, 0:3] = y - W
        put("rowsB0", b0.reshape(P, P), s * P)
        put("rowsB1", b1.reshape(P, P), s * P)
        put("rowsJ", jrow.reshape(P, BAND), s * BAND)
    for g in range(GROUPS):
        sa = np.zeros((4, 32, P))
        sm = np.zeros((P, 4, 32))
        for s, h in enumerate(heads_of(g)):
            for i in range(3):
                sa[s, i] = parts[i][h]
                sm[:, s, 2 + i] = parts[i][h]
        put("slopeA", sa.reshape(P, P), g * P)
        put("slopeM", sm.reshape(P, P), g * P)
    put("hmask", (p // DH == np.arange(8)).astype(np.float32))
    put("half", (p // DK0 == np.arange(2)).astype(np.float32))
    return c


def arrange(i):
    import numpy as np
    f = {k: np.asarray(v) for k, v in i.items()}
    c = np.ascontiguousarray
    a = {
        "xT": c(f["x"].transpose(0, 2, 1)), "ctxT": c(f["ctx_1024"].transpose(0, 2, 1)), "x": c(f["x"]),
        "mask": c(f["mask_BxS2_ik0"]),
        "wq0": c(f["L0_xattn_W_Q"].T), "wk0": c(f["L0_xattn_W_K"].T), "wv0": c(f["L0_xattn_W_V"].T), "wo0": c(f["L0_xattn_W_O"].T),
        "w1_t": c(f["L1_xattn_Wt"].T), "w1_v": c(f["L1_xattn_Wv"].T),
        "w1_gt": c(f["L1_xattn_Wg"][:, :D].T), "w1_gv": c(f["L1_xattn_Wg"][:, D:].T),
        "w_q2": c(f["L2_xattn_Wq"]), "w_k2": c(f["L2_xattn_Wk"]), "w_v2": c(f["L2_xattn_Wv"]), "w_om": c(f["L2_xattn_Wo"]),
        "w_f1": c(f["L3_xattn_w1"]), "w_f2": c(f["L3_xattn_w2"]),
        "w_out0": padded(f["L2_xattn_Wo"], f["L2_xattn_bo"], 0),
        "w_out1": padded(f["L3_xattn_swo"], f["L3_xattn_sbo"], 1),
        "w_out2": padded(f["L3_xattn_cwo"], f["L3_xattn_cbo"], 2),
        "consts": constants(),
    }
    for n in ("sq", "sk", "sv", "cq", "ck", "cv"):
        a["w_" + n] = c(f[f"L3_xattn_{n[0]}w{n[1]}"])
    col_of = {"bq0": "L0_xattn_b_Q", "bk0": "L0_xattn_b_K", "bt": "L1_xattn_bt", "bq2": "L2_xattn_bq", "bk2": "L2_xattn_bk",
              "sbq": "L3_xattn_sbq", "sbk": "L3_xattn_sbk", "cbq": "L3_xattn_cbq", "cbk": "L3_xattn_cbk", "b1": "L3_xattn_b1",
              "ga1": "L1_xattn_gamma", "be1": "L1_xattn_beta", "g1": "L3_xattn_g1", "b1n": "L3_xattn_be1",
              "g2": "L3_xattn_g2", "b2n": "L3_xattn_be2"}
    a["cols"] = c(np.concatenate([f[col_of[n]].reshape(k, P).T for n, k in COLS], axis=1))
    row_of = {"bv0": "L0_xattn_b_V", "bo0": "L0_xattn_b_O", "bv1": "L1_xattn_bv", "bg": "L1_xattn_bg", "ga1": "L1_xattn_gamma",
              "be1": "L1_xattn_beta", "bv2": "L2_xattn_bv", "bo2": "L2_xattn_bo", "sbv": "L3_xattn_sbv", "cbv": "L3_xattn_cbv",
              "b2": "L3_xattn_b2", "g1": "L3_xattn_g1", "b1n": "L3_xattn_be1", "g2": "L3_xattn_g2", "b2n": "L3_xattn_be2",
              "g3": "L3_xattn_g3", "b3n": "L3_xattn_be3"}
    a["rows"] = c(np.concatenate([f[row_of[n]].reshape(k, D) for n, k in ROWS], axis=0))
    return a


def kernel(**inputs):
    import numpy as _np
    import concourse.bacc as _bacc
    from concourse import mybir as _mybir
    from concourse.bass_utils import run_bass_kernel_spmd as _run

    nc = _bacc.Bacc("TRN2", target_bir_lowering=False, num_devices=1)
    arrays = arrange(inputs)
    io = {n: nc.dram_tensor("in_" + n, a.shape, _mybir.dt.from_np(a.dtype), kind="ExternalInput").ap() for n, a in arrays.items()}
    out = nc.dram_tensor("out", (B, S, D), F32, kind="ExternalOutput").ap()
    build(nc, io, out)
    r = _run(nc, [{"in_" + n: a for n, a in arrays.items()}], core_ids=[0])
    return r.results[0]["out"]
```

```python
from contextlib import ExitStack

import concourse.bass as bass
from concourse import mybir

ALU = mybir.AluOpType
ACT = mybir.ActivationFunctionType
F32 = mybir.dt.float32
F32R = mybir.dt.float32r
BF16 = mybir.dt.bfloat16
I32 = mybir.dt.int32
AX = mybir.AxisListType

B, S, D = 4, 512, 256
P = 128
NT = S // P
DT = D // P
H = 16
DK0 = 64
HD0 = H * DK0
PAIRS = H // 2
DH = D // H
GROUPS = H // 4
FF = 1024
FT = FF // P
W = 64
BAND = P + W
NEG = -1.0e30
CAUSAL, BANDED, FULL = range(3)
SLOTS = 3
EXP_LN_TABLES = 6
TILES_RESET = 5
UNITS0 = PAIRS * NT
E0 = 7
UNITS = GROUPS * NT
PV_ITER = UNITS0 + 3 * UNITS
OUT_ITER = PAIRS + 3 * GROUPS

COLS = [("bq0", 8), ("bk0", 8), ("bt", 2), ("bq2", 2), ("bk2", 2), ("sbq", 2), ("sbk", 2), ("cbq", 2), ("cbk", 2),
        ("b1", 8), ("ga1", 2), ("be1", 2), ("g1", 2), ("b1n", 2), ("g2", 2), ("b2n", 2)]
ROWS = [("bv0", 4), ("bo0", 1), ("bv1", 1), ("bg", 1), ("ga1", 1), ("be1", 1), ("bv2", 1), ("bo2", 1), ("sbv", 1),
        ("cbv", 1), ("b2", 1), ("g1", 1), ("b1n", 1), ("g2", 1), ("b2n", 1), ("g3", 1), ("b3n", 1)]
CONSTS = [("ident", P), ("maskA", P), ("maskB", P), ("bandA", BAND), ("bandB", BAND),
          ("rowsJ", 4 * 2 * P), ("slopeA", 4 * P), ("tri", P),
          ("pair", 1), ("half", 2)]


def offsets(parts):
    at, out = 0, {}
    for name, n in parts:
        out[name] = at
        at += n
    return out, at


COL, NCOLS = offsets(COLS)
ROW, NROWS = offsets(ROWS)
CST, NCONST = offsets(CONSTS)
NBF = CST["tri"]


Q_JOB = {CAUSAL: ("Q2",), BANDED: ("QS",), FULL: ("QC",)}
K_JOB = {CAUSAL: ("K2",), BANDED: ("KS",), FULL: ("KC",)}


def heads_of(g):
    return [4 * g + s for s in range(4)]


def group_steps(g):
    steps = []
    ahead = [("A", g + 1, t, u) for t in range(NT) for u in range(2)] if g + 1 < GROUPS else []
    if g == 0:
        steps += [("T", 0)] + ahead[:2]
        ahead = ahead[2:]
    for kt in range(NT):
        if g >= 1 and kt < 2:
            steps += [("V", g - 1, 2 * kt), ("V", g - 1, 2 * kt + 1)]
        for u in range(2):
            if g + 1 < GROUPS and (kt, u) == (NT - 1, 1):
                steps.append(("T", g + 1))
            steps.append(("B", g, kt, u))
            steps += ahead[:2]
            ahead = ahead[2:]
    return steps


def attention_jobs(a):
    jobs = [(a, "A", 0, qt, u) for qt in range(NT) for u in range(2)]
    for g in range(GROUPS):
        jobs += [(a,) + step for step in group_steps(g) if step[0] != "V"]
    return jobs


def plan_jobs():
    jobs = [("V0", t) for t in range(NT)] + [("QK0", 0)]
    for p in range(PAIRS):
        jobs += [("S0", p, kt) for kt in range(NT)]
        if p + 1 < PAIRS:
            jobs.insert(-2, ("QK0", p + 1))
    jobs += [("O0", j) for j in range(2)]
    jobs += [("vp",), ("vpT",), ("X", 0), ("K2",), ("uv",), ("tp",), ("ksum",), ("agree",)] + [("gate", j) for j in range(2)]
    jobs += [("rcol",)] + [("V2", j) for j in range(2)] + [("cnt",), ("X", 1), ("Q2",), ("meanV",), ("meanO",)]
    jobs += [("VC", j) for j in range(2)]
    jobs += attention_jobs(CAUSAL) + [("O2", j) for j in range(2)] + [("X", 2), ("KS",), ("QS",)] + [("VS", j) for j in range(2)]
    jobs += attention_jobs(BANDED) + [("KC",)] + [("OS", j) for j in range(2)] + [("X", 3), ("QC",)]
    jobs += attention_jobs(FULL) + [("OC", j) for j in range(2)] + [("X", 4)]
    jobs += [("F1", j) for j in range(FT // 2)] + [("F2", j) for j in range(2)]
    while len(jobs) % SLOTS:
        jobs.append(("pad", len(jobs)))
    return jobs


JOBS = plan_jobs()
JOB = {name: n for n, name in enumerate(JOBS)}
ROUNDS = len(JOBS) // SLOTS

DVE_LINKS = 92
ACT_LINKS = 5
POOL_LINKS = 4
HOLDS = UNITS0 + 5 + 3 * GROUPS


def build(nc, io, out):
    with ExitStack() as ctx:
        def sb(name, shape, dt=F32):
            return ctx.enter_context(nc.sbuf_tensor(name, shape, dt))

        def sem(name):
            return ctx.enter_context(nc.semaphore(name))

        ring = ctx.enter_context(nc.psum_tensor("ring", [P, SLOTS, 2, 512], F32))
        obank = ctx.enter_context(nc.psum_tensor("obank", [P, 2, 512], F32))

        def overlay(name, at, shape, dt=F32R):
            return nc.alloc_sbuf_tensor_at(name, shape, dt, offset=at)

        def next_offset():
            return (nc.sbuf_base + 31) // 32 * 32

        at_qk = next_offset()
        wqk0 = sb("wqk0", [P, 2, DT, HD0])
        wq0, wk0 = wqk0[:, 0, :, :], wqk0[:, 1, :, :]
        q_tiles_a = overlay("q_tiles_a", at_qk, [P, 2, 4, S])
        at_vo = next_offset()
        wvo = sb("wvo", [P, 2048])
        q_tiles_b = overlay("q_tiles_b", at_vo, [P, 4, S])
        q_tiles = [q_tiles_a[:, 0, :, :], q_tiles_a[:, 1, :, :], q_tiles_b[:, :, :]]
        wv0 = wvo[:, :].rearrange("p (t n) -> p t n", t=DT)
        wo0 = wvo[:, :].rearrange("p (t n) -> p t n", t=HD0 // P)
        w_l1 = {n: sb("w1_" + n, [P, DT, D]) for n in ("t", "v", "gt", "gv")}
        w_sq = {n: sb("w_" + n, [P, DT, D]) for n in ("q2", "k2", "v2", "sq", "sk", "sv", "cq", "ck", "cv")}
        w_out = {a: sb(f"w_out{a}", [P, GROUPS, D]) for a in (CAUSAL, BANDED, FULL)}
        cols = sb("cols", [P, NCOLS])
        rows = sb("rows", [P, NROWS, D])
        ident = sb("ident", [P, P])
        tri = sb("tri", [P, P])
        pair = sb("pair", [P, 3])
        ones = sb("ones", [P, P])
        cbf = sb("cbf", [P, NBF], BF16)
        kcol = sb("kcol", [P, 3, DT])
        kcol0 = sb("kcol0", [P, 2, PAIRS])
        qcol = sb("qcol", [P, 8])
        epsc = sb("epsc", [P, 1])
        zero = sb("zero", [P, 1])

        act_t = sb("act_t", [P, DT, S])
        ctx_t = sb("ctx_t", [P, DT, S])
        at_e = next_offset()
        region_e = sb("region_e", [P, 8192])
        at_b = next_offset()
        region_b = sb("region_b", [P, 4096])
        at_c = next_offset()
        region_c = sb("region_c", [P, 4096])
        region_d = sb("region_d", [P, 2048])
        at_q = next_offset()
        region_q = sb("region_q", [P, 2048])
        e0 = region_e[:, 0:E0 * 1024].rearrange("p (u h q) -> p u h q", u=E0, h=2)
        k0_odd = region_e[:, E0 * 1024:8192].rearrange("p (u k) -> p u k", u=2)
        e16 = region_e[:, :].rearrange("p (u s q) -> p u s q", u=4, s=4)
        hid = region_e[:, 0:4096].rearrange("p (t q) -> p t q", t=FT)
        v0 = region_b[:, :].rearrange("p (t n) -> p t n", t=NT)
        w_f1 = region_b[:, 2048:4096].rearrange("p (t n) -> p t n", t=DT)
        w_f2 = region_b[:, 0:2048].rearrange("p (t n) -> p t n", t=FT)
        o0 = region_c[:, :].rearrange("p (t q) -> p t q", t=PAIRS)

        k_tiles_a = overlay("k_tiles_a", at_b, [P, 4, S])
        k_tiles_b = overlay("k_tiles_b", at_c, [P, 4, S])
        k_tiles = [(k_tiles_a if g < 2 else k_tiles_b)[:, 2 * (g % 2):2 * (g % 2) + 2, :] for g in range(GROUPS)]
        k_full = region_e[:, 0:1024].rearrange("p (t k) -> p t k", t=DT)
        q_full = region_e[:, 1024:2048].rearrange("p (t k) -> p t k", t=DT)
        k_parts = overlay("k_parts", at_e + 4 * 2048, [P, 2, DT, S])
        q_parts = overlay("q_parts", at_q, [P, 2, DT, S])
        v_b = region_b[:, 2048:4096].rearrange("p (t h c) -> p t h c", t=NT, h=H)
        v_c = region_c[:, 2048:4096].rearrange("p (t h c) -> p t h c", t=NT, h=H)
        v_of = {CAUSAL: v_b, BANDED: v_b, FULL: v_c}
        sm0 = region_d[:, :].rearrange("p (u h q) -> p u h q", u=2, h=2)
        v2 = region_d[:, 0:1024].rearrange("p (t n) -> p t n", t=NT)
        w_om = region_d[:, 1024:1536].rearrange("p (t n) -> p t n", t=DT)
        oT = region_d[:, :].rearrange("p (g q) -> p g q", g=GROUPS)
        qk0 = region_q[:, :].rearrange("p (u a q) -> p u a q", u=2, a=2)
        tp_t = region_q[:, 0:1024].rearrange("p (t q) -> p t q", t=DT)

        vs0 = sb("vs0", [P, 4, 2, DK0])
        rbuf = sb("rbuf", [P, S])
        mask_i = rbuf[:, :].bitcast(I32)
        maskb = sb("maskb", [P, S])
        nat_x = sb("nat_x", [P, NT, D])
        nat_y = sb("nat_y", [P, NT, D])
        x_nat = nat_y
        nat_n = sb("nat_n", [P, NT, D])
        mcol = sb("mcol", [P, 2, NT, P], BF16)
        nmin0 = sb("nmin0", [P, UNITS0, 2])
        sum0 = sb("sum0", [P, UNITS0, 2])
        rs0 = sb("rs0", [P, UNITS0, 2])
        nmax = sb("nmax", [P, NT, 4])
        nanfix = sb("nanfix", [P, 4])
        stats = sb("stats", [P, NT, 6])
        mv = sb("mv", [P, NT, 2])
        lnv = sb("lnv", [P, NT])
        std = sb("std", [P, NT])
        rstd = sb("rstd", [P, NT])
        std1 = sb("std1", [P, NT])
        pooled = sb("pooled", [P, DT])
        small = sb("small", [P, DT])
        held = sb("held", [P, HOLDS + SLOTS])
        rrow = rbuf
        one_sum = sb("one_sum", [1, 4])
        rcol = sb("rcol", [P, NT])
        vp_b = region_q[:, 1024:1024 + D]
        u_b = region_q[:, 1024 + D:1024 + 2 * D]
        wide = sb("wide", [P, DT, P])
        km = sb("km", [P, NT])
        degen = sb("degen", [P, NT])
        mean_o = sb("mean_o", [P, D])

        def col(name, t=0):
            return cols[:, COL[name] + t:COL[name] + t + 1]

        def row(name, n=1):
            return rows[:, ROW[name]:ROW[name] + n, :]

        def cb(name, n, part=slice(0, P), at=0):
            return cbf[part, CST[name] + at:CST[name] + at + n]

        filled = [sem(f"filled{s}") for s in range(SLOTS)]
        drained = [sem(f"drained{s}") for s in range(SLOTS)]
        pv_done = sem("pv_done")
        out_drained = sem("out_drained")
        exp0_done = sem("exp0_done")
        exp_done = sem("exp_done")
        vs_ready = sem("vs_ready")
        k_loaded = {n: sem("ld_" + n) for n in ("act", "ctx", "x", "mask", "wq0", "wk0", "wv0", "wo0", "ff", "small",
                                               "const", "l1", "om", "l2", "ls", "lc")}
        stored = sem("stored")
        setup_dve = sem("setup_dve")
        setup_act = sem("setup_act")
        setup_pool = sem("setup_pool")
        dve_link = sem("dve_link")
        act_link = sem("act_link")
        pool_link = sem("pool_link")
        mask_ready = sem("mask_ready")
        resid0_ready = sem("resid0_ready")
        pooled_ready = sem("pooled_ready")
        wide_ready = sem("wide_ready")
        agree_max = sem("agree_max")
        agree_exp = sem("agree_exp")
        agree_inv = sem("agree_inv")
        gate_ready = sem("gate_ready")
        km_ready = sem("km_ready")
        vmask_ready = sem("vmask_ready")
        ones_ready = sem("ones_ready")
        k_split = sem("k_split")
        q_half = sem("q_half")
        q_full_ready = sem("q_full_ready")
        q_hi_ready = sem("q_hi_ready")
        q_stacked = [sem(f"q_stacked{g}") for g in range(GROUPS)]
        k_stacked = [sem(f"k_stacked{g}") for g in range(GROUPS)]
        tiles_reset = sem("tiles_reset")
        mcol_ready = sem("mcol_ready")
        heads_ready = sem("heads_ready")
        heads0_ready = sem("heads0_ready")
        var_ready = sem("var_ready")
        rstd_ready = sem("rstd_ready")
        norm_ready = sem("norm_ready")
        tile_normed = sem("tile_normed")
        resid_ready = sem("resid_ready")

        def slot(name):
            return ring[:, JOB[name] % SLOTS, :, :]

        def filled_by(name, b):
            return filled[JOB[name] % SLOTS], b * ROUNDS + JOB[name] // SLOTS + 1

        def drained_by(name, b):
            return drained[JOB[name] % SLOTS], b * ROUNDS + JOB[name] // SLOTS + 2

        def free_for(name, b):
            return drained[JOB[name] % SLOTS], b * ROUNDS + JOB[name] // SLOTS + 1

        def ends_fill(name):
            return filled[JOB[name] % SLOTS], 1

        def ends_drain(name):
            return drained[JOB[name] % SLOTS], 1

        def width(a, g_tile):
            if a == FULL:
                return 0, S
            if a == CAUSAL:
                return P * g_tile, S - P * g_tile
            return P * g_tile, min(BAND, S - P * g_tile)

        def seen(a, qt):
            if a == FULL:
                return 0, S
            if a == CAUSAL:
                return 0, P * (qt + 1)
            lo = max(0, P * qt - W)
            return lo, P * (qt + 1) - lo

        block = ctx.enter_context(nc.Block())

        @block.sync
        def _(sp):
            def load(dst, src, name):
                sp.dma_start(dst, src).then_inc(k_loaded[name], 16)

            def load_act(b):
                load(act_t[:, :, :], io["xT"][b].rearrange("(t p) s -> p t s", p=P), "act")

            def load_ctx(b):
                load(ctx_t[:, :, :], io["ctxT"][b].rearrange("(t p) s -> p t s", p=P), "ctx")

            def load_x(b):
                load(x_nat[:, :, :], io["x"][b].rearrange("(t p) d -> p t d", p=P), "x")

            def load_mask(b):
                load(mask_i, io["mask"][b:b + 1, :].broadcast_to([P, S]), "mask")

            def stack_k(a, b, g, strips):
                for strip, part in strips:
                    sp.dma_start(k_tiles[g][32 * strip:32 * strip + 32, :, :].bitcast(F32),
                                 k_parts[32 * g:32 * g + 32, part, :, :].bitcast(F32)).then_inc(k_stacked[g], 16)

            def stack_q(a, b, g, strips):
                tiles = q_tiles[g % 3].rearrange("p (t i) q -> p t i q", i=2)
                for strip, part in strips:
                    for i in range(2):
                        sp.dma_start(tiles[32 * strip + DH * i:32 * strip + DH * (i + 1), :, i, :].bitcast(F32),
                                     q_parts[32 * g + DH * i:32 * g + DH * (i + 1), part, :, :].bitcast(F32)).then_inc(q_stacked[g], 16)

            def stack(a, b):
                k_high, k_low, q_high, q_low = ((0, 0), (2, 0)), ((1, 1),), ((0, 0), (1, 0)), ((2, 1),)
                sp.wait_ge(*drained_by(K_JOB[a], b))
                if a == CAUSAL:
                    sp.wait_ge(tiles_reset, b * TILES_RESET + TILES_RESET)
                else:
                    sp.wait_ge(*filled_by((a - 1, "B", GROUPS - 1, NT - 1, 1), b))
                if a != BANDED:
                    sp.wait_ge(k_split, b * 3 + a + 1)
                    for g in range(GROUPS):
                        stack_k(a, b, g, k_high + k_low)
                    sp.wait_ge(q_hi_ready, (b * 3 + a + 1) * DT)
                    stack_q(a, b, 0, q_high)
                else:
                    stack_k(a, b, 0, k_high)
                    sp.wait_ge(q_hi_ready, (b * 3 + a + 1) * DT)
                    stack_q(a, b, 0, q_high)
                    sp.wait_ge(k_split, b * 3 + a + 1)
                    stack_k(a, b, 0, k_low)
                sp.wait_ge(*drained_by(Q_JOB[a], b))
                stack_q(a, b, 0, q_low)
                for g in range(1, GROUPS):
                    if a == BANDED:
                        stack_k(a, b, g, k_high + k_low)
                    if g == 3:
                        sp.wait_ge(*filled_by((a, "B", 0, NT - 1, 1), b))
                    stack_q(a, b, g, q_high + q_low)

            load_ctx(0)
            load(wv0, io["wv0"].rearrange("(t p) n -> p t n", p=P), "wv0")
            load_act(0)
            load(wq0, io["wq0"].rearrange("(t p) n -> p t n", p=P), "wq0")
            load(wk0, io["wk0"].rearrange("(t p) n -> p t n", p=P), "wk0")
            load_mask(0)
            load_x(0)
            for n in ("t", "v", "gt", "gv"):
                load(w_l1[n][:, :, :], io["w1_" + n].rearrange("(t p) n -> p t n", p=P), "l1")
            for names, a, s in ((("q2", "k2", "v2"), CAUSAL, "l2"), (("sq", "sk", "sv"), BANDED, "ls"),
                                (("cq", "ck", "cv"), FULL, "lc")):
                for n in names:
                    load(w_sq[n][:, :, :], io["w_" + n].rearrange("(t p) n -> p t n", p=P), s)
                load(w_out[a][:, :, :], io[f"w_out{a}"].rearrange("(g p) n -> p g n", p=P), s)
            for b in range(B):
                for t in range(NT):
                    sp.wait_ge(*filled_by(("V0", t), b))
                if b:
                    sp.wait_ge(stored, b * 16)
                load(wo0, io["wo0"].rearrange("(t p) n -> p t n", p=P), "wo0")
                sp.wait_ge(exp0_done, (b + 1) * UNITS0)
                load(w_om, io["w_om"].rearrange("(t p) n -> p t n", p=P), "om")
                for a in (CAUSAL, BANDED):
                    stack(a, b)
                sp.wait_ge(pv_done, b * PV_ITER + UNITS0 + 2 * UNITS)
                load(w_f1, io["w_f1"].rearrange("(t p) n -> p t n", p=P), "ff")
                if b + 1 < B:
                    sp.wait_ge(*filled_by(("KC",), b))
                    sp.wait_ge(*filled_by(("VC", 0), b))
                    sp.wait_ge(*filled_by(("VC", 1), b))
                    sp.wait_ge(pooled_ready, b + 1)
                    load_ctx(b + 1)
                stack(FULL, b)
                sp.wait_ge(*filled_by((FULL, "B", GROUPS - 1, NT - 1, 1), b))
                load(w_f2, io["w_f2"].rearrange("(t p) n -> p t n", p=P), "ff")
                if b + 1 < B:
                    load(wv0, io["wv0"].rearrange("(t p) n -> p t n", p=P), "wv0")
                    load(wq0, io["wq0"].rearrange("(t p) n -> p t n", p=P), "wq0")
                    load(wk0, io["wk0"].rearrange("(t p) n -> p t n", p=P), "wk0")
                    sp.wait_ge(out_drained, (b + 1) * OUT_ITER)
                    load_mask(b + 1)
                    for j in range(FT // 2):
                        sp.wait_ge(*filled_by(("F1", j), b))
                    load_act(b + 1)
                    sp.wait_ge(norm_ready, (b + 1) * 5)
                    load_x(b + 1)
                sp.wait_ge(resid_ready, (b + 1) * 4)
                sp.dma_start(out[b].rearrange("(t p) d -> p t d", p=P), nat_x[:, :, :]).then_inc(stored, 16)
            sp.wait_ge(stored, B * 16)

        @block.gpsimd
        def _(pool):
            pool.memset(ones[:, :], 1.0).then_inc(setup_pool, 1)
            pool.memset(mcol[:, :, :, :], 0.0).then_inc(setup_pool, 1)
            pool.memset(epsc[:, :], 1e-5).then_inc(setup_pool, 1)
            pool.memset(zero[:, :], 0.0).then_inc(setup_pool, 1)
            for s in range(SLOTS):
                pool.memset(held[:, HOLDS + s:HOLDS + s + 1], 0.0).then_inc(drained[s], 1)
            pool.wait_ge(k_loaded["small"], 32)
            pool.tensor_tensor(row("b2n"), row("b2n"), row("b2"), ALU.add).then_inc(setup_pool, 1)
            pool.wait_ge(setup_pool, 5)

            def wide_row(name):
                return row(name).broadcast_to([P, NT, D])

            with pool.Fori(0, B) as b:
                links = [0]

                def link(ins):
                    links[0] += 1
                    ins.then_inc(pool_link, 1)
                    pool.wait_ge(pool_link, b * POOL_LINKS + links[0])

                def put_ones(v):
                    one = ones[:, 0:NT * H].rearrange("p (t h) -> p t h", t=NT).unsqueeze(3).broadcast_to([P, NT, H, DH])
                    pool.tensor_tensor(v[:, :, :, DH:2 * DH], one, one, ALU.mult).then_inc(ones_ready, 1)

                def split_k(a):
                    pool.wait_ge(*drained_by(K_JOB[a], b))
                    pool.tensor_tensor(k_parts[:, 1, :, :], k_full, k_parts[:, 0, :, :], ALU.subtract).then_inc(k_split, 1)

                def reset_tiles():
                    pool.wait_ge(*filled_by(("S0", PAIRS - 1, NT - 1), b))
                    zeros = zero[:, 0:1].unsqueeze(2).broadcast_to([P, 4, S])
                    for h in range(2):
                        pool.tensor_tensor(q_tiles[h], zeros, zeros, ALU.mult).then_inc(tiles_reset, 1)
                    pool.wait_ge(pv_done, b * PV_ITER + UNITS0)
                    for j in range(2):
                        pool.wait_ge(*filled_by(("O0", j), b))
                    pool.tensor_tensor(q_tiles[2], zeros, zeros, ALU.mult).then_inc(tiles_reset, 1)
                    for tiles in (k_tiles_a, k_tiles_b):
                        one = pair[:, 0:1].unsqueeze(2).broadcast_to([P, 4, S])
                        pool.tensor_tensor(tiles[:, :, :], one, one, ALU.mult).then_inc(tiles_reset, 1)

                pool.wait_ge(k_loaded["x"], b * 16 + 16)
                pool.tensor_tensor(x_nat[:, :, :], x_nat[:, :, :], wide_row("bo0"), ALU.add).then_inc(resid0_ready, 1)

                reset_tiles()
                split_k(CAUSAL)
                def residual(n, gamma, beta):
                    pool.wait_ge(norm_ready, b * 5 + n + 1)
                    link(pool.tensor_tensor(nat_x[:, :, :], nat_n[:, :, :], wide_row(gamma), ALU.mult))
                    pool.tensor_tensor(nat_x[:, :, :], nat_x[:, :, :], wide_row(beta), ALU.add).then_inc(resid_ready, 1)

                residual(0, "ga1", "be1")
                pool.wait_ge(*filled_by(("VC", 0), b))
                put_ones(v_of[FULL])
                split_k(BANDED)
                pool.wait_ge(*filled_by(("VS", 0), b))
                put_ones(v_of[BANDED])
                split_k(FULL)
                residual(2, "g1", "b1n")
                residual(3, "g2", "b2n")
                residual(4, "g3", "b3n")
                assert links[0] == POOL_LINKS, links

        @block.scalar
        def _(act):
            def load_exp_ln():
                act.add_instruction(mybir.InstLoadActFuncSet(name=nc.get_next_instruction_name(), engine=mybir.EngineType.Activation,
                                                             ins=[], outs=[], act_func_set_id=EXP_LN_TABLES))

            load_exp_ln()
            act.dma_start(rows[:, :, :], io["rows"].rearrange("(a n) d -> a n d", a=1).broadcast_to([P, NROWS, D]))\
                .then_inc(k_loaded["small"], 16)
            act.dma_start(cols[:, :], io["cols"]).then_inc(k_loaded["small"], 16)
            act.dma_start(region_e[:, 0:NCONST], io["consts"]).then_inc(k_loaded["const"], 16)
            act.wait_ge(k_loaded["small"], 32)
            act.activation(qcol[:, :], cols[:, COL["bq0"]:COL["bq0"] + 8], ACT.Copy, scale=DK0 ** -0.5).then_inc(setup_act, 1)
            act.wait_ge(setup_dve, 3)
            for i, name in enumerate(("bk2", "sbk", "cbk")):
                act.activation(kcol[:, i, :], cols[:, COL[name]:COL[name] + DT], ACT.Copy, scale=DH ** -0.5).then_inc(setup_act, 1)
            for h in range(2):
                act.activation(kcol0[:, h, :], cols[:, COL["bk0"]:COL["bk0"] + PAIRS], ACT.Copy,
                               scale=pair[:, 1 + h:2 + h]).then_inc(setup_act, 1)
            act.wait_ge(setup_act, 6)
            act.wait_ge(setup_dve, 4)
            act.wait_ge(setup_pool, 5)

            with act.Fori(0, B) as b:
                links = [0]

                def link(ins):
                    links[0] += 1
                    ins.then_inc(act_link, 1)
                    act.wait_ge(act_link, b * ACT_LINKS + links[0])

                def drain_qk(p):
                    act.wait_ge(*filled_by(("QK0", p), b))
                    src = slot(("QK0", p))
                    act.activation(qk0[:, p % 2, 0, :], src[:, 0, :], ACT.Identity, bias=qcol[:, p:p + 1], scale=DK0 ** -0.5)
                    for h, dst in enumerate((qk0[:, p % 2, 1, :], k0_odd[:, p % 2, :])):
                        ins = act.activation(dst, src[:, 1, :], ACT.Identity, bias=kcol0[:, h, p:p + 1], scale=pair[:, 1 + h:2 + h])
                    ins.then_inc(*ends_drain(("QK0", p)))

                drain_qk(0)
                for p in range(PAIRS):
                    for kt in range(NT):
                        n = NT * p + kt
                        act.wait_ge(*drained_by(("S0", p, kt), b))
                        if n >= E0:
                            act.wait_ge(pv_done, b * PV_ITER + n - E0 + 1)
                        for h in range(2):
                            ins = act.activation(e0[:, n % E0, h, :], sm0[:, n % 2, h, :], ACT.Exp, bias=nmin0[:, n, h:h + 1],
                                                 scale=-1.0, accum_out=sum0[:, n, h:h + 1])
                        ins.then_inc(exp0_done, 1)
                        if kt == 1 and p + 1 < PAIRS:
                            drain_qk(p + 1)

                act.wait_ge(*filled_by(("vpT",), b))
                act.activation(wide[:, :, :], slot(("vpT",))[:, 0, 0:D].rearrange("p (t n) -> p t n", t=DT), ACT.Copy)\
                    .then_inc(*ends_drain(("vpT",)))

                def drain_k(name, a, i, func):
                    act.wait_ge(*filled_by(name, b))
                    for dst in (k_parts[:, 0, :, :], k_full):
                        for t in range(DT):
                            ins = act.activation(dst[:, t, :], slot(name)[:, t, :], func, bias=kcol[:, i, t:t + 1], scale=DH ** -0.5)
                    ins.then_inc(*ends_drain(name))

                def high_q(n):
                    for t in range(DT):
                        act.wait_ge(q_full_ready, (b * 3 + n) * DT + t + 1)
                        act.activation(q_parts[:, 0, t, :], q_full[:, t, :], ACT.Copy).then_inc(q_hi_ready, 1)

                def drain_x(n, gamma=None, beta=None):
                    act.wait_ge(*filled_by(("X", n), b))
                    src = slot(("X", n))
                    if gamma is None:
                        act.activation(act_t[:, :, :], src, ACT.Copy).then_inc(*ends_drain(("X", n)))
                        return
                    for t in range(DT):
                        ins = act.activation(act_t[:, t, :], src[:, t, :], ACT.Identity, bias=col(beta, t), scale=col(gamma, t))
                    ins.then_inc(*ends_drain(("X", n)))

                def rsqrt(n, sign, scale=1.0, eps=True):
                    act.wait_ge(var_ready, b * 5 + n + 1)
                    if eps:
                        link(act.activation(lnv[:, :], mv[:, :, 1], ACT.Ln, bias=epsc[:, 0:1]))
                    else:
                        link(act.activation(lnv[:, :], std1[:, :], ACT.Ln, scale=scale))
                    act.activation(std[:, :], lnv[:, :], ACT.Exp, scale=0.5 * sign).then_inc(rstd_ready, 1)

                drain_x(0)
                drain_k(("K2",), CAUSAL, 0, ACT.Relu)
                act.wait_ge(*filled_by(("tp",), b))
                for t in range(DT):
                    ins = act.activation(tp_t[:, t, :], slot(("tp",))[:, t, :], ACT.Identity, bias=col("bt", t))
                ins.then_inc(*ends_drain(("tp",)))
                act.wait_ge(agree_max, b + 1)
                act.activation(rrow[0:1, :], slot(("agree",))[0:1, 0, :], ACT.Exp, bias=one_sum[0:1, 1:2], scale=2.0,
                               accum_out=one_sum[0:1, 2:3]).then_inc(*ends_drain(("agree",)))
                for j in range(2):
                    act.wait_ge(*drained_by(("gate", j), b))
                    part = nat_n[:, 2 * j:2 * j + 2, :]
                    act.activation(part, part, ACT.Sigmoid).then_inc(gate_ready, 1)
                load_exp_ln()
                rsqrt(0, -1)
                drain_x(1, "ga1", "be1")

                def maxima_rows(a, g):
                    act.wait_ge(*filled_by((a, "T", g), b))
                    act.wait_ge(q_stacked[g], (b * 3 + a + 1) * 96)
                    turned = slot((a, "T", g))[:, 0, 0:256].bitcast(BF16)
                    for s in range(4):
                        ins = act.activation(q_tiles[g % 3][3 * 32:P, s, :], turned[32 * s:32 * s + 32, :], ACT.Copy)
                    ins.then_inc(*ends_drain((a, "T", g)))

                def exponentials(a, g, kt, u):
                    n = UNITS * a + NT * g + kt
                    _, nq = width(a, kt)
                    act.wait_ge(*filled_by((a, "B", g, kt, u), b))
                    act.wait_ge(pv_done, b * PV_ITER + UNITS0 + max(0, n - 3))
                    act.activation(e16[:, n % 4, 2 * u:2 * u + 2, 0:nq], slot((a, "B", g, kt, u))[:, :, 0:nq], ACT.Exp)\
                        .then_inc(*ends_drain((a, "B", g, kt, u)))

                def attention(a):
                    for g in range(GROUPS):
                        for kind, *which in group_steps(g):
                            if kind == "T":
                                maxima_rows(a, *which)
                            if kind == "B":
                                if g == 0 and which == [0, 0, 0]:
                                    for k in range(1, GROUPS):
                                        act.wait_ge(k_stacked[k], (b * 3 + a + 1) * 48)
                                exponentials(a, *which)

                high_q(0)
                attention(CAUSAL)
                rsqrt(1, +1, scale=D / (D - 1), eps=False)
                drain_x(2)
                drain_k(("KS",), BANDED, 1, ACT.Identity)
                high_q(1)
                attention(BANDED)
                drain_k(("KC",), FULL, 2, ACT.Identity)
                rsqrt(2, -1)
                drain_x(3, "g1", "b1n")
                high_q(2)
                attention(FULL)
                rsqrt(3, -1)
                drain_x(4, "g2", "b2n")
                for j in range(FT // 2):
                    act.wait_ge(*filled_by(("F1", j), b))
                    for i in range(2):
                        ins = act.activation(hid[:, 2 * j + i, :], slot(("F1", j))[:, i, :], ACT.Gelu, bias=col("b1", 2 * j + i))
                    ins.then_inc(*ends_drain(("F1", j)))
                load_exp_ln()
                rsqrt(4, -1)
                assert links[0] == ACT_LINKS, links

        @block.vector
        def _(dve):
            dve.wait_ge(k_loaded["const"], 16)
            c = region_e
            dve.tensor_copy(cbf[:, :], c[:, 0:NBF]).then_inc(setup_dve, 1)
            dve.tensor_copy(ident[:, :], c[:, CST["ident"]:CST["ident"] + P]).then_inc(setup_dve, 1)
            dve.tensor_copy(pair[:, :], c[:, CST["pair"]:CST["pair"] + 3]).then_inc(setup_dve, 1)
            dve.tensor_copy(tri[:, :], c[:, CST["tri"]:CST["tri"] + P]).then_inc(setup_dve, 1)
            dve.wait_ge(setup_dve, 4)
            dve.wait_ge(setup_pool, 5)
            dve.wait_ge(setup_act, 6)

            with dve.Fori(0, B) as b:
                links = [0]

                def link(ins):
                    links[0] += 1
                    ins.then_inc(dve_link, 1)
                    dve.wait_ge(dve_link, b * DVE_LINKS + links[0])

                holds = [0]

                def hold():
                    dve.memset(held[0:1, holds[0]:holds[0] + 1], 0.0)
                    holds[0] += 1

                dve.wait_ge(k_loaded["mask"], b * 16 + 16)
                link(dve.tensor_scalar(maskb[:, :], mask_i, 0.0, NEG, ALU.is_equal, ALU.mult))
                link(dve.tensor_reduce(nanfix[:, 0:1], maskb[:, :], AX.X, ALU.max))
                link(dve.tensor_scalar(nanfix[:, 1:2], nanfix[:, 0:1], 0.0, None, ALU.is_equal))
                link(dve.reciprocal(nanfix[:, 2:3], nanfix[:, 1:2]))
                link(dve.tensor_scalar(nanfix[:, 3:4], nanfix[:, 2:3], 0.0, None, ALU.mult))

                for t in range(NT):
                    dve.wait_ge(*filled_by(("V0", t), b))
                    dve.tensor_tensor(v0[:, t, :], slot(("V0", t)).rearrange("p a n -> p (a n)"),
                                      row("bv0", 4).rearrange("p a n -> p (a n)"), ALU.add).then_inc(*ends_drain(("V0", t)))
                dve.wait_ge(*drained_by(("V0", NT - 1), b))
                dve.wait_ge(k_loaded["ctx"], b * 16 + 16)
                link(dve.tensor_reduce(small[:, 0:2], ctx_t[:, :, :], AX.X, ALU.add))
                dve.tensor_scalar(pooled[:, :], small[:, 0:2], 1.0 / S, None, ALU.mult).then_inc(pooled_ready, 1)
                dve.wait_ge(pooled_ready, b + 1)
                dve.tensor_copy(wide[:, :, :], pooled[:, :].unsqueeze(2).broadcast_to([P, DT, P])).then_inc(wide_ready, 1)

                def scale_v(n):
                    p, kt = n // NT, n % NT
                    dve.wait_ge(exp0_done, b * UNITS0 + n + 1)
                    link(dve.reciprocal(rs0[:, n, :], sum0[:, n, :]))
                    if n >= 4:
                        dve.wait_ge(pv_done, b * PV_ITER + n - 3)
                    dve.tensor_tensor(vs0[:, n % 4, :, :], v0[:, kt, 2 * DK0 * p:2 * DK0 * (p + 1)].rearrange("p (h c) -> p h c", h=2),
                                      rs0[:, n, :].unsqueeze(2).broadcast_to([P, 2, DK0]), ALU.mult).then_inc(vs_ready, 1)

                def drain_heads0(p):
                    dve.wait_ge(pv_done, b * PV_ITER + NT * (p + 1))
                    dve.tensor_copy(o0[:, p, :], obank[:, p % 2, :]).then_inc(out_drained, 1)

                for n in range(UNITS0):
                    p, kt = n // NT, n % NT
                    dve.wait_ge(*filled_by(("S0", p, kt), b))
                    if n >= 2:
                        dve.wait_ge(exp0_done, b * UNITS0 + n - 1)
                    hold()
                    for h in range(2):
                        ins = dve.tensor_tensor_reduce(out=sm0[:, n % 2, h, :], in0=slot(("S0", p, kt))[:, h, :], in1=maskb[:, :],
                                                       scale=-1.0, scalar=3.0e38, op0=ALU.add, op1=ALU.min,
                                                       accum_out=nmin0[:, n, h:h + 1])
                    ins.then_inc(*ends_drain(("S0", p, kt)))
                    if n >= 1:
                        scale_v(n - 1)
                    if kt == 2 and p >= 2:
                        drain_heads0(p - 2)
                scale_v(UNITS0 - 1)
                drain_heads0(PAIRS - 2)
                drain_heads0(PAIRS - 1)

                dve.wait_ge(resid0_ready, b + 1)
                for j in range(2):
                    dve.wait_ge(*filled_by(("O0", j), b))
                    dve.scalar_tensor_tensor(out=nat_x[:, 2 * j:2 * j + 2, :], in0=slot(("O0", j))[:, :, 0:D], scalar=nanfix[:, 3:4],
                                             in1=x_nat[:, 2 * j:2 * j + 2, :], op0=ALU.add, op1=ALU.add)\
                        .then_inc(*ends_drain(("O0", j)))

                dve.wait_ge(*filled_by(("vp",), b))
                dve.tensor_tensor(vp_b[:, :], slot(("vp",))[:, 0, 0:D], row("bv1").squeeze(1), ALU.add).then_inc(*ends_drain(("vp",)))

                def drain_v(name, bias, dst):
                    for j in range(2):
                        dve.wait_ge(*filled_by((name, j), b))
                        for i in range(2):
                            ins = dve.tensor_tensor(dst(2 * j + i), slot((name, j))[:, i, 0:D].rearrange("p (h c) -> p h c", h=H),
                                                    row(bias).squeeze(1).rearrange("p (h c) -> p h c", h=H), ALU.add)
                        ins.then_inc(*ends_drain((name, j)))

                dve.wait_ge(*filled_by(("uv",), b))
                dve.tensor_copy(u_b[:, :], slot(("uv",))[:, 0, 0:D]).then_inc(*ends_drain(("uv",)))
                dve.wait_ge(*filled_by(("ksum",), b))
                dve.tensor_scalar(km[:, :], slot(("ksum",))[:, 0, 0:NT], 0.0, None, ALU.is_gt).then_inc(*ends_drain(("ksum",)))
                dve.wait_ge(*filled_by(("agree",), b))
                link(dve.tensor_reduce(one_sum[0:1, 0:1], slot(("agree",))[0:1, 0, :], AX.X, ALU.max))
                dve.tensor_scalar(one_sum[0:1, 1:2], one_sum[0:1, 0:1], -2.0, None, ALU.mult).then_inc(agree_max, 1)
                dve.wait_ge(*drained_by(("agree",), b))
                dve.reciprocal(one_sum[0:1, 3:4], one_sum[0:1, 2:3]).then_inc(agree_inv, 1)
                dve.wait_ge(*filled_by(("rcol",), b))
                dve.tensor_copy(rcol[:, :], slot(("rcol",))[:, 0, 0:NT]).then_inc(*ends_drain(("rcol",)))
                dve.wait_ge(*drained_by(("rcol",), b))
                for j in range(2):
                    dve.wait_ge(*filled_by(("gate", j), b))
                    for i in range(2):
                        t = 2 * j + i
                        ins = dve.scalar_tensor_tensor(out=nat_n[:, t, :], in0=u_b[:, :], scalar=rcol[:, t:t + 1],
                                                       in1=slot(("gate", j))[:, i, 0:D], op0=ALU.mult, op1=ALU.add)
                    ins.then_inc(*ends_drain(("gate", j)))
                drain_v("V2", "bv2", lambda t: v2[:, t, :].rearrange("p (h c) -> p h c", h=H))
                dve.wait_ge(gate_ready, b * 2 + 2)
                for t in range(NT):
                    ins = dve.scalar_tensor_tensor(out=nat_y[:, t, :], in0=vp_b[:, :], scalar=rcol[:, t:t + 1], in1=nat_n[:, t, :],
                                                   op0=ALU.mult, op1=ALU.mult)
                link(ins)
                link(dve.tensor_tensor(nat_y[:, :, :], nat_y[:, :, :], nat_x[:, :, :], ALU.add))

                def norm(n):
                    for t in range(NT):
                        ins = dve.bn_stats(stats[:, t, :], nat_y[:, t, :])
                    link(ins)
                    hold()
                    for t in range(NT):
                        ins = dve.bn_aggr(mv[:, t, :], stats[:, t, :])
                    if n == 1:
                        link(ins)
                        ins = dve.tensor_scalar(std1[:, :], mv[:, :, 1], 1e-18, None, ALU.max)
                    ins.then_inc(var_ready, 1)
                    dve.wait_ge(rstd_ready, b * 5 + n + 1)
                    scale = std
                    if n == 1:
                        link(dve.tensor_scalar(std1[:, :], std[:, :], 1e-8, None, ALU.add))
                        link(dve.reciprocal(rstd[:, :], std1[:, :]))
                        scale = rstd
                    for t in range(NT):
                        ins = dve.tensor_scalar(nat_n[:, t, :], nat_y[:, t, :], mv[:, t, 0:1], scale[:, t:t + 1],
                                                ALU.subtract, ALU.mult)
                        if t + 1 < NT:
                            ins.then_inc(tile_normed, 1)
                    ins.then_inc(norm_ready, 1)

                norm(0)
                for j in range(2):
                    dve.wait_ge(*drained_by(("V2", j), b))
                link(dve.tensor_scalar(v2[:, :, :], v2[:, :, :], 0.0, None, ALU.max))
                dve.wait_ge(*drained_by(("ksum",), b))
                for t in range(NT):
                    dve.tensor_scalar(v_of[CAUSAL][:, t, :, 0:DH], v2[:, t, :].rearrange("p (h c) -> p h c", h=H),
                                      km[:, t:t + 1], None, ALU.mult)
                    ins = dve.tensor_scalar(v_of[CAUSAL][:, t, :, DH:2 * DH], ones[:, 0:DH].unsqueeze(1).broadcast_to([P, H, DH]),
                                            km[:, t:t + 1], None, ALU.mult)
                ins.then_inc(vmask_ready, 1)
                dve.wait_ge(*filled_by(("cnt",), b))
                dve.tensor_scalar(degen[:, :], slot(("cnt",))[:, 0, 0:NT], 0.5, None, ALU.is_lt).then_inc(*ends_drain(("cnt",)))
                def drain_q(n, name, bias, relu=False):
                    for t in range(DT):
                        dve.wait_ge(*((q_half, b * 3 + n + 1) if t == 0 else filled_by(name, b)))
                        dve.tensor_scalar(q_full[:, t, :], slot(name)[:, t, :], col(bias, t), 0.0 if relu else None,
                                          ALU.add, ALU.max if relu else ALU.bypass).then_inc(q_full_ready, 1)
                    dve.wait_ge(q_hi_ready, (b * 3 + n + 1) * DT)
                    dve.tensor_tensor(q_parts[:, 1, :, :], q_full, q_parts[:, 0, :, :], ALU.subtract).then_inc(*ends_drain(name))

                def maxima(a, g, qt, u):
                    _, nk = seen(a, qt)
                    name = (a, "A", g, qt, u)
                    dve.wait_ge(*filled_by(name, b))
                    dve.tensor_reduce(nmax[:, qt, 2 * u:2 * u + 2], slot(name)[:, :, 0:nk], AX.X, ALU.max, negate=True)\
                        .then_inc(*ends_drain(name))

                def maxima_cols(a, g):
                    m = mcol[:, g % 2, :, :].rearrange("p t (u c) -> p t u c", u=2)
                    high, low = (m[:, :, :, i:i + 49:48] for i in range(2))
                    top = nmax[:, :, :].rearrange("p t (u i) -> p t u i", u=2)
                    dve.wait_ge(*drained_by((a, "A", g, NT - 1, 1), b))
                    link(dve.tensor_copy(high, top))
                    dve.tensor_tensor(low, top, high, ALU.subtract).then_inc(mcol_ready, 1)
                    dve.wait_ge(mcol_ready, b * 12 + a * GROUPS + g + 1)

                def head_out(a, g):
                    n = a * GROUPS + g
                    dve.wait_ge(out_drained, b * OUT_ITER + PAIRS + n)
                    dve.wait_ge(pv_done, b * PV_ITER + UNITS0 + NT * (n + 1))
                    hold()
                    o = obank[:, (PAIRS + n) % 2, :]
                    link(dve.stream_shuffle(rbuf[:, :], o, [DH + i % DH for i in range(32)]))
                    if a == CAUSAL:
                        link(dve.tensor_scalar(rbuf[:, :], rbuf[:, :], 1e-30, None, ALU.max))
                    link(dve.reciprocal(rbuf[:, :], rbuf[:, :]))
                    dve.tensor_tensor(oT[:, g, :], o, rbuf[:, :], ALU.mult).then_inc(out_drained, 1)

                def attention(a):
                    for qt in range(NT):
                        for u in range(2):
                            maxima(a, 0, qt, u)
                    maxima_cols(a, 0)
                    for g in range(GROUPS):
                        if g + 1 < GROUPS:
                            for qt in range(NT):
                                for u in range(2):
                                    maxima(a, g + 1, qt, u)
                            maxima_cols(a, g + 1)
                        if g >= 1:
                            head_out(a, g - 1)
                    head_out(a, GROUPS - 1)

                drain_q(0, ("Q2",), "bq2", relu=True)
                dve.wait_ge(*filled_by(("meanV",), b))
                dve.tensor_scalar(wide[:, :, :], slot(("meanV",))[:, 0, 0:DT].unsqueeze(2).broadcast_to([P, DT, P]), 1.0 / S, None, ALU.mult)\
                    .then_inc(*ends_drain(("meanV",)))
                dve.wait_ge(*filled_by(("meanO",), b))
                dve.tensor_tensor(mean_o[:, :], slot(("meanO",))[:, 0, 0:D], row("bo2").squeeze(1), ALU.add)\
                    .then_inc(*ends_drain(("meanO",)))

                drain_v("VC", "cbv", lambda t: v_of[FULL][:, t, :, 0:DH])
                attention(CAUSAL)
                dve.wait_ge(resid_ready, b * 4 + 1)
                for j in range(2):
                    dve.wait_ge(*filled_by(("O2", j), b))
                    for i in range(2):
                        t = 2 * j + i
                        ins = dve.scalar_tensor_tensor(out=nat_y[:, t, :], in0=mean_o[:, :], scalar=degen[:, t:t + 1],
                                                       in1=slot(("O2", j))[:, i, 0:D], op0=ALU.mult, op1=ALU.add)
                    ins.then_inc(*ends_drain(("O2", j)))
                    dve.wait_ge(*drained_by(("O2", j), b))
                    part = slice(2 * j, 2 * j + 2)
                    link(dve.scalar_tensor_tensor(out=nat_y[:, part, :], in0=nat_y[:, part, :], scalar=0.0, in1=nat_x[:, part, :],
                                                  op0=ALU.max, op1=ALU.add))
                norm(1)

                def drain_out(name, resid):
                    for j in range(2):
                        part = slice(2 * j, 2 * j + 2)
                        dve.wait_ge(*filled_by((name, j), b))
                        dve.tensor_tensor(nat_y[:, part, :], slot((name, j))[:, :, 0:D], resid[:, part, :], ALU.add)\
                            .then_inc(*ends_drain((name, j)))
                    for j in range(2):
                        dve.wait_ge(*drained_by((name, j), b))

                drain_q(1, ("QS",), "sbq")
                drain_v("VS", "sbv", lambda t: v_of[BANDED][:, t, :, 0:DH])
                attention(BANDED)
                drain_out("OS", nat_n)
                norm(2)
                drain_q(2, ("QC",), "cbq")
                attention(FULL)
                dve.wait_ge(resid_ready, b * 4 + 2)
                drain_out("OC", nat_x)
                norm(3)
                dve.wait_ge(resid_ready, b * 4 + 3)
                drain_out("F2", nat_x)
                norm(4)
                dve.wait_ge(norm_ready, b * 5 + 5)
                assert links[0] == DVE_LINKS, links

        @block.tensor
        def _(pe):
            pe.wait_ge(setup_dve, 4)
            pe.wait_ge(setup_act, 6)
            pe.wait_ge(setup_pool, 5)
            with pe.Fori(0, B) as b:
                order = [0]

                def start(name):
                    assert JOBS[order[0]] == name, (JOBS[order[0]], name)
                    order[0] += 1
                    pe.wait_ge(*free_for(name, b))
                    return slot(name)

                def project(name, w, src, tiles):
                    dst = start(name)
                    for i, m in enumerate(tiles):
                        for t in range(DT):
                            ins = pe.matmul(dst[:, i, :], w[:, t, m * P:(m + 1) * P], src[:, t, :], start=(t == 0), stop=(t == DT - 1))
                        if name in Q_JOB.values() and i == 0:
                            ins.then_inc(q_half, 1)
                    ins.then_inc(*ends_fill(name))

                def project_nat(name, w, src):
                    for j in range(2):
                        dst = start((name, j))
                        for i in range(2):
                            m = 2 * j + i
                            for t in range(DT):
                                ins = pe.matmul(dst[:, i, 0:D], src[:, t, m * P:(m + 1) * P], w[:, t, :], start=(t == 0), stop=(t == DT - 1))
                        ins.then_inc(*ends_fill((name, j)))

                def out_project(name, w, src, n):
                    for j in range(2):
                        dst = start((name, j))
                        for i in range(2):
                            m = 2 * j + i
                            for t in range(n):
                                ins = pe.matmul(dst[:, i, 0:D], src[:, t, m * P:(m + 1) * P], w[:, t, :], start=(t == 0), stop=(t == n - 1))
                        ins.then_inc(*ends_fill((name, j)))

                pe.wait_ge(k_loaded["ctx"], b * 16 + 16)
                pe.wait_ge(k_loaded["wv0"], b * 16 + 16)
                for kt in range(NT):
                    dst = start(("V0", kt))
                    for i in range(2):
                        for t in range(DT):
                            ins = pe.matmul(dst[:, i, :], ctx_t[:, t, kt * P:(kt + 1) * P], wv0[:, t, i * 512:(i + 1) * 512],
                                            start=(t == 0), stop=(t == DT - 1))
                    ins.then_inc(*ends_fill(("V0", kt)))

                def qk(p):
                    dst = start(("QK0", p))
                    for i, (w, src) in enumerate(((wq0, act_t), (wk0, ctx_t))):
                        for t in range(DT):
                            ins = pe.matmul(dst[:, i, :], w[:, t, p * P:(p + 1) * P], src[:, t, :], start=(t == 0), stop=(t == DT - 1))
                    ins.then_inc(*ends_fill(("QK0", p)))

                def scores0(p, kt):
                    name = ("S0", p, kt)
                    dst = start(name)
                    if kt == 0:
                        pe.wait_ge(*drained_by(("QK0", p), b))
                    for h, k in enumerate((qk0[:, p % 2, 1, :], k0_odd[:, p % 2, :])):
                        ins = pe.matmul(dst[:, h, :], k[:, kt * P:(kt + 1) * P], qk0[:, p % 2, 0, :], start=True, stop=True)
                    ins.then_inc(*ends_fill(name))

                def values0(p, kt):
                    n = NT * p + kt
                    if kt == 0 and p >= 2:
                        pe.wait_ge(out_drained, b * OUT_ITER + p - 1)
                    pe.wait_ge(exp0_done, b * UNITS0 + n + 1)
                    pe.wait_ge(vs_ready, b * UNITS0 + n + 1)
                    for h in range(2):
                        ins = pe.matmul(obank[DK0 * h:DK0 * (h + 1), p % 2, :], vs0[:, n % 4, h, :], e0[:, n % E0, h, :],
                                        start=(kt == 0), stop=(kt == NT - 1))
                    ins.then_inc(pv_done, 1)

                pe.wait_ge(k_loaded["act"], b * 16 + 16)
                pe.wait_ge(k_loaded["wq0"], b * 16 + 16)
                pe.wait_ge(k_loaded["wk0"], b * 16 + 16)
                qk(0)
                for p in range(PAIRS):
                    for kt in range(NT):
                        scores0(p, kt)
                        if p >= 1:
                            values0(p - 1, kt)
                        if kt == 1 and p + 1 < PAIRS:
                            qk(p + 1)
                for kt in range(NT):
                    values0(PAIRS - 1, kt)
                pe.wait_ge(out_drained, b * OUT_ITER + PAIRS)
                pe.wait_ge(k_loaded["wo0"], b * 16 + 16)
                out_project("O0", wo0, o0, PAIRS)

                pe.wait_ge(k_loaded["l1"], 64)
                pe.wait_ge(wide_ready, b + 1)
                dst = start(("vp",))
                for t in range(DT):
                    ins = pe.matmul(dst[:, 0, 0:D], wide[:, t, :], w_l1["v"][:, t, :], start=(t == 0), stop=(t == DT - 1))
                ins.then_inc(*ends_fill(("vp",)))
                dst = start(("vpT",))
                pe.wait_ge(*drained_by(("vp",), b))
                for t in range(DT):
                    ins = pe.transpose(dst[:, 0, t * P:(t + 1) * P], vp_b[:, t * P:(t + 1) * P], ident[:, :])
                ins.then_inc(*ends_fill(("vpT",)))
                def turn(n, src):
                    dst = start(("X", n))
                    for m in range(NT):
                        if n and m + 1 < NT:
                            pe.wait_ge(tile_normed, (b * 5 + n - 1) * (NT - 1) + m + 1)
                        elif n:
                            pe.wait_ge(norm_ready, b * 5 + n)
                        for t in range(DT):
                            ins = pe.transpose(dst[:, t, m * P:(m + 1) * P], src[:, m, t * P:(t + 1) * P], ident[:, :])
                    ins.then_inc(*ends_fill(("X", n)))

                for j in range(2):
                    pe.wait_ge(*drained_by(("O0", j), b))
                turn(0, nat_x)
                pe.wait_ge(k_loaded["l2"], 64)
                project(("K2",), w_sq["k2"], ctx_t, range(DT))
                dst = start(("uv",))
                pe.wait_ge(*drained_by(("vpT",), b))
                for t in range(DT):
                    ins = pe.matmul(dst[:, 0, 0:D], wide[:, t, :], w_l1["gv"][:, t, :], start=(t == 0), stop=(t == DT - 1))
                ins.then_inc(*ends_fill(("uv",)))
                pe.wait_ge(*drained_by(("X", 0), b))
                project(("tp",), w_l1["t"], act_t, range(DT))
                dst = start(("ksum",))
                pe.wait_ge(*drained_by(("K2",), b))
                for kt in range(NT):
                    for i in range(DT):
                        ins = pe.matmul(dst[:, 0, kt:kt + 1], k_full[:, i, kt * P:(kt + 1) * P], ones[:, 0:1],
                                        start=(i == 0), stop=(i == DT - 1))
                ins.then_inc(*ends_fill(("ksum",)))
                dst = start(("agree",))
                pe.wait_ge(*drained_by(("tp",), b))
                for t in range(DT):
                    ins = pe.matmul(dst[0:1, 0, :], wide[:, t, 0:1], tp_t[:, t, :], start=(t == 0), stop=(t == DT - 1))
                ins.then_inc(*ends_fill(("agree",)))
                for j in range(2):
                    dst = start(("gate", j))
                    for i in range(2):
                        m = 2 * j + i
                        for t in range(DT):
                            pe.matmul(dst[:, i, 0:D], tp_t[:, t, m * P:(m + 1) * P], w_l1["gt"][:, t, :], start=(t == 0), stop=False)
                        ins = pe.matmul(dst[:, i, 0:D], ones[0:1, :], rows[0:1, ROW["bg"], :], start=False, stop=True)
                    ins.then_inc(*ends_fill(("gate", j)))
                dst = start(("rcol",))
                pe.wait_ge(*drained_by(("agree",), b))
                pe.wait_ge(agree_inv, b + 1)
                for t in range(NT):
                    ins = pe.matmul(dst[:, 0, t:t + 1], rrow[0:1, t * P:(t + 1) * P], one_sum[0:1, 3:4], start=True, stop=True)
                ins.then_inc(*ends_fill(("rcol",)))
                project_nat("V2", w_sq["v2"], ctx_t)
                dst = start(("cnt",))
                pe.wait_ge(*drained_by(("ksum",), b))
                for qt in range(NT):
                    for kt in range(qt + 1):
                        ins = pe.matmul(dst[:, 0, qt:qt + 1], (tri if kt == qt else ones)[:, :], km[:, kt:kt + 1],
                                        start=(kt == 0), stop=(kt == qt))
                ins.then_inc(*ends_fill(("cnt",)))
                turn(1, nat_n)
                pe.wait_ge(*drained_by(("X", 1), b))
                project(("Q2",), w_sq["q2"], act_t, range(DT))
                dst = start(("meanV",))
                pe.wait_ge(vmask_ready, b + 1)
                for i in range(DT):
                    for kt in range(NT):
                        ins = pe.matmul(dst[:, 0, i:i + 1], v2[:, kt, i * P:(i + 1) * P], ones[:, 0:1], start=(kt == 0), stop=(kt == NT - 1))
                ins.then_inc(*ends_fill(("meanV",)))
                dst = start(("meanO",))
                pe.wait_ge(*drained_by(("meanV",), b))
                pe.wait_ge(k_loaded["om"], b * 16 + 16)
                for t in range(DT):
                    ins = pe.matmul(dst[:, 0, 0:D], wide[:, t, :], w_om[:, t, :], start=(t == 0), stop=(t == DT - 1))
                ins.then_inc(*ends_fill(("meanO",)))
                pe.wait_ge(k_loaded["lc"], 64)
                project_nat("VC", w_sq["cv"], ctx_t)

                def pass_a(a, g, qt, u):
                    name = (a, "A", g, qt, u)
                    dst = start(name)
                    if qt == 0 and u == 0:
                        pe.wait_ge(q_stacked[g], (b * 3 + a + 1) * 96)
                        pe.wait_ge(k_stacked[g], (b * 3 + a + 1) * 48)
                    k0, nk = seen(a, qt)
                    for i in range(2):
                        ins = pe.matmul(dst[:, i, 0:nk], q_tiles[g % 3][0:96, 2 * u + i, qt * P:(qt + 1) * P], k_tiles[g][0:96, u, k0:k0 + nk],
                                        start=True, stop=(a == FULL))
                        if a == BANDED:
                            pe.matmul(dst[:, i, 0:nk], cb("slopeA", P, at=g * P), cb("rowsJ", nk, at=(2 * u + i) * 2 * P + 2 * P - nk),
                                      start=False, stop=False)
                        if a != FULL:
                            mask, n, whole = ("bandA", nk, BAND) if a == BANDED else ("maskA", P, P)
                            ins = pe.matmul(dst[:, i, nk - n:nk], cb("ident", P), cb(mask, n, at=whole - n), start=False, stop=True)
                    ins.then_inc(*ends_fill(name))

                def pass_b(a, g, kt, u):
                    name = (a, "B", g, kt, u)
                    dst = start(name)
                    if (kt, u) == (0, 0):
                        pe.wait_ge(*drained_by((a, "T", g), b))
                    q0, nq = width(a, kt)
                    for i in range(2):
                        s = 2 * u + i
                        ins = pe.matmul(dst[:, i, 0:nq], k_tiles[g][:, u, kt * P:(kt + 1) * P], q_tiles[g % 3][:, s, q0:q0 + nq],
                                        start=True, stop=(a == FULL))
                        if a == BANDED:
                            pe.matmul(dst[:, i, 0:P], cb("rowsJ", P, at=s * 2 * P + P), cb("slopeA", P, at=g * P), start=False, stop=False)
                            if nq > P:
                                pe.matmul(dst[:, i, P:nq], cb("rowsJ", P, at=s * 2 * P), cb("slopeA", nq - P, at=g * P), start=False, stop=False)
                        if a != FULL:
                            mask, n = ("bandB", nq) if a == BANDED else ("maskB", P)
                            ins = pe.matmul(dst[:, i, 0:n], cb("ident", P), cb(mask, n), start=False, stop=True)
                    ins.then_inc(*ends_fill(name))

                def values(a, g, kt):
                    n = UNITS * a + NT * g + kt
                    o = a * GROUPS + g
                    q0, nq = width(a, kt)
                    if kt == 0:
                        pe.wait_ge(out_drained, b * OUT_ITER + PAIRS + max(0, o - 1))
                    first, second = ((a, "B", g, kt, u) for u in range(2))
                    pe.wait_ge(*drained_by(second, b))
                    if JOB[first] % SLOTS != JOB[second] % SLOTS:
                        pe.wait_ge(*drained_by(first, b))
                    for s, h in enumerate(heads_of(g)):
                        ins = pe.matmul(obank[32 * s:32 * s + 32, (PAIRS + o) % 2, q0:q0 + nq], v_of[a][:, kt, h, :], e16[:, n % 4, s, 0:nq],
                                        start=(kt == 0), stop=(kt == NT - 1), skip_group_check=(a != FULL))
                    ins.then_inc(pv_done, 1)

                def turn_maxima(a, g):
                    name = (a, "T", g)
                    dst = start(name)
                    pe.wait_ge(mcol_ready, b * 12 + a * GROUPS + g + 1)
                    turned = dst[:, 0, 0:256].bitcast(BF16)
                    for t in range(NT):
                        ins = pe.transpose(turned[:, t * P:(t + 1) * P], mcol[:, g % 2, t, :], cb("ident", P))
                    ins.then_inc(*ends_fill(name))

                def attention(a):
                    for qt in range(NT):
                        for u in range(2):
                            pass_a(a, 0, qt, u)
                    if a == BANDED:
                        pe.wait_ge(*drained_by(("VS", 1), b))
                        pe.wait_ge(ones_ready, b * 2 + 2)
                    for g in range(GROUPS):
                        for kind, *which in group_steps(g):
                            {"A": pass_a, "B": pass_b, "T": turn_maxima, "V": values}[kind](a, *which)
                    for kt in range(NT):
                        values(a, GROUPS - 1, kt)

                def out_heads(a, name):
                    dst = [start((name, j)) for j in range(2)]
                    for t in range(GROUPS):
                        pe.wait_ge(out_drained, b * OUT_ITER + PAIRS + a * GROUPS + t + 1)
                        for j in range(2):
                            for i in range(2):
                                m = 2 * j + i
                                ins = pe.matmul(dst[j][:, i, 0:D], oT[:, t, m * P:(m + 1) * P], w_out[a][:, t, :],
                                                start=(t == 0), stop=(t == GROUPS - 1))
                            if t == GROUPS - 1:
                                ins.then_inc(*ends_fill((name, j)))

                attention(CAUSAL)
                out_heads(CAUSAL, "O2")

                pe.wait_ge(k_loaded["ls"], 64)
                turn(2, nat_n)
                pe.wait_ge(*drained_by(("X", 2), b))
                project(("KS",), w_sq["sk"], act_t, range(DT))
                project(("QS",), w_sq["sq"], act_t, range(DT))
                project_nat("VS", w_sq["sv"], act_t)
                pe.wait_ge(*drained_by(("KS",), b))
                attention(BANDED)
                project(("KC",), w_sq["ck"], ctx_t, range(DT))
                out_heads(BANDED, "OS")
                turn(3, nat_n)
                pe.wait_ge(*drained_by(("X", 3), b))
                project(("QC",), w_sq["cq"], act_t, range(DT))
                attention(FULL)
                out_heads(FULL, "OC")
                turn(4, nat_n)
                pe.wait_ge(*drained_by(("X", 4), b))
                pe.wait_ge(k_loaded["ff"], b * 32 + 32)
                for j in range(FT // 2):
                    project(("F1", j), w_f1, act_t, (2 * j, 2 * j + 1))
                for j in range(FT // 2):
                    pe.wait_ge(*drained_by(("F1", j), b))
                out_project("F2", w_f2, hid, FT)
                while order[0] < len(JOBS):
                    name = JOBS[order[0]]
                    start(name)
                    pe.nop().then_inc(*ends_fill(name))
                    pe.nop().then_inc(*ends_drain(name))


def padded(w, bias, a):
    import numpy as np
    out = np.zeros((GROUPS, 4, 32, D), np.float32)
    for g in range(GROUPS):
        for s, h in enumerate(heads_of(g)):
            out[g, s, 0:DH] = w[h * DH:(h + 1) * DH]
    out[0, 0, DH] = bias
    return out.reshape(GROUPS * P, D)


def constants():
    import numpy as np
    c = np.zeros((P, NCONST), np.float32)

    def put(name, table, at=0):
        c[:, CST[name] + at:CST[name] + at + table.shape[1]] = table

    p = np.arange(P)[:, None]
    x = np.arange(P)[None, :]
    y = np.arange(BAND)[None, :]
    put("ident", (p == x).astype(np.float32))
    put("tri", (p <= x).astype(np.float32))
    put("maskA", np.where(x > p, NEG, 0.0))
    put("maskB", np.where(p > x, NEG, 0.0))
    ahead = y - W - p
    put("bandA", np.where((ahead <= 0) & (ahead > -W), 0.0, NEG))
    behind = y - p
    put("bandB", np.where((behind >= 0) & (behind < W), 0.0, NEG))
    slopes = (2.0 ** (-8.0 * np.arange(1, H + 1, dtype=np.float32) / H)).astype(np.float32)
    parts, rest = [], slopes.copy()
    for _ in range(3):
        hi = (rest.view(np.uint32) & np.uint32(0xFFFF0000)).view(np.float32)
        parts.append(hi)
        rest = (rest - hi).astype(np.float32)
    for s in range(4):
        jrow = np.zeros((4, 32, 2 * P))
        jrow[s, 0:3] = np.arange(-P, P)
        put("rowsJ", jrow.reshape(P, 2 * P), s * 2 * P)
    for g in range(GROUPS):
        sa = np.zeros((4, 32, P))
        for s, h in enumerate(heads_of(g)):
            for i in range(3):
                sa[s, i] = parts[i][h]
        put("slopeA", sa.reshape(P, P), g * P)
    put("pair", ((p >= 3 * 32) & (p % DH < 2)).astype(np.float32))
    put("half", (p // DK0 == np.arange(2)).astype(np.float32))
    return c


def arrange(i):
    import numpy as np
    f = {k: np.asarray(v) for k, v in i.items()}
    order = np.arange(D).reshape(GROUPS, DT, 2 * DH).transpose(1, 0, 2).ravel()
    for n in ("L2_xattn_Wq", "L2_xattn_Wk", "L3_xattn_swq", "L3_xattn_swk", "L3_xattn_cwq", "L3_xattn_cwk"):
        f[n] = f[n][:, order]
    for n in ("L2_xattn_bq", "L2_xattn_bk", "L3_xattn_sbq", "L3_xattn_sbk", "L3_xattn_cbq", "L3_xattn_cbk"):
        f[n] = f[n][order]
    c = np.ascontiguousarray
    a = {
        "xT": c(f["x"].transpose(0, 2, 1)), "ctxT": c(f["ctx_1024"].transpose(0, 2, 1)), "x": c(f["x"]),
        "mask": c(f["mask_BxS2_ik0"]),
        "wq0": c(f["L0_xattn_W_Q"].T), "wk0": c(f["L0_xattn_W_K"].T), "wv0": c(f["L0_xattn_W_V"].T), "wo0": c(f["L0_xattn_W_O"].T),
        "w1_t": c(f["L1_xattn_Wt"].T), "w1_v": c(f["L1_xattn_Wv"].T),
        "w1_gt": c(f["L1_xattn_Wg"][:, :D].T), "w1_gv": c(f["L1_xattn_Wg"][:, D:].T),
        "w_q2": c(f["L2_xattn_Wq"]), "w_k2": c(f["L2_xattn_Wk"]), "w_v2": c(f["L2_xattn_Wv"]), "w_om": c(f["L2_xattn_Wo"]),
        "w_f1": c(f["L3_xattn_w1"]), "w_f2": c(f["L3_xattn_w2"]),
        "w_out0": padded(f["L2_xattn_Wo"], f["L2_xattn_bo"], 0),
        "w_out1": padded(f["L3_xattn_swo"], f["L3_xattn_sbo"], 1),
        "w_out2": padded(f["L3_xattn_cwo"], f["L3_xattn_cbo"], 2),
        "consts": constants(),
    }
    for n in ("sq", "sk", "sv", "cq", "ck", "cv"):
        a["w_" + n] = c(f[f"L3_xattn_{n[0]}w{n[1]}"])
    col_of = {"bq0": "L0_xattn_b_Q", "bk0": "L0_xattn_b_K", "bt": "L1_xattn_bt", "bq2": "L2_xattn_bq", "bk2": "L2_xattn_bk",
              "sbq": "L3_xattn_sbq", "sbk": "L3_xattn_sbk", "cbq": "L3_xattn_cbq", "cbk": "L3_xattn_cbk", "b1": "L3_xattn_b1",
              "ga1": "L1_xattn_gamma", "be1": "L1_xattn_beta", "g1": "L3_xattn_g1", "b1n": "L3_xattn_be1",
              "g2": "L3_xattn_g2", "b2n": "L3_xattn_be2"}
    a["cols"] = c(np.concatenate([f[col_of[n]].reshape(k, P).T for n, k in COLS], axis=1))
    row_of = {"bv0": "L0_xattn_b_V", "bo0": "L0_xattn_b_O", "bv1": "L1_xattn_bv", "bg": "L1_xattn_bg", "ga1": "L1_xattn_gamma",
              "be1": "L1_xattn_beta", "bv2": "L2_xattn_bv", "bo2": "L2_xattn_bo", "sbv": "L3_xattn_sbv", "cbv": "L3_xattn_cbv",
              "b2": "L3_xattn_b2", "g1": "L3_xattn_g1", "b1n": "L3_xattn_be1", "g2": "L3_xattn_g2", "b2n": "L3_xattn_be2",
              "g3": "L3_xattn_g3", "b3n": "L3_xattn_be3"}
    a["rows"] = c(np.concatenate([f[row_of[n]].reshape(k, D) for n, k in ROWS], axis=0))
    return a


def kernel(**inputs):
    import numpy as _np
    import concourse.bacc as _bacc
    from concourse import mybir as _mybir
    from concourse.bass_utils import run_bass_kernel_spmd as _run

    nc = _bacc.Bacc("TRN2", target_bir_lowering=False, num_devices=1)
    arrays = arrange(inputs)
    io = {n: nc.dram_tensor("in_" + n, a.shape, _mybir.dt.from_np(a.dtype), kind="ExternalInput").ap() for n, a in arrays.items()}
    out = nc.dram_tensor("out", (B, S, D), F32, kind="ExternalOutput").ap()
    build(nc, io, out)
    r = _run(nc, [{"in_" + n: a for n, a in arrays.items()}], core_ids=[0])
    return r.results[0]["out"]
```
